# Optimizing a Trainium2 kernel written in Bass

```python
import numpy as np
import jax
import jax.numpy as jnp

def _softmax(x, axis=-1):
    return jax.nn.softmax(x, axis=axis)

def _gelu(x):
    return jax.nn.gelu(x, approximate=True)

def _silu(x):
    return jax.nn.silu(x)

def _sigmoid(x):
    return jax.nn.sigmoid(x)

def _layernorm(x, axis=-1, eps=1e-05):
    m = jnp.mean(x, axis=axis, keepdims=True)
    v = jnp.var(x, axis=axis, keepdims=True)
    return (x - m) / jnp.sqrt(v + eps)

def _scatter_add(tgt, idx, src, axis=0):
    return tgt.at[idx].add(src)

def _segment_sum(src, seg, n):
    return jax.ops.segment_sum(src, seg, n)
kernel_name = 'mk_gnn_preln_d4_gnn_r16_c67ffd'

def setup_inputs(seed: int=0):
    np.random.seed(seed)
    _w = jnp.asarray

    def _rec_inputs():
        import jax
        import jax.numpy as jnp
        _gk = jax.random.key(seed)
        x = -0.000364 + 1 * jax.random.normal(jax.random.fold_in(_gk, 1), (625, 768), jnp.float32)
        src = jax.random.randint(jax.random.fold_in(_gk, 2), (10000,), 0, 625, jnp.int32)
        dst = jax.random.randint(jax.random.fold_in(_gk, 3), (10000,), 0, 625, jnp.int32)
        _o = jnp.argsort(dst, stable=True)
        src = src[_o]
        dst = dst[_o]
        edge_type_34 = jax.random.randint(jax.random.fold_in(_gk, 13), (10000,), 0, 34, jnp.int32)
        edge_type_8 = jax.random.randint(jax.random.fold_in(_gk, 14), (10000,), 0, 8, jnp.int32)
        return (x, src, dst, edge_type_34, edge_type_8)
    x, src, dst, edge_type_34, edge_type_8 = _rec_inputs()

    def _L0_gnn_setup():
        import jax, jax.numpy as jnp
        import numpy as np
        N, IN, OUT, R, E = (1250, 768, 768, 8, 20000)

        def _rgcn_conv(x, src, dst, etype, W, root, b):
            num_nodes = x.shape[0]
            num_rel = W.shape[0]
            x_src = x[src]
            seg = dst * num_rel + etype
            sums = jax.ops.segment_sum(x_src, seg, num_segments=num_nodes * num_rel)
            cnt = jax.ops.segment_sum(jnp.ones((src.shape[0],), dtype=x.dtype), seg, num_segments=num_nodes * num_rel)
            mean = sums / jnp.maximum(cnt, 1.0)[:, None]
            mean = mean.reshape(num_nodes, num_rel, -1)
            out = jnp.einsum('nri,rio->no', mean, W)
            return out + x @ root + b
        key = jax.random.key(seed)
        ks = jax.random.split(key, 9)
        x = jax.random.normal(ks[0], (N, IN), dtype=jnp.float32)
        edge_index = jax.random.randint(ks[1], (2, E), 0, N, dtype=jnp.int64)
        edge_type = jax.random.randint(ks[2], (E,), 0, R, dtype=jnp.int64)
        s1 = 1.0 / np.sqrt(IN)
        s2 = 1.0 / np.sqrt(OUT)
        W1 = jax.random.normal(ks[3], (R, IN, OUT), dtype=jnp.float32) * s1
        root1 = jax.random.normal(ks[4], (IN, OUT), dtype=jnp.float32) * s1
        b1 = jnp.zeros((OUT,), dtype=jnp.float32)
        W2 = jax.random.normal(ks[5], (R, OUT, OUT), dtype=jnp.float32) * s2
        root2 = jax.random.normal(ks[6], (OUT, OUT), dtype=jnp.float32) * s2
        b2 = jnp.zeros((OUT,), dtype=jnp.float32)
        return {'x': x, 'edge_index': edge_index, 'edge_type': edge_type, 'W1': W1, 'root1': root1, 'b1': b1, 'W2': W2, 'root2': root2, 'b2': b2}
    _L0_gnn_all = _L0_gnn_setup()
    _L0_gnn_in = {k: v for k, v in _L0_gnn_all.items() if k in ('W1', 'root1', 'b1', 'W2', 'root2', 'b2')}
    del _L0_gnn_all

    def _L1_gnn_setup():
        import jax, jax.numpy as jnp
        import numpy as np
        N_NODES = 625
        N_EDGES = 6250
        N_REL = 34
        DIM = 768

        def _graph_encoder(x, edge_index, edge_type, W_rel, W_root, b_rgcn, W_gcn, b_gcn):
            n = x.shape[0]
            src, dst = (edge_index[0], edge_index[1])
            ones = jnp.ones((src.shape[0],), dtype=x.dtype)
            seg = edge_type * n + dst
            agg = jax.ops.segment_sum(x[src], seg, num_segments=N_REL * n)
            cnt = jax.ops.segment_sum(ones, seg, num_segments=N_REL * n)
            mean = agg.reshape(N_REL, n, -1) / jnp.maximum(cnt, 1.0).reshape(N_REL, n, 1)
            h1 = jnp.einsum('rni,rio->no', mean, W_rel) + x @ W_root + b_rgcn
            xw = h1 @ W_gcn
            deg = jax.ops.segment_sum(ones, dst, num_segments=n) + 1.0
            dinv = jax.lax.rsqrt(deg)
            norm = dinv[src] * dinv[dst]
            out = jax.ops.segment_sum(xw[src] * norm[:, None], dst, num_segments=n)
            out = out + xw * (dinv * dinv)[:, None]
            return out + b_gcn
        key = jax.random.key(seed)
        ks = jax.random.split(key, 6)
        scale = 1.0 / np.sqrt(DIM)
        x = jax.random.normal(ks[0], (N_NODES, DIM), dtype=jnp.float32)
        edge_index = jax.random.randint(ks[1], (2, N_EDGES), 0, N_NODES, dtype=jnp.int32)
        edge_type = jax.random.randint(ks[2], (N_EDGES,), 0, N_REL, dtype=jnp.int32)
        W_rel = jax.random.normal(ks[3], (N_REL, DIM, DIM), dtype=jnp.float32) * scale
        W_root = jax.random.normal(ks[4], (DIM, DIM), dtype=jnp.float32) * scale
        b_rgcn = jnp.zeros((DIM,), dtype=jnp.float32)
        W_gcn = jax.random.normal(ks[5], (DIM, DIM), dtype=jnp.float32) * scale
        b_gcn = jnp.zeros((DIM,), dtype=jnp.float32)
        return {'x': x, 'edge_index': edge_index, 'edge_type': edge_type, 'W_rel': W_rel, 'W_root': W_root, 'b_rgcn': b_rgcn, 'W_gcn': W_gcn, 'b_gcn': b_gcn}
    _L1_gnn_all = _L1_gnn_setup()
    _L1_gnn_in = {k: v for k, v in _L1_gnn_all.items() if k in ('W_rel', 'W_root', 'b_rgcn', 'W_gcn', 'b_gcn')}
    del _L1_gnn_all

    def _L2_gnn_setup():
        import jax, jax.numpy as jnp
        import numpy as np
        N = 1250
        E_RAND = 20000
        NEG_SLOPE = 0.2

        def gat_layer(x, W, a_src, a_dst, bias, src, dst, heads, out_c, concat):
            n = x.shape[0]
            h = (x @ W).reshape(n, heads, out_c)
            al_s = jnp.einsum('nhc,hc->nh', h, a_src)
            al_d = jnp.einsum('nhc,hc->nh', h, a_dst)
            e = jax.nn.leaky_relu(al_s[src] + al_d[dst], NEG_SLOPE)
            m = jax.ops.segment_max(e, dst, num_segments=n)
            ex = jnp.exp(e - m[dst])
            z = jax.ops.segment_sum(ex, dst, num_segments=n)
            alpha = ex / (z[dst] + 1e-16)
            msg = h[src] * alpha[:, :, None]
            out = jax.ops.segment_sum(msg, dst, num_segments=n)
            out = out.reshape(n, heads * out_c) if concat else out.mean(axis=1)
            return out + bias
        key = jax.random.key(seed)
        ks = jax.random.split(key, 10)
        x = jax.random.normal(ks[0], (N, 768), dtype=jnp.float32)
        src = jax.random.randint(ks[1], (E_RAND,), 0, N)
        dst = jax.random.randint(ks[2], (E_RAND,), 0, N)
        loop = jnp.arange(N)
        edge_index = jnp.stack([jnp.concatenate([src, loop]), jnp.concatenate([dst, loop])])
        s = 1.0 / np.sqrt(768.0)
        W1 = jax.random.normal(ks[3], (768, 768), dtype=jnp.float32) * s
        a_src1 = jax.random.normal(ks[4], (8, 96), dtype=jnp.float32) * 0.1
        a_dst1 = jax.random.normal(ks[5], (8, 96), dtype=jnp.float32) * 0.1
        b1 = jnp.zeros((768,), dtype=jnp.float32)
        W2 = jax.random.normal(ks[6], (768, 768), dtype=jnp.float32) * s
        a_src2 = jax.random.normal(ks[7], (1, 768), dtype=jnp.float32) * 0.1
        a_dst2 = jax.random.normal(ks[8], (1, 768), dtype=jnp.float32) * 0.1
        b2 = jnp.zeros((768,), dtype=jnp.float32)
        return {'x': x, 'edge_index': edge_index, 'W1': W1, 'a_src1': a_src1, 'a_dst1': a_dst1, 'b1': b1, 'W2': W2, 'a_src2': a_src2, 'a_dst2': a_dst2, 'b2': b2}
    _L2_gnn_all = _L2_gnn_setup()
    _L2_gnn_in = {k: v for k, v in _L2_gnn_all.items() if k in ('W1', 'a_src1', 'a_dst1', 'b1', 'W2', 'a_src2', 'a_dst2', 'b2')}
    del _L2_gnn_all

    def _L3_gnn_setup():
        import jax, jax.numpy as jnp
        import numpy as np
        N = 1250
        DEG = 16
        E = N * DEG
        H = 12
        DIN = 64
        DOUT = 64
        NEG_SLOPE = 0.2
        key = jax.random.key(seed)
        k_h, k_src, k_w, k_al, k_ar, k_wr = jax.random.split(key, 6)
        std = 1.414 * np.sqrt(2.0 / (DIN + DOUT))
        h = jax.random.normal(k_h, (N, H * DIN), dtype=jnp.float32)
        src = jax.random.randint(k_src, (E,), 0, N, dtype=jnp.int64)
        dst = jnp.repeat(jnp.arange(N, dtype=jnp.int64), DEG)
        W = jax.random.normal(k_w, (DOUT, DIN), dtype=jnp.float32) * std
        attn_l = jax.random.normal(k_al, (1, H, DOUT), dtype=jnp.float32) * std
        attn_r = jax.random.normal(k_ar, (1, H, DOUT), dtype=jnp.float32) * std
        W_res = jax.random.normal(k_wr, (DOUT, DIN), dtype=jnp.float32) * std
        return {'h': h, 'src': src, 'dst': dst, 'W': W, 'attn_l': attn_l, 'attn_r': attn_r, 'W_res': W_res}
    _L3_gnn_all = _L3_gnn_setup()
    _L3_gnn_in = {k: v for k, v in _L3_gnn_all.items() if k in ('W', 'attn_l', 'attn_r', 'W_res')}
    del _L3_gnn_all
    return {'x': x, 'src': src, 'dst': dst, 'edge_type_34': edge_type_34, 'edge_type_8': edge_type_8, 'L0_gnn_W1': _L0_gnn_in['W1'], 'L0_gnn_root1': _L0_gnn_in['root1'], 'L0_gnn_b1': _L0_gnn_in['b1'], 'L0_gnn_W2': _L0_gnn_in['W2'], 'L0_gnn_root2': _L0_gnn_in['root2'], 'L0_gnn_b2': _L0_gnn_in['b2'], 'L1_gnn_W_rel': _L1_gnn_in['W_rel'], 'L1_gnn_W_root': _L1_gnn_in['W_root'], 'L1_gnn_b_rgcn': _L1_gnn_in['b_rgcn'], 'L1_gnn_W_gcn': _L1_gnn_in['W_gcn'], 'L1_gnn_b_gcn': _L1_gnn_in['b_gcn'], 'L2_gnn_W1': _L2_gnn_in['W1'], 'L2_gnn_a_src1': _L2_gnn_in['a_src1'], 'L2_gnn_a_dst1': _L2_gnn_in['a_dst1'], 'L2_gnn_b1': _L2_gnn_in['b1'], 'L2_gnn_W2': _L2_gnn_in['W2'], 'L2_gnn_a_src2': _L2_gnn_in['a_src2'], 'L2_gnn_a_dst2': _L2_gnn_in['a_dst2'], 'L2_gnn_b2': _L2_gnn_in['b2'], 'L3_gnn_W': _L3_gnn_in['W'], 'L3_gnn_attn_l': _L3_gnn_in['attn_l'], 'L3_gnn_attn_r': _L3_gnn_in['attn_r'], 'L3_gnn_W_res': _L3_gnn_in['W_res']}

def reference(x, src, dst, edge_type_34, edge_type_8, L0_gnn_W1, L0_gnn_root1, L0_gnn_b1, L0_gnn_W2, L0_gnn_root2, L0_gnn_b2, L1_gnn_W_rel, L1_gnn_W_root, L1_gnn_b_rgcn, L1_gnn_W_gcn, L1_gnn_b_gcn, L2_gnn_W1, L2_gnn_a_src1, L2_gnn_a_dst1, L2_gnn_b1, L2_gnn_W2, L2_gnn_a_src2, L2_gnn_a_dst2, L2_gnn_b2, L3_gnn_W, L3_gnn_attn_l, L3_gnn_attn_r, L3_gnn_W_res):
    import jax
    import jax.numpy as jnp

    def _L0_gnn_ref(x, edge_index, edge_type, W1, root1, b1, W2, root2, b2):
        import jax, jax.numpy as jnp
        import numpy as np
        N, IN, OUT, R, E = (1250, 768, 768, 8, 20000)

        def _rgcn_conv(x, src, dst, etype, W, root, b):
            num_nodes = x.shape[0]
            num_rel = W.shape[0]
            x_src = x[src]
            seg = dst * num_rel + etype
            sums = jax.ops.segment_sum(x_src, seg, num_segments=num_nodes * num_rel)
            cnt = jax.ops.segment_sum(jnp.ones((src.shape[0],), dtype=x.dtype), seg, num_segments=num_nodes * num_rel)
            mean = sums / jnp.maximum(cnt, 1.0)[:, None]
            mean = mean.reshape(num_nodes, num_rel, -1)
            out = jnp.einsum('nri,rio->no', mean, W)
            return out + x @ root + b
        src, dst = (edge_index[0], edge_index[1])
        h = _rgcn_conv(x, src, dst, edge_type, W1, root1, b1)
        h = jax.nn.relu(h)
        out = _rgcn_conv(h, src, dst, edge_type, W2, root2, b2)
        return out

    def _L1_gnn_ref(x, edge_index, edge_type, W_rel, W_root, b_rgcn, W_gcn, b_gcn):
        import jax, jax.numpy as jnp
        import numpy as np
        N_NODES = 625
        N_EDGES = 6250
        N_REL = 34
        DIM = 768

        def _graph_encoder(x, edge_index, edge_type, W_rel, W_root, b_rgcn, W_gcn, b_gcn):
            n = x.shape[0]
            src, dst = (edge_index[0], edge_index[1])
            ones = jnp.ones((src.shape[0],), dtype=x.dtype)
            seg = edge_type * n + dst
            agg = jax.ops.segment_sum(x[src], seg, num_segments=N_REL * n)
            cnt = jax.ops.segment_sum(ones, seg, num_segments=N_REL * n)
            mean = agg.reshape(N_REL, n, -1) / jnp.maximum(cnt, 1.0).reshape(N_REL, n, 1)
            h1 = jnp.einsum('rni,rio->no', mean, W_rel) + x @ W_root + b_rgcn
            xw = h1 @ W_gcn
            deg = jax.ops.segment_sum(ones, dst, num_segments=n) + 1.0
            dinv = jax.lax.rsqrt(deg)
            norm = dinv[src] * dinv[dst]
            out = jax.ops.segment_sum(xw[src] * norm[:, None], dst, num_segments=n)
            out = out + xw * (dinv * dinv)[:, None]
            return out + b_gcn
        return _graph_encoder(x, edge_index, edge_type, W_rel, W_root, b_rgcn, W_gcn, b_gcn)

    def _L2_gnn_ref(x, edge_index, W1, a_src1, a_dst1, b1, W2, a_src2, a_dst2, b2):
        import jax, jax.numpy as jnp
        import numpy as np
        N = 1250
        E_RAND = 20000
        NEG_SLOPE = 0.2

        def gat_layer(x, W, a_src, a_dst, bias, src, dst, heads, out_c, concat):
            n = x.shape[0]
            h = (x @ W).reshape(n, heads, out_c)
            al_s = jnp.einsum('nhc,hc->nh', h, a_src)
            al_d = jnp.einsum('nhc,hc->nh', h, a_dst)
            e = jax.nn.leaky_relu(al_s[src] + al_d[dst], NEG_SLOPE)
            m = jax.ops.segment_max(e, dst, num_segments=n)
            ex = jnp.exp(e - m[dst])
            z = jax.ops.segment_sum(ex, dst, num_segments=n)
            alpha = ex / (z[dst] + 1e-16)
            msg = h[src] * alpha[:, :, None]
            out = jax.ops.segment_sum(msg, dst, num_segments=n)
            out = out.reshape(n, heads * out_c) if concat else out.mean(axis=1)
            return out + bias
        src, dst = (edge_index[0], edge_index[1])
        h = gat_layer(x, W1, a_src1, a_dst1, b1, src, dst, heads=8, out_c=96, concat=True)
        h = jax.nn.elu(h)
        out = gat_layer(h, W2, a_src2, a_dst2, b2, src, dst, heads=1, out_c=768, concat=False)
        return out

    def _L3_gnn_ref(h, src, dst, W, attn_l, attn_r, W_res):
        import jax, jax.numpy as jnp
        import numpy as np
        N = 1250
        DEG = 16
        E = N * DEG
        H = 12
        DIN = 64
        DOUT = 64
        NEG_SLOPE = 0.2
        n = h.shape[0]
        hv = h.reshape(n, H, DIN)
        ft = jnp.einsum('nhd,od->nho', hv, W)
        a1 = jnp.sum(ft * attn_l, axis=-1)
        a2 = jnp.sum(ft * attn_r, axis=-1)
        e = jax.nn.leaky_relu(a1[src] + a2[dst], negative_slope=NEG_SLOPE)
        m = jax.ops.segment_max(e, dst, num_segments=n)
        m = jnp.where(jnp.isfinite(m), m, 0.0)
        w = jnp.exp(e - m[dst])
        denom = jax.ops.segment_sum(w, dst, num_segments=n)
        alpha = w / jnp.maximum(denom[dst], 1e-16)
        msg = alpha[:, :, None] * ft[src]
        agg = jax.ops.segment_sum(msg, dst, num_segments=n)
        res = jnp.einsum('nhd,od->nho', hv, W_res)
        out = jax.nn.relu((agg + res).reshape(n, H * DOUT))
        return out
    edge_index = jnp.stack([src, dst])
    h = jnp.maximum(_layernorm(x, axis=-1), 0.0)
    x = x + _L0_gnn_ref(h, edge_index, edge_type_8, L0_gnn_W1, L0_gnn_root1, L0_gnn_b1, L0_gnn_W2, L0_gnn_root2, L0_gnn_b2)
    h = jnp.maximum(_layernorm(x, axis=-1), 0.0)
    x = x + _L1_gnn_ref(h, edge_index, edge_type_34, L1_gnn_W_rel, L1_gnn_W_root, L1_gnn_b_rgcn, L1_gnn_W_gcn, L1_gnn_b_gcn)
    h = jnp.maximum(_layernorm(x, axis=-1), 0.0)
    x = x + _L2_gnn_ref(h, edge_index, L2_gnn_W1, L2_gnn_a_src1, L2_gnn_a_dst1, L2_gnn_b1, L2_gnn_W2, L2_gnn_a_src2, L2_gnn_a_dst2, L2_gnn_b2)
    h = jnp.maximum(_layernorm(x, axis=-1), 0.0)
    x = x + _L3_gnn_ref(h, src, dst, L3_gnn_W, L3_gnn_attn_l, L3_gnn_attn_r, L3_gnn_W_res)
    return x

_drawn_inputs = setup_inputs


def setup_inputs(seed=0):
    import zlib

    import numpy as np

    out = dict(_drawn_inputs(seed))
    spreads = {'L0_gnn_b1': (0.0, 0.1),
     'L0_gnn_b2': (0.0, 0.275),
     'L1_gnn_b_rgcn': (0.0, 0.308),
     'L1_gnn_b_gcn': (0.0, 0.286),
     'L2_gnn_b1': (0.0, 0.376),
     'L2_gnn_b2': (0.0, 0.321)}
    factors = {'L2_gnn_a_src1': 8.0,
     'L2_gnn_a_dst1': 8.0,
     'L2_gnn_a_src2': 8.0,
     'L2_gnn_a_dst2': 200.0,
     'L3_gnn_attn_l': 2.855,
     'L3_gnn_attn_r': 65.068}
    for name, (base, spread) in spreads.items():
        noise = np.random.default_rng([zlib.crc32(name.encode()), seed]).standard_normal(out[name].shape)
        drawn = base * np.exp(spread * noise) if base else spread * noise
        out[name] = jnp.asarray(drawn.astype(out[name].dtype))
    for name, factor in factors.items():
        out[name] = (out[name] * factor).astype(out[name].dtype)
    return out
```

```python
from contextlib import ExitStack

import concourse.bass as bass
from concourse import mybir

ALU = mybir.AluOpType
ACT = mybir.ActivationFunctionType
AX = mybir.AxisListType
F32 = mybir.dt.float32
F32R = mybir.dt.float32r
F16 = mybir.dt.float16
I32 = mybir.dt.int32

P = 128
N, D, E = 625, 768, 10000
NG = -(-N // P)
NP = NG * P
LAST = N - (NG - 1) * P
KT = D // P
HALF = D // 2
EP, EC = 125, 80
NT = 84
R0, R1 = 8, 34
H2, C2 = 8, 96
H3, C3 = 12, 64
NEG = -1.0e30
GB = 4
CW = NP // 2
EPS = 1e-5
ds = bass.ds


def gnn_kernel(nc, a, out):
    ctx = ExitStack()
    with ctx:
        def sb(name, shape, dt=F32):
            return ctx.enter_context(nc.sbuf_tensor(name, shape, dt))

        def sem(name):
            return ctx.enter_context(nc.semaphore(name))

        x = sb("x", [P, NG, D])
        h = sb("h", [P, NG, D])
        hT_hi = sb("hT_hi", [P, KT, NP], F32R)
        hT_lo = sb("hT_lo", [P, KT, NP], F32R)
        w_hi = sb("w_hi", [P, 2, KT, HALF], F32R)
        w_lo = sb("w_lo", [P, 2, KT, HALF], F32R)
        R = sb("R", [P, NG, 780])
        arena = sb("arena", [P, 9600])
        raw = arena[:, 0:4608].rearrange("p (b k n) -> p b k n", b=2, k=KT)
        ust = arena[:, 4608:6528].rearrange("p (g n) -> p g n", g=NG)
        gat = arena[:, 6528:8064].rearrange("p (b n) -> p b n", b=GB)
        rowS = arena[:, 0:1280].rearrange("p (b n) -> p b n", b=2)
        rowM = arena[:, 1280:2560].rearrange("p (b n) -> p b n", b=2)
        zt = arena[:, 2560:3840].rearrange("p (b n) -> p b n", b=2)
        qt = arena[:, 3840:5120].rearrange("p (b n) -> p b n", b=2)
        lt = arena[:, 5120:6400].rearrange("p (b n) -> p b n", b=2)
        pt = arena[:, 6400:7680].rearrange("p (b n) -> p b n", b=2)
        alT = arena[0:H3, 7680:9600].rearrange("p (k n) -> p k n", k=3)
        msg_hi = sb("msg_hi", [P, 2, HALF], F32R)
        msg_lo = sb("msg_lo", [P, 2, HALF], F32R)
        onehot = sb("onehot", [P, 2, P], F32R)
        counts = sb("counts", [P, 2, NG, NP])
        C = counts[:, 0]
        CT = counts[:, 1]
        rad = counts[:].rearrange("p a g n -> p (a g n)").bitcast(F16)
        RC = 10
        oh_lo = rad[:, 0:2 * RC * P].rearrange("p (b c n) -> p b c n", b=2, c=RC)
        oh_hi = rad[:, 2560:2560 + RC * NT].rearrange("p (c n) -> p c n", c=RC)
        val_hi = rad[:, 3400:3400 + 2 * RC * 4 * NT].rearrange("p (b c v n) -> p b c v n", b=2, c=RC, v=4)
        vec = sb("vec", [P, 2, D])
        at = [0]

        def edge(shape, dt=F32):
            n = 1
            for d in shape[1:]:
                n *= d
            t = R[:].rearrange("p g n -> p (g n)")[0:shape[0], at[0]:at[0] + n]
            at[0] += n
            if dt != F32:
                t = t.bitcast(dt)
            if len(shape) == 3:
                t = t.rearrange("p (a b) -> p a b", a=shape[1])
            return t
        e_i = edge([EP, 4, EC], I32)
        e_f = edge([EP, 4, EC])
        ge = edge([EP, NG + 1, EC])
        grp1 = edge([EP, NG, EC])
        pre = edge([EP, NG, EC])
        zer = edge([EP, EC])
        rs = edge([EP, NG])
        off = edge([EP, NG])
        pos = edge([EP, EC])
        pos_i = edge([EP, EC], I32)
        hi_i = edge([EP, EC], I32)
        hi_f = edge([EP, EC])
        lo_f = edge([EP, EC])
        vals = edge([EP, EC, 4])
        tot = edge([P, NG])
        ntl = edge([P, NG, EC])
        tiles = edge([P, NG])
        tb = edge([P, NG])
        tbi = edge([P, NG])
        tab = sb("tab", [P, 4, NT])
        gt = sb("gt", [P, 4, NT])
        grp_f = sb("grp_f", [P, NT])
        grp = sb("grp", [P, NT], I32)
        ix_f = sb("ix_f", [P, 2, NT])
        ix = sb("ix", [P, 2, NT], I32)
        ixb = sb("ixb", [P, GB], I32)
        wgt = sb("wgt", [P, 2, NT])
        oh_d = sb("oh_d", [P, 2, P], F16)
        oh_r = sb("oh_r", [P, 2, R0 + R1], F16)
        oh_s = sb("oh_s", [P, 2, CW], F16)
        ohT = sb("ohT", [P, 2, P])
        kinv = sb("kinv", [P, NG, 64])
        kprod = sb("kprod", [P, 2, R0 + R1])
        ident = sb("ident", [P, P])
        ident16 = sb("ident16", [P, P], F16)
        ones = sb("ones", [P, P])
        below = sb("below", [EP, EP])
        iota = sb("iota", [P, P + 2])
        iota16 = sb("iota16", [P, NP + 1], F16)
        iota128 = sb("iota128", [P, EC])
        z16 = sb("z16", [P, 512], F16)
        bst = sb("bst", [P, NG, 2, 6])
        mv = sb("mv", [P, NG, 2])
        var = sb("var", [P, NG])
        std = sb("std", [P, NG])
        rstd = sb("rstd", [P, NG])
        deg = sb("deg", [P, NG])
        dinv = sb("dinv", [P, NG])
        al = sb("al", [P, 3, NG, H3])
        mxt = sb("mxt", [P, 2, NG])
        mz = sb("mz", [P, NG, H3])
        rz = sb("rz", [P, 2, NG])
        bd = sb("bd", [P, 2, P])
        bd_hi = sb("bd_hi", [P, 2, P], F32R)
        bd_lo = sb("bd_lo", [P, 2, P], F32R)
        w64 = sb("w64", [64, 2, P])
        ps = ctx.enter_context(nc.psum_tensor("ps", [P, 8, 512], F32))
        psf = ps[:].rearrange("p b n -> p (b n)")
        U = [nc.dram_tensor(f"U{i}", [R1 * NP, HALF], F32, kind="Internal").ap() for i in range(2)]
        rows_d = nc.dram_tensor("rows_d", [3, 3, H3, NP], F32, kind="Internal").ap()

        S = {n: sem(n) for n in (
            "x_in edges_in dve_nop w64_in consts vec_ok ln_var ln_std ln_h hT_tp hT_hi hT_lo "
            "w_hi w_lo steps evac pool_idx pool_nop msg_hi msg_lo agg_pe acc_out "
            "srt_rs srt_ps srt_rhs srt_mm srt_tab cnt_oh cnt_pe k_inv w_oh w_tp w_cp w_kg w_pr w_done "
            "c_oh c_pe ct_tp ct_cp deg_ok deg_sq gcn_y gcn_mm gcn_ev x_ok ln_c ln_cc ct_ln "
            "elu_v elu_m elu_e bd_z bd_tp bd_ok ft_mm ft_ev chain out_st").split()}
        w_in = [sem("w_in0"), sem("w_in1")]
        v_in = [sem("v_in0"), sem("v_in1")]
        u_st = [sem(f"u_st{g}") for g in range(NG)]
        g_in = [sem(f"g_in{b}") for b in range(GB)]
        A = [{m: sem(f"{m}_{n}") for m in "al_ok al_tp al_cp al_st rs0 rs1 rm0 rm1 seg q_ok z_ok l_ok t_ok p_ok o_mm o_r o_ev".split()}
             for n in range(3)]
        HEADS = ((H2, C2), (1, D), (H3, C3))

        Q_C1, Q_C2 = 0, 2 * (R0 + 1)
        Q_L1 = 2 * Q_C2
        Q_GCN = Q_L1 + 2 * (R1 + 1)
        Q_G1, Q_G2 = Q_GCN + 2, Q_GCN + 4
        Q_END = Q_G2 + 2
        Q_SPLIT = {Q_GCN: Q_G1 + 1, Q_G1: Q_G2, Q_G2: Q_END}
        ST_C1, ST_C2, ST_L1 = 0, 2 * R0, 4 * R0

        block = ctx.enter_context(nc.Block())

        def sides_at(stride, i):
            return list(range(stride * i // 10, stride * (i + 1) // 10))

        @block.sync
        def _(sp):
            sp.dma_start(x[:, 0:NG - 1, :], a["x"][0:(NG - 1) * P, :].rearrange("(g p) d -> p g d", p=P)).then_inc(S["x_in"], 16)
            sp.wait_ge(S["consts"], 1)
            sp.dma_start(x[0:LAST, NG - 1, :], a["x"][(NG - 1) * P:N, :]).then_inc(S["x_in"], 16)
            for k, name in enumerate(("src", "dst", "edge_type_8", "edge_type_34")):
                sp.dma_start(e_i[:, k, :], a[name].rearrange("(p c) -> p c", c=EC)).then_inc(S["edges_in"], 16)
            for k, name in enumerate(("L3_gnn_W", "L3_gnn_W_res")):
                for i in range(2):
                    sp.dma_start(w64[:, k, 64 * i:64 * i + 64], a[name]).then_inc(S["w64_in"], 16)

            def load(it, o, src):
                sp.wait_ge(S["w_lo"], o + 2 * it + 1)
                sp.dma_start(raw[:, o % 2], src).then_inc(w_in[o % 2], 16)

            def halves(w, hf):
                return w[:, hf * HALF:(hf + 1) * HALF].rearrange("(k p) n -> p k n", p=P)

            def rel(w, r, hf):
                return w[ds(r, 1), :, hf * HALF:(hf + 1) * HALF].rearrange("r (k p) n -> p (r k) n", p=P)

            def store(it, o, r, hf):
                for g in range(NG):
                    sp.wait_ge(S["evac"], 5 * (o + 2 * it) + g + 3)
                    sp.dma_start(U[hf][ds(r * NP + g * P, P), :], ust[:, g, :]).then_inc(u_st[g], 16)

            def phase(Wr, root, q0, nr, after):
                for hf in range(2):
                    o = q0 + hf * (nr + 1)
                    with sp.Fori(0, nr // 2 - 1) as it:
                        for j in range(2):
                            load(it, o + 2 + j, rel(Wr, 2 * it + j + 2, hf))
                            store(it, o + j, 2 * it + j, hf)
                    load(0, o + nr, halves(root, hf))
                    store(0, o + nr - 2, nr - 2, hf)
                    if hf == 0:
                        load(0, o + nr + 1, rel(Wr, 0, 1))
                        store(0, o + nr - 1, nr - 1, hf)
                        load(0, o + nr + 2, rel(Wr, 1, 1))
                    else:
                        after(0)
                        store(0, o + nr - 1, nr - 1, hf)
                        after(1)

            def vector(name, v):
                if v >= 2:
                    sp.wait_ge(S["vec_ok"], v - 1)
                src = a[name]
                if len(src.shape) == 2:
                    src = src.rearrange("h c -> (h c)")
                elif len(src.shape) == 3:
                    src = src.rearrange("o h c -> (o h c)")
                sp.dma_start(vec[:, v % 2, :], src.partition_broadcast(P)).then_inc(v_in[v % 2], 16)

            load(0, 0, rel(a["L0_gnn_W1"], 0, 0))
            load(0, 1, rel(a["L0_gnn_W1"], 1, 0))
            vector("L0_gnn_b1", 0)
            phase(a["L0_gnn_W1"], a["L0_gnn_root1"], Q_C1, R0,
                  lambda k: load(0, Q_C2 + k, rel(a["L0_gnn_W2"], k, 0)))
            vector("L0_gnn_b2", 1)
            phase(a["L0_gnn_W2"], a["L0_gnn_root2"], Q_C2, R0,
                  lambda k: load(0, Q_L1 + k, rel(a["L1_gnn_W_rel"], k, 0)))
            vector("L1_gnn_b_rgcn", 2)
            phase(a["L1_gnn_W_rel"], a["L1_gnn_W_root"], Q_L1, R1,
                  lambda k: load(0, Q_GCN + k, halves(a["L1_gnn_W_gcn"], k)))
            vector("L1_gnn_b_gcn", 3)
            for k in range(2):
                load(0, Q_G1 + k, halves(a["L2_gnn_W1"], k))


            def spread(n, j, k, hd, buf, done):
                src = rows_d[n, k, ds(hd, 1), :].rearrange("o n -> (o n)").partition_broadcast(P)
                sp.dma_start(buf[:, j, :], src).then_inc(done, 16)

            def attention(n, v, bias):
                H, s = HEADS[n][0], A[n]
                sp.wait_ge(s["al_cp"], 1)
                sp.dma_start(rows_d[n, 0, 0:H, :], alT[0:H, 0, :]).then_inc(s["al_st"], 16)
                sp.wait_ge(s["al_st"], 16)

                def maxima(it, j):
                    sp.wait_ge(s["seg"], 2 * it + j + 1)
                    spread(n, j, 0, 2 * it + j, rowS, s[f"rs{j}"])

                def tiles_(it, j):
                    sp.wait_ge(s["z_ok"], 5 * (2 * it + j) + 5)
                    spread(n, j, 1, 2 * it + j, rowS, s[f"rs{j}"])
                    sp.wait_ge(s["q_ok"], 5 * (2 * it + j) + 5)
                    spread(n, j, 2, 2 * it + j, rowM, s[f"rm{j}"])
                if H == 1:
                    maxima(0, 0)
                else:
                    with sp.Fori(0, H // 2) as it:
                        for j in range(2):
                            maxima(it, j)
                for k in (1, 2):
                    sp.wait_ge(s["al_cp"], k + 1)
                    sp.dma_start(rows_d[n, k, 0:H, :], alT[0:H, k, :]).then_inc(s["al_st"], 16)
                sp.wait_ge(s["al_st"], 48)
                sp.wait_ge(s["seg"], H + 2)
                if bias is not None:
                    vector(bias, v)
                if H == 1:
                    tiles_(0, 0)
                else:
                    with sp.Fori(0, H // 2) as it:
                        for j in range(2):
                            tiles_(it, j)

            vector("L2_gnn_a_src1", 4)
            vector("L2_gnn_a_dst1", 5)
            attention(0, 6, "L2_gnn_b1")
            sp.wait_ge(S["elu_v"], 1)
            for k in range(2):
                load(0, Q_G2 + k, halves(a["L2_gnn_W2"], k))
            vector("L2_gnn_a_src2", 7)
            vector("L2_gnn_a_dst2", 8)
            attention(1, 9, "L2_gnn_b2")
            vector("L3_gnn_attn_l", 10)
            vector("L3_gnn_attn_r", 11)
            attention(2, None, None)
            sp.wait_ge(S["x_ok"], 1)
            sp.dma_start(out[0:(NG - 1) * P, :].rearrange("(g p) d -> p g d", p=P), x[:, 0:NG - 1, :]).then_inc(S["out_st"], 16)
            sp.dma_start(out[(NG - 1) * P:N, :], x[0:LAST, NG - 1, :]).then_inc(S["out_st"], 16)
            sp.wait_ge(S["out_st"], 32)

        @block.gpsimd
        def _(pool):
            pool.memset(x[:, NG - 1, :], 0.0).then_inc(S["consts"], 1)
            pool.memset(ident[:], 0.0).then_inc(S["consts"], 1)
            pool.memset(below[:], 1.0).then_inc(S["consts"], 1)
            pool.memset(bd[:], 0.0).then_inc(S["bd_z"], 1)
            pool.wait_ge(S["consts"], 3)
            pool.affine_select(out=ident[:], in_=ident[:], compare_op=ALU.not_equal, fill=1.0, base=0,
                               pattern=[[-1, P]], channel_multiplier=1).then_inc(S["consts"], 1)
            pool.affine_select(out=below[:], in_=below[:], compare_op=ALU.is_gt, fill=0.0, base=0,
                               pattern=[[1, EP]], channel_multiplier=-1).then_inc(S["consts"], 1)
            pool.memset(ones[:], 1.0).then_inc(S["consts"], 1)
            pool.memset(z16[:], 0.0).then_inc(S["consts"], 1)
            pool.memset(zer[:], 0.0).then_inc(S["consts"], 1)
            pool.iota(iota[:], [[1, P + 2]], base=0, channel_multiplier=0, allow_small_or_imprecise_dtypes=True).then_inc(S["consts"], 1)
            pool.iota(iota16[:], [[1, NP + 1]], base=0, channel_multiplier=0, allow_small_or_imprecise_dtypes=True).then_inc(S["consts"], 1)
            pool.iota(iota128[:], [[P, EC]], base=0, channel_multiplier=0, allow_small_or_imprecise_dtypes=True).then_inc(S["consts"], 1)
            pool.wait_ge(S["consts"], 4)
            pool.tensor_copy(ident16[:], ident[:]).then_inc(S["consts"], 1)

            def gather(it, stride, o, phase):
                t = o + stride * it
                b = o % GB
                table, hf = [0, 0, 0, 0, 1, 1][phase], phase % 2
                pool.wait_ge(S["msg_lo"], NT * phase + t + 1)
                pool.tensor_copy(ixb[:, b:b + 1], ix[:, table, ds(t, 1)]).then_inc(S["pool_idx"], 1)
                pool.wait_ge(S["pool_idx"], NT * phase + t + 1)
                pool.sem_inc(S["pool_nop"], 1)
                pool.indirect_dma_start(out=gat[:, b, :], out_offset=None, in_=U[hf][0:NP * (R0 if phase < 4 else R1), :],
                                        in_offset=bass.IndirectOffsetOnAxis(ap=ixb[:, b:b + 1], axis=0)).then_inc(g_in[b], 16)

            def gathers(phase, stored):
                for g in range(NG):
                    pool.wait_ge(u_st[g], 16 * stored)
                with pool.Fori(0, NT // GB) as it:
                    for o in range(GB):
                        gather(it, GB, o, phase)

            pool.wait_ge(S["srt_tab"], 1)
            gathers(0, ST_C1 + R0)
            gathers(1, ST_C1 + 2 * R0)
            gathers(2, ST_C2 + R0)
            gathers(3, ST_C2 + 2 * R0)
            gathers(4, ST_L1 + R1)
            gathers(5, ST_L1 + 2 * R1)

            def q_tiles(n):
                H, s = HEADS[n][0], A[n]

                def one(it, j, t):
                    k = 5 * (2 * it + j) + t
                    b = (5 * j + t) % 2
                    if t == 0:
                        pool.wait_ge(s[f"rm{j}"], 16 * it + 16)
                    pool.wait_ge(s["t_ok"], k + 1)
                    pool.tensor_tensor(qt[:, b, :], CT[:, t, :], rowM[:, j, :], ALU.subtract).then_inc(s["q_ok"], 1)
                if H == 1:
                    for t in range(NG):
                        one(0, 0, t)
                else:
                    with pool.Fori(0, H // 2) as it:
                        for j in range(2):
                            for t in range(NG):
                                one(it, j, t)
            for n in range(3):
                pool.sem_inc(A[n]["q_ok"], 10)
            pool.wait_ge(S["ct_ln"], 1)
            for n in range(3):
                q_tiles(n)

        @block.scalar
        def _(act):
            cp, rl = ACT.Copy, ACT.Relu

            def split(it, o):
                act.wait_ge(w_in[o % 2], 16 * (it + o // 2 + 1))
                act.wait_ge(S["steps"], 5 * (o + 2 * it) + 5)
                act.activation(w_hi[:, o % 2], raw[:, o % 2], cp).then_inc(S["w_hi"], 1)

            def evac(it, o, g, dst, stored):
                s = 5 * (o + 2 * it) + g
                act.wait_ge(S["steps"], s + 11)
                if stored is not None:
                    act.wait_ge(u_st[g], stored)
                act.activation(dst, ps[:, (o + g) % 2, 0:HALF] if len(dst.shape) == 2 else
                               ps[:, (o + g) % 2, 0:HALF].rearrange("p (h c) -> p h c", h=dst.shape[1]), cp).then_inc(S["evac"], 1)

            def ln(i):
                act.wait_ge(S["ln_var"], i + 1)
                act.activation(std[:], var[:], ACT.Sqrt).then_inc(S["ln_std"], 1)

            def transpose(k, fn):
                for kt in range(KT):
                    act.wait_ge(S["hT_tp"], KT * k + kt + 1)
                    b = 2 * (kt % 2)
                    act.activation(hT_hi[:, kt, :], psf[:, 512 * b:512 * b + NP], fn).then_inc(S["hT_hi"], 1)

            def msg(it, stride, o, phase):
                t = o + stride * it
                k = NT * phase + t
                act.wait_ge(g_in[o % GB], 16 * (NT // GB * phase + (stride // GB) * it + o // GB + 1))
                act.wait_ge(S["agg_pe"], k + 1)
                act.activation(msg_hi[:, o % 2, :], gat[:, o % GB, :], cp,
                               scale=wgt[:, [0, 0, 0, 0, 1, 1][phase], ds(t, 1)]).then_inc(S["msg_hi"], 1)

            def w_side(it, stride, o):
                t = o + stride * it
                act.wait_ge(S["w_tp"], t + 3)
                act.wait_ge(S["w_kg"], t + 1)
                act.activation(ohT[:, o % 2, :], ps[:, 6 + o % 2, 0:64].bitcast(F16), cp).then_inc(S["w_cp"], 1)

            def none(it, stride, o):
                pass

            def phase(q0, nr, stride, n_it, st0, side0, side1):
                for hf, side in ((0, side0), (1, side1)):
                    o = q0 + hf * (nr + 1)
                    st = st0 + hf * nr

                    def pair(it, sides, first=False):
                        for j in range(2):
                            split(it, o + j + 1)
                            for g in range(NG):
                                evac(it, o + j, g, ust[:, g, :], None if first and j == 0 else 16 * (st + 2 * it + j))
                                if sides:
                                    for t in sides_at(stride, 5 * j + g):
                                        side(it, stride, t)
                    lo = 0
                    if st == 0:
                        pair(0, True, True)
                        lo = 1
                    with act.Fori(lo, n_it) as it:
                        pair(it, True)
                    if n_it < nr // 2:
                        with act.Fori(n_it, nr // 2) as it:
                            pair(it, False)
                    if o + nr + 1 < Q_END:
                        split(0, o + nr + 1)
                    for g in range(NG):
                        evac(0, o + nr, g, R[:, g, hf * HALF:(hf + 1) * HALF], None)
                        t = stride * n_it + g
                        if t < NT:
                            side(0, stride, t)
                    if st == 0:
                        act.wait_ge(S["w_done"], NT + 2)

            def tail(ph):
                with act.Fori(0, NT // GB) as it:
                    for o in range(GB):
                        msg(it, GB, o, ph)

            act.wait_ge(S["consts"], 12)
            act.sem_inc(S["evac"], 2)
            act.sem_inc(S["w_cp"], 2)
            ln(0)
            split(0, 0)
            transpose(0, rl)
            phase(Q_C1, R0, 20, R0 // 2, ST_C1, w_side, lambda it, st, o: msg(it, st, o, 0))
            tail(1)
            transpose(1, rl)
            phase(Q_C2, R0, 20, R0 // 2, ST_C2, none, lambda it, st, o: msg(it, st, o, 2))
            tail(3)
            ln(1)
            transpose(2, rl)
            phase(Q_L1, R1, 12, NT // 12, ST_L1, none, lambda it, st, o: msg(it, st, o, 4))
            tail(5)
            for s in range(NG):
                act.wait_ge(S["ct_tp"], s + 1)
                b = 4 + 2 * (s % 2)
                act.activation(CT[:, s, :], psf[:, 512 * b:512 * b + NP], cp).then_inc(S["ct_cp"], 1)
            act.wait_ge(S["deg_ok"], 1)
            act.activation(std[:], deg[:], ACT.Sqrt).then_inc(S["deg_sq"], 1)
            transpose(3, cp)

            def dense(q, dst):
                for k in range(2):
                    if q + k + 1 < Q_SPLIT[q]:
                        split(0, q + k + 1)
                    for g in range(NG):
                        evac(0, q + k, g, dst(g, k), None)
            dense(Q_GCN, lambda g, k: R[:, g, k * HALF:(k + 1) * HALF])
            ln(2)
            transpose(4, rl)
            act.wait_ge(S["ln_c"], 1)
            act.activation(CT, CT, ACT.Ln).then_inc(S["ln_cc"], 1)
            dense(Q_G1, lambda g, k: R[:, g, 0:H2 * (C2 + 1)].rearrange("p (h c) -> p h c", c=C2 + 1)[:, 4 * k:4 * k + 4, 0:C2])

            def rows(n):
                H, s = HEADS[n][0], A[n]
                for k in range(3):
                    act.wait_ge(s["al_tp"], k + 1)
                    act.activation(alT[0:H, k, :], psf[0:H, 1024 * (k % 2):1024 * (k % 2) + NP], cp).then_inc(s["al_cp"], 1)

            def tiles_(n, out_tile):
                H, s = HEADS[n][0], A[n]
                act.sem_inc(s["z_ok"], 10)

                def z(it, j, t):
                    k = 5 * (2 * it + j) + t
                    if t == 0:
                        act.wait_ge(s[f"rs{j}"], 16 * it + 16 * (max(1, H // 2) + 1))
                    act.wait_ge(s["l_ok"], k + 1)
                    act.activation(zt[:, (5 * j + t) % 2, :], rowS[:, j, :], ACT.Identity,
                                   bias=al[:, 0, t, ds(2 * it + j, 1)]).then_inc(s["z_ok"], 1)

                def e(it, j, t):
                    k = 5 * (2 * it + j) + t
                    b = (5 * j + t) % 2
                    act.wait_ge(s["t_ok"], k + 3)
                    if H > 1:
                        act.wait_ge(s["o_mm"], k + 1)
                    act.activation(out_tile(b, t), lt[:, b, :], ACT.Exp).then_inc(s["p_ok"], 1)

                def heads(it, nj):
                    for i in range(5 * nj):
                        z(it, i // 5, i % 5)
                        if i:
                            e(it, (i - 1) // 5, (i - 1) % 5)
                    e(it, nj - 1, NG - 1)
                if H == 1:
                    heads(0, 1)
                else:
                    with act.Fori(0, H // 2) as it:
                        heads(it, 2)

            rows(0)
            tiles_(0, lambda b, t: pt[:, b, :])
            act.wait_ge(S["elu_m"], 1)
            act.activation(R[:, :, 0:D], R[:, :, 0:D], ACT.Exp).then_inc(S["elu_e"], 1)
            split(0, Q_G2)
            transpose(5, cp)
            dense(Q_G2, lambda g, k: R[:, g, k * HALF:(k + 1) * HALF])
            rows(1)
            tiles_(1, lambda b, t: h[:, t, 0:NP])
            ln(3)
            transpose(6, rl)
            for i in range(2 * NG):
                g = i // 2
                act.wait_ge(S["ft_mm"], i + 1)
                src = psf[:, 1024 * (i % 4):1024 * (i % 4) + D]
                if i % 2 == 0:
                    act.activation(R[:, g, :].rearrange("p (h c) -> p h c", c=C3 + 1)[:, :, 0:C3],
                                   src.rearrange("p (h c) -> p h c", c=C3), cp).then_inc(S["ft_ev"], 1)
                else:
                    act.activation(h[:, g, :], src, cp).then_inc(S["ft_ev"], 1)
            rows(2)
            tiles_(2, lambda b, t: pt[:, b, :])

        @block.vector
        def _(dve):
            n_chain = [0]

            def link(ins):
                n_chain[0] += 1
                ins.then_inc(S["chain"], 1)
                dve.wait_ge(S["chain"], n_chain[0])

            def ln(i):
                for g in range(NG):
                    for k in range(2):
                        ins = dve.bn_stats(bst[:, g, k, :], x[:, g, k * HALF:(k + 1) * HALF])
                link(ins)
                for g in range(NG):
                    ins = dve.bn_aggr(mv[:, g, :], bst[:, g, :, :])
                link(ins)
                dve.tensor_scalar(var[:], mv[:, :, 1], EPS, None, ALU.add).then_inc(S["ln_var"], 1)
                dve.wait_ge(S["ln_std"], i + 1)
                link(dve.reciprocal(rstd[:], std[:]))
                for g in range(NG):
                    dve.tensor_scalar(h[:, g, :], x[:, g, :], mv[:, g, 0:1], rstd[:, g:g + 1],
                                      ALU.subtract, ALU.mult).then_inc(S["ln_h"], 1)

            def transpose(k, relu):
                for kt in range(KT):
                    dve.wait_ge(S["hT_hi"], KT * k + kt + 1)
                    b = 2 * (kt % 2)
                    src, hi = psf[:, 512 * b:512 * b + NP], hT_hi[:, kt, :].bitcast(F32)
                    if relu:
                        dve.scalar_tensor_tensor(hT_lo[:, kt, :], src, 0.0, hi, ALU.max, ALU.subtract).then_inc(S["hT_lo"], 1)
                    else:
                        dve.tensor_tensor(hT_lo[:, kt, :], src, hi, ALU.subtract).then_inc(S["hT_lo"], 1)

            def split(it, o):
                dve.wait_ge(S["w_hi"], o + 2 * it + 1)
                dve.tensor_tensor(w_lo[:, o % 2], raw[:, o % 2], w_hi[:, o % 2].bitcast(F32), ALU.subtract).then_inc(S["w_lo"], 1)

            def sort():
                dve.wait_ge(S["edges_in"], 64)
                link(dve.tensor_copy(e_f[:], e_i[:]))
                for j in range(NG + 1):
                    ins = dve.tensor_scalar(ge[:, j, :], e_f[:, 1, :], float(P * j), None, ALU.is_ge)
                link(ins)
                link(dve.tensor_tensor(grp1[:], ge[:, 0:NG, :], ge[:, 1:NG + 1, :], ALU.subtract))
                for g in range(NG):
                    ins = dve.tensor_tensor_scan(pre[:, g, :], grp1[:, g, :], zer[:], 0.0, ALU.add, ALU.add)
                link(ins)
                dve.tensor_copy(rs[:], pre[:, :, EC - 1]).then_inc(S["srt_rs"], 1)
                dve.tensor_scalar(vals[:, :, 0], e_f[:, 0, :], 1.0, None, ALU.add)
                dve.tensor_copy(vals[:, :, 2], e_f[:, 2, :])
                dve.tensor_copy(vals[:, :, 3], e_f[:, 3, :])
                link(dve.tensor_reduce(hi_f[:], ge[:, 1:NG, :].rearrange("p g c -> p c g"), AX.X, ALU.add))
                link(dve.scalar_tensor_tensor(lo_f[:], hi_f[:], -float(P), e_f[:, 1, :], ALU.mult, ALU.add))
                link(dve.tensor_scalar(vals[:, :, 1], lo_f[:], 1.0, None, ALU.add))
                dve.wait_ge(S["srt_ps"], 1)
                link(dve.tensor_copy(tot[:], ps[:, 6, 0:NG]))
                for g in range(NG):
                    ins = dve.tensor_scalar(ntl[:, g, :], iota128[:], tot[:, g:g + 1], None, ALU.is_lt)
                link(ins)
                link(dve.tensor_reduce(tiles[:], ntl[:], AX.X, ALU.add))
                link(dve.tensor_tensor_scan(tbi[:], tiles[:], z16[:, 0:NG], 0.0, ALU.add, ALU.add))
                link(dve.tensor_tensor(tb[:], tbi[:], tiles[:], ALU.subtract))
                link(dve.scalar_tensor_tensor(off[:], tb[0:EP, :], float(P), ps[0:EP, 7, 0:NG], ALU.mult, ALU.add))
                for g in range(NG):
                    ins = dve.scalar_tensor_tensor(pre[:, g, :], pre[:, g, :], off[:, g:g + 1], grp1[:, g, :], ALU.add, ALU.mult)
                link(ins)
                link(dve.tensor_reduce(pos[:], pre[:].rearrange("p g c -> p c g"), AX.X, ALU.add))
                link(dve.tensor_scalar(pos_i[:], pos[:], -1.0, None, ALU.add))
                link(dve.tensor_single_scalar(hi_i[:], pos_i[:], 7, ALU.arith_shift_right))
                link(dve.tensor_copy(hi_f[:], hi_i[:]))
                link(dve.scalar_tensor_tensor(lo_f[:], hi_f[:], -float(P), pos[:], ALU.mult, ALU.add))
                for s in range(EC // RC):
                    b, c0 = s % 2, s * RC
                    if s >= 1:
                        dve.wait_ge(S["srt_rhs"], s)
                    if s >= 2:
                        dve.wait_ge(S["srt_mm"], s - 1)
                    dve.tensor_tensor(oh_lo[0:EP, b], lo_f[:, c0:c0 + RC].unsqueeze(2).to_broadcast([EP, RC, P]),
                                      iota[0:EP, 1:P + 1].unsqueeze(1).to_broadcast([EP, RC, P]), ALU.is_equal)
                    link(dve.tensor_tensor(oh_hi[0:EP], hi_f[:, c0:c0 + RC].unsqueeze(2).to_broadcast([EP, RC, NT]),
                                           iota[0:EP, 0:NT].unsqueeze(1).to_broadcast([EP, RC, NT]), ALU.is_equal))
                    dve.tensor_tensor(val_hi[0:EP, b], oh_hi[0:EP].unsqueeze(2).to_broadcast([EP, RC, 4, NT]),
                                      vals[:, c0:c0 + RC, :].unsqueeze(3).to_broadcast([EP, RC, 4, NT]), ALU.mult).then_inc(S["srt_rhs"], 1)
                dve.wait_ge(S["srt_mm"], EC // RC)
                link(dve.tensor_copy(tab[:].rearrange("p v t -> p (v t)"), ps[:, 5, 0:4 * NT]))
                for k in range(NG - 1):
                    dve.tensor_scalar(gt[:, k, :], iota[:, 0:NT], tb[:, k + 1:k + 2], None, ALU.is_ge)
                for k in range(2):
                    ins = dve.scalar_tensor_tensor(ix_f[:, k, :], tab[:, 2 + k, :], float(NP), tab[:, 0, :], ALU.mult, ALU.add)
                link(ins)
                dve.tensor_scalar(ix[:], ix_f[:], -1.0, 0.0, ALU.add, ALU.max)
                link(dve.tensor_reduce(grp_f[:], gt[:].rearrange("p k t -> p t k"), AX.X, ALU.add))
                dve.tensor_copy(grp[:], grp_f[:]).then_inc(S["srt_tab"], 1)

            def one_hot_dst(b, t):
                return dve.tensor_scalar(oh_d[:, b, :], iota16[:, 1:P + 1], tab[:, 1, ds(t, 1)], None, ALU.is_equal)

            def count():
                with dve.Fori(0, NT // 2) as it:
                    for j in range(2):
                        t = 2 * it + j
                        dve.wait_ge(S["cnt_pe"], t + 1)
                        one_hot_dst(j, t)
                        dve.tensor_scalar(oh_r[:, j, 0:R0], iota16[:, 0:R0], tab[:, 2, ds(t, 1)], None, ALU.is_equal)
                        dve.tensor_scalar(oh_r[:, j, R0:R0 + R1], iota16[:, 0:R1], tab[:, 3, ds(t, 1)], None, ALU.is_equal).then_inc(S["cnt_oh"], 1)
                dve.wait_ge(S["cnt_pe"], NT + 2)
                link(dve.tensor_scalar(kinv[:].rearrange("p g n -> p (g n)"), ps[:, 6, 0:64 * NG], 1.0, None, ALU.max))
                dve.reciprocal(kinv[:], kinv[:]).then_inc(S["k_inv"], 1)

            def weigh(t):
                b = t[1]
                t = t[0]
                dve.wait_ge(S["w_kg"], t + 3)
                kg = ps[:, 4 + b, 0:R0 + R1]
                dve.scalar_tensor_tensor(kprod[:, b, 0:R0], iota16[:, 0:R0], tab[:, 2, ds(t, 1)], kg[:, 0:R0], ALU.is_equal, ALU.mult)
                dve.scalar_tensor_tensor(kprod[:, b, R0:R0 + R1], iota16[:, 0:R1], tab[:, 3, ds(t, 1)], kg[:, R0:R0 + R1], ALU.is_equal, ALU.mult).then_inc(S["w_pr"], 1)
                dve.wait_ge(S["w_pr"], t + 1)
                dve.tensor_reduce(wgt[:, 0, ds(t, 1)], kprod[:, b, 0:R0], AX.X, ALU.add)
                dve.tensor_reduce(wgt[:, 1, ds(t, 1)], kprod[:, b, R0:R0 + R1], AX.X, ALU.add).then_inc(S["w_done"], 1)

            def w_side(it, stride, o):
                t = o + stride * it
                dve.wait_ge(S["w_tp"], t + 1)
                one_hot_dst(o % 2, t).then_inc(S["w_oh"], 1)
                if not (isinstance(t, int) and t < 2):
                    weigh((t - 2, o % 2))

            def c_side(part):
                def side(it, stride, o):
                    t = o + stride * it
                    dve.wait_ge(S["c_pe"], NT * part + t + 1)
                    one_hot_dst(o % 2, t)
                    dve.tensor_scalar(oh_s[:, o % 2, :], iota16[:, 1 + CW * part:1 + CW * (part + 1)], tab[:, 0, ds(t, 1)],
                                      None, ALU.is_equal).then_inc(S["c_oh"], 1)
                return side

            def msg(it, stride, o, ph):
                t = o + stride * it
                b = o % 2
                dve.wait_ge(S["msg_hi"], NT * ph + t + 1)
                dve.tensor_scalar(onehot[:, b, :], iota[:, 1:P + 1], tab[:, 1, ds(t, 1)], None, ALU.is_equal)
                dve.scalar_tensor_tensor(msg_lo[:, b, :], gat[:, o % GB, :], wgt[:, [0, 0, 0, 0, 1, 1][ph], ds(t, 1)],
                                         msg_hi[:, b, :].bitcast(F32), ALU.mult, ALU.subtract).then_inc(S["msg_lo"], 1)

            def phase(q0, nr, stride, n_it, st0, side0, side1, v, after0, after1):
                for hf, side in ((0, side0), (1, side1)):
                    o = q0 + hf * (nr + 1)

                    def pair(it, sides):
                        for j in range(2):
                            split(it, o + j + 1)
                            if sides:
                                for g in range(NG):
                                    for t in sides_at(stride, 5 * j + g):
                                        side(it, stride, t)
                    lo = 0
                    if st0 + hf == 0:
                        pair(0, True)
                        lo = 1
                    with dve.Fori(lo, n_it) as it:
                        pair(it, True)
                    if n_it < nr // 2:
                        with dve.Fori(n_it, nr // 2) as it:
                            pair(it, False)
                    split(0, o + nr + 1)
                    for g in range(NG):
                        if stride * n_it + g < NT:
                            side(0, stride, stride * n_it + g)
                    dve.wait_ge(S["evac"], 5 * (o + nr + 1) + 2)
                    dve.wait_ge(v_in[v % 2], 16 * (v // 2 + 1))
                    rh = R[:, :, hf * HALF:(hf + 1) * HALF]
                    ins = dve.tensor_tensor(rh, rh, vec[:, v % 2, hf * HALF:(hf + 1) * HALF].unsqueeze(1).to_broadcast([P, NG, HALF]), ALU.add)
                    if hf == 1:
                        ins.then_inc(S["vec_ok"], 1)
                    (after0 if hf == 0 else after1)()

            def counts_out(part):
                dve.wait_ge(S["c_pe"], NT * (part + 1) + 2)
                dve.tensor_copy(C[:, :, CW * part:CW * (part + 1)], ps[:, 2:2 + NG, 0:CW]).then_inc(S["acc_out"], 1)

            def sums_out(ph, into_x):
                hf = ph % 2
                cols = slice(hf * HALF, (hf + 1) * HALF)
                dve.wait_ge(S["agg_pe"], NT * (ph + 1) + 2)
                if into_x:
                    link(dve.tensor_tensor(R[:, :, cols], R[:, :, cols], ps[:, 2:2 + NG, 0:HALF], ALU.add))
                    ins = dve.tensor_tensor(x[:, :, cols], x[:, :, cols], R[:, :, cols], ALU.add)
                else:
                    ins = dve.tensor_tensor(h[:, :, cols], R[:, :, cols], ps[:, 2:2 + NG, 0:HALF], ALU.add)
                ins.then_inc(S["acc_out"], 1)

            def tail(ph):
                with dve.Fori(0, NT // GB) as it:
                    for o in range(GB):
                        msg(it, GB, o, ph)

            dve.wait_ge(S["consts"], 12)
            dve.sem_inc(S["w_lo"], 2)
            dve.sem_inc(S["msg_lo"], GB)
            dve.sem_inc(S["w_done"], 2)
            dve.wait_ge(S["x_in"], 32)
            ln(0)
            split(0, 0)
            transpose(0, True)
            dve.wait_ge(S["bd_z"], 1)
            dve.wait_ge(S["bd_tp"], 1)
            for k in range(2):
                for i in range(2):
                    r = slice(64 * i, 64 * i + 64)
                    ins = dve.tensor_copy(bd[r, k, r], ps[r, 4, 64 * k:64 * k + 64])
            link(ins)
            link(dve.tensor_copy(bd_hi[:], bd[:]))
            link(dve.tensor_tensor(bd_lo[:], bd[:], bd_hi[:].bitcast(F32), ALU.subtract))
            dve.sem_inc(S["bd_ok"], 1)
            sort()
            count()

            def w_end():
                for t in (NT - 2, NT - 1):
                    weigh((t, t % 2))
                dve.wait_ge(S["w_done"], NT + 2)
            phase(Q_C1, R0, 20, R0 // 2, ST_C1, w_side, lambda it, st, o: msg(it, st, o, 0), 0, w_end, lambda: sums_out(0, False))
            tail(1)
            sums_out(1, False)
            transpose(1, True)
            phase(Q_C2, R0, 20, R0 // 2, ST_C2, c_side(0), lambda it, st, o: msg(it, st, o, 2), 1, lambda: counts_out(0), lambda: sums_out(2, True))
            tail(3)
            sums_out(3, True)
            dve.wait_ge(S["acc_out"], 5)
            ln(1)
            transpose(2, True)
            phase(Q_L1, R1, 12, NT // 12, ST_L1, c_side(1), lambda it, st, o: msg(it, st, o, 4), 2, lambda: counts_out(1), lambda: sums_out(4, False))
            tail(5)
            sums_out(5, False)
            link(dve.tensor_reduce(deg[:], C, AX.X, ALU.add))
            link(dve.tensor_scalar(deg[:], deg[:], 1.0, None, ALU.add))
            dve.sem_inc(S["deg_ok"], 1)
            dve.wait_ge(S["ct_tp"], NG)
            dve.tensor_scalar(C, C, 0.0, NEG, ALU.is_equal, ALU.mult)
            dve.wait_ge(S["deg_sq"], 1)
            link(dve.reciprocal(dinv[:], std[:]))
            transpose(3, False)
            for k in range(2):
                if Q_GCN + k + 1 < Q_SPLIT[Q_GCN]:
                    split(0, Q_GCN + k + 1)
            dve.wait_ge(v_in[1], 32)
            dve.tensor_tensor(x[:], x[:], vec[:, 1, :].unsqueeze(1).to_broadcast([P, NG, D]), ALU.add).then_inc(S["vec_ok"], 1)
            dve.wait_ge(S["vec_ok"], 4)
            dve.wait_ge(S["evac"], 5 * (Q_GCN + 2) + 2)
            for g in range(NG):
                dve.tensor_scalar(R[:, g, 0:D], R[:, g, 0:D], dinv[:, g:g + 1], None, ALU.mult).then_inc(S["gcn_y"], 1)
            for i in range(2 * NG):
                j, cols = i // 2, slice((i % 2) * HALF, (i % 2 + 1) * HALF)
                dve.wait_ge(S["gcn_mm"], i + 1)
                ins = dve.scalar_tensor_tensor(x[:, j, cols], ps[:, 2 + i % 2, 0:HALF], dinv[:, j:j + 1], x[:, j, cols], ALU.mult, ALU.add)
                ins.then_inc(S["gcn_ev"], 1)
            dve.wait_ge(S["gcn_ev"], 2 * NG)
            ln(2)
            transpose(4, True)
            dve.wait_ge(S["hT_tp"], 5 * KT)
            link(dve.tensor_scalar(h[:, :, 0:NP], CT, 0.0, NEG, ALU.is_equal, ALU.mult))
            dve.tensor_scalar(CT, CT, 1.0, None, ALU.max).then_inc(S["ln_c"], 1)
            split(0, Q_G1 + 1)
            dve.wait_ge(S["ln_cc"], 1)
            dve.tensor_tensor(CT, CT, h[:, :, 0:NP], ALU.add).then_inc(S["ct_ln"], 1)

            def heads_of(n, g):
                H, c = HEADS[n]
                return R[:, g, 0:H * (c + 1)].rearrange("p (h c) -> p h c", c=c + 1) if H > 1 else R[:, g, 0:c].unsqueeze(1)

            def scores(n, v):
                H, c = HEADS[n]
                i = 0
                for k in range(2):
                    dve.wait_ge(v_in[v % 2], 16 * (v // 2 + 1))
                    for g in range(NG):
                        t = arena[:, 2560 + 1280 * (i % 2):2560 + 1280 * (i % 2) + D].rearrange("p (h c) -> p h c", c=c)
                        link(dve.tensor_tensor(t, heads_of(n, g)[:, :, 0:c], vec[:, v % 2, :].rearrange("p (h c) -> p h c", c=c), ALU.mult))
                        link(dve.tensor_reduce(al[:, k, g, 0:H], t, AX.X, ALU.add))
                        i += 1
                    dve.sem_inc(A[n]["al_ok"], 1)
                    dve.sem_inc(S["vec_ok"], 1)
                    v += 1

            def maxima(n):
                H, s = HEADS[n][0], A[n]

                def one(it, j):
                    hd = 2 * it + j
                    dve.wait_ge(s[f"rs{j}"], 16 * it + 16)
                    dve.wait_ge(s["seg"], hd + 2)
                    dve.sem_inc(S["dve_nop"], 1)
                    for g in range(NG):
                        t = arena[:, 2560 + NP * g:2560 + NP * (g + 1)]
                        ins = dve.tensor_tensor_reduce(t, rowS[:, j, :], C[:, g, :], 1.0, -3.0e38, ALU.add, ALU.max, mxt[:, j, g:g + 1])
                    ins.then_inc(s["o_r"], 1)
                    dve.wait_ge(s["o_r"], hd + 1)
                    dve.tensor_copy(mz[:, :, ds(hd, 1)], mxt[:, j, :].unsqueeze(2)).then_inc(s["seg"], 1)
                if H == 1:
                    one(0, 0)
                else:
                    with dve.Fori(0, H // 2) as it:
                        for j in range(2):
                            one(it, j)
                dve.wait_ge(s["seg"], H + 2)
                link(dve.tensor_tensor(mz[:, :, 0:H], mz[:, :, 0:H], al[:, 1, :, 0:H], ALU.add))
                dve.scalar_tensor_tensor(al[:, 2, :, 0:H], mz[:, :, 0:H], 0.2, mz[:, :, 0:H], ALU.mult, ALU.max).then_inc(s["al_ok"], 1)

            def leaky(n, it, j, t):
                s = A[n]
                k = 5 * (2 * it + j) + t
                b = (5 * j + t) % 2
                dve.wait_ge(s["z_ok"], k + 11)
                dve.wait_ge(s["p_ok"], k + 1)
                dve.scalar_tensor_tensor(lt[:, b, :], zt[:, b, :], 0.2, zt[:, b, :], ALU.mult, ALU.max).then_inc(s["l_ok"], 1)
                dve.wait_ge(s["q_ok"], k + 11)
                dve.wait_ge(s["l_ok"], k + 3)
                dve.tensor_tensor(lt[:, b, :], lt[:, b, :], qt[:, b, :], ALU.add).then_inc(s["t_ok"], 1)

            def head_out(n, it, j, put, steps):
                H, c = HEADS[n]
                s = A[n]
                hd = 2 * it + j
                base = H + steps * hd
                o = ps[:, 6 + j, 0:NG * (c + 1)].rearrange("p (g c) -> p g c", c=c + 1)
                dve.wait_ge(s["o_mm"], 5 * hd + 7)
                dve.tensor_scalar(rz[:, j, :].unsqueeze(2), o[:, :, c:c + 1], 1e-16, None, ALU.add if n == 0 else ALU.max).then_inc(s["o_r"], 1)
                dve.wait_ge(s["o_r"], base + 1)
                dve.reciprocal(rz[:, j, :], rz[:, j, :]).then_inc(s["o_r"], 1)
                dve.wait_ge(s["o_r"], base + 2)
                put(hd, o[:, :, 0:c], rz[:, j, :].unsqueeze(2).to_broadcast([P, NG, c]), s, base)

            def all_heads(n, put, steps):
                H = HEADS[n][0]
                with dve.Fori(0, H // 2) as it:
                    for i in range(10):
                        leaky(n, it, i // 5, i % 5)
                        if i == 6:
                            head_out(n, it, 0, put, steps)
                    head_out(n, it, 1, put, steps)

            for n in range(3):
                for m, c in (("seg", 2), ("l_ok", 2), ("t_ok", 2)):
                    dve.sem_inc(A[n][m], c)

            dve.memset(R[:, :, 0:H2 * (C2 + 1)].rearrange("p g (h c) -> p g h c", c=C2 + 1)[:, :, :, C2:C2 + 1], 1.0).then_inc(S["bd_ok"], 1)
            dve.wait_ge(S["evac"], 5 * Q_G2 + 2)
            scores(0, 4)
            maxima(0)
            all_heads(0, lambda hd, o, r, s, base: dve.tensor_tensor(h[:, :, ds(hd * C2, C2)], o, r, ALU.mult).then_inc(s["o_ev"], 1), 2)
            dve.wait_ge(A[0]["o_ev"], H2 + 2)
            dve.wait_ge(v_in[0], 64)
            link(dve.tensor_tensor(h[:], h[:], vec[:, 0, :].unsqueeze(1).to_broadcast([P, NG, D]), ALU.add))
            dve.sem_inc(S["vec_ok"], 1)
            dve.tensor_scalar(R[:, :, 0:D], h[:], 0.0, None, ALU.min).then_inc(S["elu_m"], 1)
            dve.wait_ge(S["elu_m"], 1)
            link(dve.tensor_scalar(h[:], h[:], 0.0, None, ALU.max))
            dve.wait_ge(S["elu_e"], 1)
            dve.scalar_tensor_tensor(h[:], R[:, :, 0:D], -1.0, h[:], ALU.add, ALU.add).then_inc(S["elu_v"], 1)
            dve.wait_ge(S["elu_v"], 1)
            dve.memset(R[:, :, D:D + 1], 1.0).then_inc(S["bd_ok"], 1)
            split(0, Q_G2)
            transpose(5, False)
            split(0, Q_G2 + 1)
            dve.wait_ge(S["evac"], 5 * Q_END + 2)
            scores(1, 7)
            maxima(1)
            for t in range(NG):
                leaky(1, 0, 0, t)
            dve.wait_ge(v_in[1], 80)
            link(dve.tensor_tensor(x[:], x[:], vec[:, 1, :].unsqueeze(1).to_broadcast([P, NG, D]), ALU.add))
            dve.sem_inc(S["vec_ok"], 1)
            for g in range(NG):
                b = 4 + 2 * (g % 2)
                dve.wait_ge(A[1]["o_mm"], g + 1)
                link(dve.tensor_scalar(rz[:, 0, g:g + 1], ps[:, b + 1, HALF:HALF + 1], 1e-16, None, ALU.add))
                link(dve.reciprocal(rz[:, 0, g:g + 1], rz[:, 0, g:g + 1]))
                for k in range(2):
                    cols = slice(k * HALF, (k + 1) * HALF)
                    ins = dve.scalar_tensor_tensor(x[:, g, cols], ps[:, b + k, 0:HALF], rz[:, 0, g:g + 1], x[:, g, cols], ALU.mult, ALU.add)
                ins.then_inc(A[1]["o_ev"], 1)
            dve.wait_ge(A[1]["o_ev"], NG)
            dve.memset(R[:, :, :].rearrange("p g (h c) -> p g h c", c=C3 + 1)[:, :, :, C3:C3 + 1], 1.0).then_inc(S["bd_ok"], 1)
            ln(3)
            transpose(6, True)
            dve.wait_ge(S["ft_ev"], 2 * NG)
            scores(2, 10)
            maxima(2)

            def residual(hd, o, r, s, base):
                t = kinv[:]
                cols = ds(hd * C3, C3)
                dve.tensor_tensor(t, o, r, ALU.mult).then_inc(s["o_r"], 1)
                dve.wait_ge(s["o_r"], base + 3)
                dve.tensor_tensor(t, t, h[:, :, cols], ALU.add).then_inc(s["o_r"], 1)
                dve.wait_ge(s["o_r"], base + 4)
                dve.scalar_tensor_tensor(x[:, :, cols], t, 0.0, x[:, :, cols], ALU.max, ALU.add).then_inc(s["o_ev"], 1)
                dve.wait_ge(s["o_ev"], hd + 3)
            all_heads(2, residual, 4)
            dve.sem_inc(S["x_ok"], 1)

        @block.tensor
        def _(pe):
            def transpose(k):
                for kt in range(KT):
                    b = 2 * (kt % 2)
                    if kt >= 2:
                        pe.wait_ge(S["hT_lo"], KT * k + kt - 1)
                    for g in range(NG):
                        ins = pe.transpose(psf[:, 512 * b + P * g:512 * b + P * (g + 1)], h[:, g, P * kt:P * (kt + 1)], ident[:])
                    ins.then_inc(S["hT_tp"], 1)

            def step(it, o, g):
                s = 5 * (o + 2 * it) + g
                if g == 0:
                    pe.wait_ge(S["w_lo"], o + 2 * it + 3)
                pe.wait_ge(S["evac"], s + 1)
                acc = ps[:, (o + g) % 2, 0:HALF]
                n = 0
                for kt in range(KT):
                    hi, lo = hT_hi[:, kt, P * g:P * (g + 1)], hT_lo[:, kt, P * g:P * (g + 1)]
                    for l, r in ((hi, w_hi), (hi, w_lo), (lo, w_hi)):
                        ins = pe.matmul(acc, l, r[:, o % 2, kt, :], start=(n == 0), stop=(n == 3 * KT - 1))
                        n += 1
                ins.then_inc(S["steps"], 1)

            def group(t):
                return pe.value_load(grp[0:1, ds(t, 1)], min_val=0, max_val=NG - 1)

            def bank(g, n):
                return ps[:, ds(g + 2, 1), 0:n].rearrange("p a n -> p (a n)")

            def clear(i):
                if i:
                    pe.wait_ge(S["acc_out"], i)
                else:
                    pe.wait_ge(S["w_done"], NT + 2)
                for g in range(NG):
                    pe.matmul(ps[:, 2 + g, :], z16[:, 0:P], z16[:], start=True, stop=True)

            def gains(t, b):
                g = group(t)
                pe.wait_ge(S["w_cp"], t + 3)
                pe.wait_ge(S["w_done"], t + 1)
                pe.matmul(ps[:, 4 + b, 0:R0 + R1], ohT[:, b, :],
                          kinv[:, ds(g, 1), 0:R0 + R1].rearrange("p a n -> p (a n)"), start=True, stop=True).then_inc(S["w_kg"], 1)

            def w_side(it, stride, o):
                t = o + stride * it
                if not (isinstance(t, int) and t < 2):
                    gains(t - 2, o % 2)
                pe.wait_ge(S["w_oh"], t + 1)
                pe.wait_ge(S["w_cp"], t + 1)
                pe.transpose(ps[:, 6 + o % 2, 0:64].bitcast(F16), oh_d[:, o % 2, :], ident16[:]).then_inc(S["w_tp"], 1)

            def c_side(part):
                def side(it, stride, o):
                    t = o + stride * it
                    g = group(t)
                    pe.wait_ge(S["c_oh"], NT * part + t + 1)
                    pe.matmul(bank(g, CW), oh_d[:, o % 2, :], oh_s[:, o % 2, :], start=False, stop=True, skip_group_check=True).then_inc(S["c_pe"], 1)
                return side

            def msg(it, stride, o, ph):
                t = o + stride * it
                b = o % 2
                g = group(t)
                pe.wait_ge(S["msg_lo"], NT * ph + t + 1 + GB)
                pe.matmul(bank(g, HALF), onehot[:, b, :], msg_hi[:, b, :], start=False, stop=False, skip_group_check=True)
                pe.matmul(bank(g, HALF), onehot[:, b, :], msg_lo[:, b, :], start=False, stop=True, skip_group_check=True).then_inc(S["agg_pe"], 1)

            def phase(q0, nr, stride, n_it, st0, side0, side1, clear0, clear1, end0=None):
                for hf, side in ((0, side0), (1, side1)):
                    o = q0 + hf * (nr + 1)
                    i = (clear0, clear1)[hf]
                    if i is not None:
                        clear(i)

                    def pair(it, sides):
                        for j in range(2):
                            for g in range(NG):
                                step(it, o + j, g)
                                if sides:
                                    for t in sides_at(stride, 5 * j + g):
                                        side(it, stride, t)
                    lo = 0
                    if st0 + hf == 0:
                        pair(0, True)
                        lo = 1
                    with pe.Fori(lo, n_it) as it:
                        pair(it, True)
                    if n_it < nr // 2:
                        with pe.Fori(n_it, nr // 2) as it:
                            pair(it, False)
                    for g in range(NG):
                        step(0, o + nr, g)
                        if stride * n_it + g < NT:
                            side(0, stride, stride * n_it + g)
                    if hf == 0 and end0:
                        end0()

            def tail(ph, i):
                clear(i)
                with pe.Fori(0, NT // GB) as it:
                    for o in range(GB):
                        msg(it, GB, o, ph)

            pe.sem_inc(S["steps"], 10)
            pe.sem_inc(S["cnt_pe"], 2)
            pe.sem_inc(S["c_pe"], 2)
            pe.sem_inc(S["agg_pe"], 2)
            pe.sem_inc(S["w_tp"], 2)
            pe.sem_inc(S["w_kg"], 2)
            pe.wait_ge(S["consts"], 12)
            pe.wait_ge(S["ln_h"], NG)
            transpose(0)
            pe.wait_ge(S["w64_in"], 64)
            for k in range(2):
                ins = pe.transpose(ps[:, 4, 64 * k:64 * k + 64], w64[:, k, :], ident[0:64, 0:64])
            ins.then_inc(S["bd_tp"], 1)
            pe.wait_ge(S["srt_rs"], 1)
            pe.matmul(ps[0:EP, 7, 0:NG], below[:], rs[:], start=True, stop=True)
            pe.matmul(ps[:, 6, 0:NG], ones[0:EP, :], rs[:], start=True, stop=True).then_inc(S["srt_ps"], 1)
            for s in range(EC // RC):
                pe.wait_ge(S["srt_rhs"], s + 1)
                for c in range(RC):
                    ins = pe.matmul(ps[:, 5, 0:4 * NT], oh_lo[0:EP, s % 2, c, :], val_hi[0:EP, s % 2, c].rearrange("p v n -> p (v n)"),
                                    start=(s + c == 0), stop=(s * RC + c == EC - 1))
                ins.then_inc(S["srt_mm"], 1)
            pe.wait_ge(S["srt_tab"], 1)
            pe.matmul(ps[:, 6, :], z16[:, 0:P], z16[:], start=True, stop=True)
            with pe.Fori(0, NT // 2) as it:
                for j in range(2):
                    t = 2 * it + j
                    g = group(t)
                    pe.wait_ge(S["cnt_oh"], t + 1)
                    pe.matmul(ps[:, 6, ds(g * 64, R0 + R1)], oh_d[:, j, :], oh_r[:, j, :], start=False, stop=True,
                              skip_group_check=True).then_inc(S["cnt_pe"], 1)
            pe.wait_ge(S["k_inv"], 1)
            pe.wait_ge(S["hT_lo"], KT)

            def w_end():
                for t in (NT - 2, NT - 1):
                    gains(t, t % 2)
            phase(Q_C1, R0, 20, R0 // 2, ST_C1, w_side, lambda it, st, o: msg(it, st, o, 0), None, 0, w_end)
            tail(1, 1)
            pe.wait_ge(S["acc_out"], 2)
            transpose(1)
            pe.wait_ge(S["hT_lo"], 2 * KT)
            phase(Q_C2, R0, 20, R0 // 2, ST_C2, c_side(0), lambda it, st, o: msg(it, st, o, 2), 2, 3)
            tail(3, 4)
            pe.wait_ge(S["ln_h"], 2 * NG)
            transpose(2)
            pe.wait_ge(S["hT_lo"], 3 * KT)
            phase(Q_L1, R1, 12, NT // 12, ST_L1, c_side(1), lambda it, st, o: msg(it, st, o, 4), 5, 6)
            tail(5, 7)
            pe.wait_ge(S["acc_out"], 8)
            for s in range(NG):
                if s >= 2:
                    pe.wait_ge(S["ct_cp"], s - 1)
                b = 4 + 2 * (s % 2)
                for g in range(NG):
                    ins = pe.transpose(psf[:, 512 * b + P * g:512 * b + P * (g + 1)], C[:, g, P * s:P * (s + 1)], ident[:])
                ins.then_inc(S["ct_tp"], 1)
            transpose(3)
            pe.wait_ge(S["hT_lo"], 4 * KT)
            for k in range(2):
                for g in range(NG):
                    step(0, Q_GCN + k, g)
            pe.wait_ge(S["gcn_y"], NG)
            pe.wait_ge(S["ct_cp"], NG)
            for i in range(2 * NG):
                j, cols = i // 2, slice((i % 2) * HALF, (i % 2 + 1) * HALF)
                if i >= 2:
                    pe.wait_ge(S["gcn_ev"], i - 1)
                acc = ps[:, 2 + i % 2, 0:HALF]
                for s in range(NG):
                    pe.matmul(acc, CT[:, s, P * j:P * (j + 1)], R[:, s, cols], start=(s == 0), stop=False)
                pe.matmul(acc, ident[:], R[:, j, cols], start=False, stop=True).then_inc(S["gcn_mm"], 1)
            pe.wait_ge(S["ln_h"], 3 * NG)
            transpose(4)
            pe.wait_ge(S["hT_lo"], 5 * KT)
            for k in range(2):
                for g in range(NG):
                    step(0, Q_G1 + k, g)

            def rows(n):
                H, s = HEADS[n][0], A[n]
                for k in range(3):
                    pe.wait_ge(s["al_ok"], k + 1)
                    if k == 2:
                        pe.wait_ge(s["al_cp"], 1)
                    for g in range(NG):
                        o = 1024 * (k % 2) + P * g
                        ins = pe.transpose(psf[0:H, o:o + P], al[:, k, g, 0:H], ident[:])
                    ins.then_inc(s["al_tp"], 1)

            def tiles_(n):
                H, c = HEADS[n]
                s = A[n]
                for m, v in (("o_mm", 2), ("o_ev", 2)):
                    pe.sem_inc(s[m], v)

                def one(it, j, t):
                    k = 5 * (2 * it + j) + t
                    b = (5 * j + t) % 2
                    if t == 0:
                        pe.wait_ge(s["o_ev"], 2 * it + j + 1)
                        pe.matmul(ps[:, 6 + j, :], z16[:, 0:P], z16[:], start=True, stop=True)
                    pe.wait_ge(s["p_ok"], k + 3)
                    for g in range(NG):
                        ins = pe.matmul(ps[:, 6 + j, (c + 1) * g:(c + 1) * (g + 1)], pt[:, b, P * g:P * (g + 1)],
                                        R[:, t, ds((2 * it + j) * (c + 1), c + 1)], start=False, stop=True, skip_group_check=True)
                    ins.then_inc(s["o_mm"], 1)
                with pe.Fori(0, H // 2) as it:
                    for j in range(2):
                        for t in range(NG):
                            one(it, j, t)

            for n in range(3):
                pe.sem_inc(A[n]["p_ok"], 2)
            rows(0)
            tiles_(0)
            pe.wait_ge(S["elu_v"], 1)
            transpose(5)
            pe.wait_ge(S["hT_lo"], 6 * KT)
            for k in range(2):
                for g in range(NG):
                    step(0, Q_G2 + k, g)
            rows(1)
            pe.wait_ge(A[1]["p_ok"], NG + 2)
            for g in range(NG):
                b = 4 + 2 * (g % 2)
                if g >= 2:
                    pe.wait_ge(A[1]["o_ev"], g - 1)
                for k, (c0, c1) in enumerate(((0, HALF), (HALF, D + 1))):
                    for t in range(NG):
                        ins = pe.matmul(ps[:, b + k, 0:c1 - c0], h[:, t, P * g:P * (g + 1)], R[:, t, c0:c1],
                                        start=(t == 0), stop=(t == NG - 1))
                ins.then_inc(A[1]["o_mm"], 1)
            pe.wait_ge(S["ln_h"], 4 * NG)
            transpose(6)
            pe.wait_ge(S["hT_lo"], 7 * KT)
            pe.wait_ge(S["bd_ok"], 1)
            for i in range(2 * NG):
                g, k = i // 2, i % 2
                if i >= 4:
                    pe.wait_ge(S["ft_ev"], i - 3)
                for kt in range(KT):
                    o = 1024 * (i % 4) + P * kt
                    rows_ = slice(P * g, P * (g + 1))
                    for m, (l, r) in enumerate(((hT_hi, bd_hi), (hT_hi, bd_lo), (hT_lo, bd_hi))):
                        ins = pe.matmul(psf[:, o:o + P], l[:, kt, rows_], r[:, k, :], start=(m == 0), stop=(m == 2))
                ins.then_inc(S["ft_mm"], 1)
            rows(2)
            tiles_(2)


def kernel(**inputs):
    import numpy as _np
    import concourse.bacc as _bacc
    from concourse import mybir as _mybir
    from concourse.bass_utils import run_bass_kernel_spmd as _run

    nc = _bacc.Bacc("TRN2", target_bir_lowering=False, num_devices=1)
    arrays, aps = {}, {}
    for name, value in inputs.items():
        arr = _np.ascontiguousarray(value)
        arrays[f"in_{name}"] = arr
        aps[name] = nc.dram_tensor(f"in_{name}", arr.shape, _mybir.dt.from_np(arr.dtype), kind="ExternalInput").ap()
    out = nc.dram_tensor("out_x", (N, D), _mybir.dt.float32, kind="ExternalOutput").ap()
    gnn_kernel(nc, aps, out)
    r = _run(nc, [arrays], core_ids=[0])
    return r.results[0]["out_x"]
```

```python
from contextlib import ExitStack

import concourse.bass as bass
from concourse import mybir

ALU = mybir.AluOpType
ACT = mybir.ActivationFunctionType
AX = mybir.AxisListType
F32 = mybir.dt.float32
F32R = mybir.dt.float32r
F16 = mybir.dt.float16
I32 = mybir.dt.int32

P = 128
N, D, E = 625, 768, 10000
NG = -(-N // P)
NP = NG * P
LAST = N - (NG - 1) * P
KT = D // P
HALF = D // 2
EP, EC = 125, 80
NT = 84
R0, R1 = 8, 34
H2, C2 = 8, 96
H3, C3 = 12, 64
NEG = -1.0e30
GB = 6
MB = 3
GU = 2 * GB
CW = NP // 2
EPS = 1e-5
ds = bass.ds


def gnn_kernel(nc, a, out):
    ctx = ExitStack()
    with ctx:
        def sb(name, shape, dt=F32):
            return ctx.enter_context(nc.sbuf_tensor(name, shape, dt))

        def sem(name):
            return ctx.enter_context(nc.semaphore(name))

        x = sb("x", [P, NG, D])
        h = sb("h", [P, NG, D])
        hT_hi = sb("hT_hi", [P, KT, NP], F32R)
        hT_lo = sb("hT_lo", [P, KT, NP], F32R)
        w_hi = sb("w_hi", [P, 2, KT, HALF], F32R)
        w_lo = sb("w_lo", [P, 2, KT, HALF], F32R)
        R = sb("R", [P, NG, 780])
        arena = sb("arena", [P, 9600])
        raw = arena[:, 0:4608].rearrange("p (b k n) -> p b k n", b=2, k=KT)
        ust = arena[:, 4608:6528].rearrange("p (g n) -> p g n", g=NG)
        gat = arena[:, 6528:6528 + GB * HALF].rearrange("p (b n) -> p b n", b=GB)
        rowS = arena[:, 0:1280].rearrange("p (b n) -> p b n", b=2)
        rowM = arena[:, 1280:2560].rearrange("p (b n) -> p b n", b=2)
        zt = arena[:, 2560:5760].rearrange("p (b n) -> p b n", b=NG)
        pt = arena[:, 5760:7040].rearrange("p (b n) -> p b n", b=2)
        alT = arena[0:H3, 7680:9600].rearrange("p (k n) -> p k n", k=3)
        msg_hi = sb("msg_hi", [P, MB, HALF], F32R)
        msg_lo = sb("msg_lo", [P, MB, HALF], F32R)
        onehot = sb("onehot", [P, MB, P], F32R)
        counts = sb("counts", [P, 2, NG, NP])
        C = counts[:, 0]
        CT = counts[:, 1]
        rad = counts[:].rearrange("p a g n -> p (a g n)").bitcast(F16)
        RC = 10
        oh_lo = rad[:, 0:2 * RC * P].rearrange("p (b c n) -> p b c n", b=2, c=RC)
        oh_hi = rad[:, 2560:2560 + RC * NT].rearrange("p (c n) -> p c n", c=RC)
        val_hi = rad[:, 3400:3400 + 2 * RC * 4 * NT].rearrange("p (b c v n) -> p b c v n", b=2, c=RC, v=4)
        vec = sb("vec", [P, 2, D])
        oh_all = rad[:, 0:NT * P].rearrange("p (t n) -> p t n", t=NT)
        kgat = counts[:].rearrange("p a g n -> p (a g n)")[:, NT * P // 2:NT * P // 2 + GU * (R0 + R1)].rearrange(
            "p (b n) -> p b n", b=GU)
        oh_r = gat.rearrange("p b n -> p (b n)").bitcast(F16)[:, 0:NT * (R0 + R1)].rearrange("p (t n) -> p t n", t=NT)
        at = [0]

        def edge(shape, dt=F32):
            n = 1
            for d in shape[1:]:
                n *= d
            t = R[:].rearrange("p g n -> p (g n)")[0:shape[0], at[0]:at[0] + n]
            at[0] += n
            if dt != F32:
                t = t.bitcast(dt)
            if len(shape) == 3:
                t = t.rearrange("p (a b) -> p a b", a=shape[1])
            return t
        e_i = edge([EP, 4, EC], I32)
        e_f = edge([EP, 4, EC])
        ge = edge([EP, NG + 1, EC])
        grp1 = edge([EP, NG, EC])
        pre = edge([EP, NG, EC])
        zer = edge([EP, EC])
        rs = edge([EP, NG])
        off = edge([EP, NG])
        pos = edge([EP, EC])
        pos_i = edge([EP, EC], I32)
        hi_i = edge([EP, EC], I32)
        hi_f = edge([EP, EC])
        lo_f = edge([EP, EC])
        vals = edge([EP, EC, 4])
        tot = edge([P, NG])
        ntl = edge([P, NG, EC])
        tiles = edge([P, NG])
        tb = edge([P, NG])
        tbi = edge([P, NG])
        tab = sb("tab", [P, 4, NT])
        gt = sb("gt", [P, 4, NT])
        grp_f = sb("grp_f", [P, NT])
        grp_p = sb("grp_p", [P, NT // GB, GB])
        grp = sb("grp", [P, NT // GB], I32)
        ix_f = sb("ix_f", [P, 3, NT])
        ix = sb("ix", [P, 3, NT], I32)
        ixb = sb("ixb", [P, GU], I32)
        wgt = sb("wgt", [P, 2, NT])
        oh_d = sb("oh_d", [P, 2, P], F16)
        oh_s = sb("oh_s", [P, 2, CW], F16)
        kinv = sb("kinv", [P, NG, 64])
        ident = sb("ident", [P, P])
        ones = sb("ones", [P, P])
        below = sb("below", [EP, EP])
        iota = sb("iota", [P, P + 2])
        iota16 = sb("iota16", [P, NP + 1], F16)
        iota128 = sb("iota128", [P, EC])
        z16 = sb("z16", [P, 512], F16)
        bst = sb("bst", [P, NG, 2, 6])
        mv = sb("mv", [P, NG, 2])
        var = sb("var", [P, NG])
        std = sb("std", [P, NG])
        rstd = sb("rstd", [P, NG])
        deg = sb("deg", [P, NG])
        dinv = sb("dinv", [P, NG])
        al = sb("al", [P, 4, NG, H3])
        mxt = sb("mxt", [P, 2, NG])
        mz = sb("mz", [P, NG, H3])
        rz = sb("rz", [P, 2, NG])
        bd = arena[:, 8832:9088].rearrange("p (k n) -> p k n", k=2)
        bd_hi = sb("bd_hi", [P, 2, P], F32R)
        bd_lo = sb("bd_lo", [P, 2, P], F32R)
        w64 = arena[0:64, 9088:9344].rearrange("p (k n) -> p k n", k=2)
        ps = ctx.enter_context(nc.psum_tensor("ps", [P, 8, 512], F32))
        psf = ps[:].rearrange("p b n -> p (b n)")
        U = [nc.dram_tensor(f"U{i}", [R1 * NP, HALF], F32, kind="Internal").ap() for i in range(2)]
        kinv_d = nc.dram_tensor("kinv_d", [NP, R0 + R1], F32, kind="Internal").ap()
        rows_d = nc.dram_tensor("rows_d", [3, 3, H3, NP], F32, kind="Internal").ap()

        S = {n: sem(n) for n in (
            "x_in edges_in dve_nop w64_in consts vec_ok ln_var ln_std ln_h hT_tp hT_hi hT_lo "
            "w_hi w_lo steps evac pool_idx pool_nop msg_hi msg_lo agg_pe acc_out "
            "srt_rs srt_ps srt_rhs srt_mm srt_tab cnt_oh cnt_pe k_inv kinv_st w_pr w_done "
            "c_oh c_pe ct_tp ct_cp deg_ok deg_sq gcn_y gcn_mm gcn_ev x_ok ln_c ln_cc ct_ln "
            "elu_v elu_m elu_e bd_z bd_tp bd_ok ft_mm ft_ev chain out_st").split()}
        w_in = [sem("w_in0"), sem("w_in1")]
        v_in = [sem("v_in0"), sem("v_in1")]
        u_st = [sem(f"u_st{g}") for g in range(NG)]
        k_in = [sem("k_in0"), sem("k_in1")]
        g_in = [sem(f"g_in{b}") for b in range(GB)]
        A = [{m: sem(f"{m}_{n}") for m in "al_ok al_tp al_cp al_st rs0 rs1 rm0 rm1 seg q_ok z_ok l_ok d_ok p_ok o_mm o_r o_ev".split()}
             for n in range(3)]
        ADD_DVE = (0, 1, 3)
        HEADS = ((H2, C2), (1, D), (H3, C3))

        Q_C1, Q_C2 = 0, 2 * (R0 + 1)
        Q_L1 = 2 * Q_C2
        Q_GCN = Q_L1 + 2 * (R1 + 1)
        Q_G1, Q_G2 = Q_GCN + 2, Q_GCN + 4
        Q_END = Q_G2 + 2
        Q_SPLIT = {Q_GCN: Q_G1 + 1, Q_G1: Q_G2, Q_G2: Q_END}
        ST_C1, ST_C2, ST_L1 = 0, 2 * R0, 4 * R0

        block = ctx.enter_context(nc.Block())

        LEAD = 2

        def sides_at(stride, i):
            return list(range(stride * i // 10, stride * (i + 1) // 10))

        def sides_last(first, g):
            return list(range(first + (NT - first) * g // NG, first + (NT - first) * (g + 1) // NG))

        @block.sync
        def _(sp):
            sp.dma_start(x[:, 0:NG - 1, :], a["x"][0:(NG - 1) * P, :].rearrange("(g p) d -> p g d", p=P)).then_inc(S["x_in"], 16)
            sp.wait_ge(S["consts"], 1)
            sp.dma_start(x[0:LAST, NG - 1, :], a["x"][(NG - 1) * P:N, :]).then_inc(S["x_in"], 16)
            for k, name in enumerate(("src", "dst", "edge_type_8", "edge_type_34")):
                sp.dma_start(e_i[:, k, :], a[name].rearrange("(p c) -> p c", c=EC)).then_inc(S["edges_in"], 16)
            for k, name in enumerate(("L3_gnn_W", "L3_gnn_W_res")):
                for i in range(2):
                    sp.dma_start(w64[:, k, 64 * i:64 * i + 64], a[name]).then_inc(S["w64_in"], 16)

            def load(it, o, src):
                sp.wait_ge(S["w_lo"], o + 2 * it + 1)
                sp.dma_start(raw[:, o % 2], src).then_inc(w_in[o % 2], 16)

            def halves(w, hf):
                return w[:, hf * HALF:(hf + 1) * HALF].rearrange("(k p) n -> p k n", p=P)

            def rel(w, r, hf):
                return w[ds(r, 1), :, hf * HALF:(hf + 1) * HALF].rearrange("r (k p) n -> p (r k) n", p=P)

            def store(it, o, r, hf):
                for g in range(NG):
                    sp.wait_ge(S["evac"], 5 * (o + 2 * it) + g + 3)
                    sp.dma_start(U[hf][ds(r * NP + g * P, P), :], ust[:, g, :]).then_inc(u_st[g], 16)

            def phase(Wr, root, q0, nr, after):
                for hf in range(2):
                    o = q0 + hf * (nr + 1)

                    def pair(it):
                        for j in range(2):
                            load(it, o + 2 + j, rel(Wr, 2 * it + j + 2, hf))
                            store(it, o + j, 2 * it + j, hf)
                    lo = 0
                    if o == Q_C1:
                        with sp.Fori(0, 2) as it:
                            pair(it)
                        sp.wait_ge(S["k_inv"], 1)
                        sp.dma_start(kinv_d.rearrange("(g p) r -> p g r", p=P), kinv[:, :, 0:R0 + R1]).then_inc(S["kinv_st"], 16)
                        lo = 2
                    with sp.Fori(lo, nr // 2 - 1) as it:
                        pair(it)
                    load(0, o + nr, halves(root, hf))
                    store(0, o + nr - 2, nr - 2, hf)
                    if hf == 0:
                        load(0, o + nr + 1, rel(Wr, 0, 1))
                        store(0, o + nr - 1, nr - 1, hf)
                        load(0, o + nr + 2, rel(Wr, 1, 1))
                    else:
                        after(0)
                        store(0, o + nr - 1, nr - 1, hf)
                        after(1)

            def vector(name, v):
                if v >= 2:
                    sp.wait_ge(S["vec_ok"], v - 1)
                src = a[name]
                if len(src.shape) == 2:
                    src = src.rearrange("h c -> (h c)")
                elif len(src.shape) == 3:
                    src = src.rearrange("o h c -> (o h c)")
                sp.dma_start(vec[:, v % 2, :], src.partition_broadcast(P)).then_inc(v_in[v % 2], 16)

            load(0, 0, rel(a["L0_gnn_W1"], 0, 0))
            load(0, 1, rel(a["L0_gnn_W1"], 1, 0))
            vector("L0_gnn_b1", 0)
            phase(a["L0_gnn_W1"], a["L0_gnn_root1"], Q_C1, R0,
                  lambda k: load(0, Q_C2 + k, rel(a["L0_gnn_W2"], k, 0)))
            vector("L0_gnn_b2", 1)
            phase(a["L0_gnn_W2"], a["L0_gnn_root2"], Q_C2, R0,
                  lambda k: load(0, Q_L1 + k, rel(a["L1_gnn_W_rel"], k, 0)))
            vector("L1_gnn_b_rgcn", 2)
            phase(a["L1_gnn_W_rel"], a["L1_gnn_W_root"], Q_L1, R1,
                  lambda k: load(0, Q_GCN + k, halves(a["L1_gnn_W_gcn"], k)))
            vector("L1_gnn_b_gcn", 3)
            for k in range(2):
                load(0, Q_G1 + k, halves(a["L2_gnn_W1"], k))


            def spread(n, j, k, hd, buf, done):
                src = rows_d[n, k, ds(hd, 1), :].rearrange("o n -> (o n)").partition_broadcast(P)
                sp.dma_start(buf[:, j, :], src).then_inc(done, 16)

            def attention(n, v, bias):
                H, s = HEADS[n][0], A[n]
                sp.wait_ge(s["al_cp"], 1)
                sp.dma_start(rows_d[n, 0, 0:H, :], alT[0:H, 0, :]).then_inc(s["al_st"], 16)
                sp.wait_ge(s["al_st"], 16)

                def maxima(it, j):
                    sp.wait_ge(s["seg"], 2 * it + j + 1)
                    spread(n, j, 0, 2 * it + j, rowS, s[f"rs{j}"])

                def tiles_(it, j):
                    sp.wait_ge(s["z_ok"], 5 * (2 * it + j) + 5)
                    spread(n, j, 1, 2 * it + j, rowS, s[f"rs{j}"])
                    sp.wait_ge(s["l_ok"], 5 * (2 * it + j) + 5)
                    spread(n, j, 2, 2 * it + j, rowM, s[f"rm{j}"])
                if H == 1:
                    maxima(0, 0)
                else:
                    with sp.Fori(0, H // 2) as it:
                        for j in range(2):
                            maxima(it, j)
                for k in (1, 2):
                    sp.wait_ge(s["al_cp"], k + 1)
                    sp.dma_start(rows_d[n, k, 0:H, :], alT[0:H, k, :]).then_inc(s["al_st"], 16)
                sp.wait_ge(s["al_st"], 48)
                sp.wait_ge(s["seg"], H + 2)
                if bias is not None:
                    vector(bias, v)
                if H == 1:
                    tiles_(0, 0)
                else:
                    with sp.Fori(0, H // 2) as it:
                        for j in range(2):
                            tiles_(it, j)

            vector("L2_gnn_a_src1", 4)
            vector("L2_gnn_a_dst1", 5)
            attention(0, 6, "L2_gnn_b1")
            sp.wait_ge(S["elu_v"], 1)
            for k in range(2):
                load(0, Q_G2 + k, halves(a["L2_gnn_W2"], k))
            vector("L2_gnn_a_src2", 7)
            vector("L2_gnn_a_dst2", 8)
            attention(1, 9, "L2_gnn_b2")
            vector("L3_gnn_attn_l", 10)
            vector("L3_gnn_attn_r", 11)
            attention(2, None, None)
            sp.wait_ge(S["x_ok"], 1)
            sp.dma_start(out[0:(NG - 1) * P, :].rearrange("(g p) d -> p g d", p=P), x[:, 0:NG - 1, :]).then_inc(S["out_st"], 16)
            sp.dma_start(out[(NG - 1) * P:N, :], x[0:LAST, NG - 1, :]).then_inc(S["out_st"], 16)
            sp.wait_ge(S["out_st"], 32)

        @block.gpsimd
        def _(pool):
            pool.memset(x[:, NG - 1, :], 0.0).then_inc(S["consts"], 1)
            pool.memset(ident[:], 0.0).then_inc(S["consts"], 1)
            pool.memset(below[:], 1.0).then_inc(S["consts"], 1)
            pool.memset(bd[:], 0.0).then_inc(S["bd_z"], 1)
            pool.wait_ge(S["consts"], 3)
            pool.affine_select(out=ident[:], in_=ident[:], compare_op=ALU.not_equal, fill=1.0, base=0,
                               pattern=[[-1, P]], channel_multiplier=1).then_inc(S["consts"], 1)
            pool.affine_select(out=below[:], in_=below[:], compare_op=ALU.is_gt, fill=0.0, base=0,
                               pattern=[[1, EP]], channel_multiplier=-1).then_inc(S["consts"], 1)
            pool.memset(ones[:], 1.0).then_inc(S["consts"], 1)
            pool.memset(z16[:], 0.0).then_inc(S["consts"], 1)
            pool.memset(zer[:], 0.0).then_inc(S["consts"], 1)
            pool.iota(iota[:], [[1, P + 2]], base=0, channel_multiplier=0, allow_small_or_imprecise_dtypes=True).then_inc(S["consts"], 1)
            pool.iota(iota16[:], [[1, NP + 1]], base=0, channel_multiplier=0, allow_small_or_imprecise_dtypes=True).then_inc(S["consts"], 1)
            pool.iota(iota128[:], [[P, EC]], base=0, channel_multiplier=0, allow_small_or_imprecise_dtypes=True).then_inc(S["consts"], 1)

            def indices(table, it, j, k):
                pool.tensor_copy(ixb[:, j:j + GB], ix[:, table, ds(GU * it + j, GB)]).then_inc(S["pool_idx"], 1)
                pool.wait_ge(S["pool_idx"], NT // GB * k + 2 * it + j // GB + 1)
                pool.sem_inc(S["pool_nop"], 1)

            def gather(it, j, phase):
                t = j + GU * it
                b = j % GB
                table, hf = [0, 0, 0, 0, 1, 1][phase], phase % 2
                pool.wait_ge(S["msg_lo"], NT * phase + t + 1)
                if b == 0:
                    indices(table, it, j, phase + 1)
                else:
                    pool.sem_inc(S["pool_nop"], 1)
                pool.indirect_dma_start(out=gat[:, b, :], out_offset=None, in_=U[hf][0:NP * (R0 if phase < 4 else R1), :],
                                        in_offset=bass.IndirectOffsetOnAxis(ap=ixb[:, j:j + 1], axis=0)).then_inc(g_in[b], 16)

            def gathers(phase, stored):
                for g in range(NG):
                    pool.wait_ge(u_st[g], 16 * stored)
                with pool.Fori(0, NT // GU) as it:
                    for j in range(GU):
                        gather(it, j, phase)

            pool.wait_ge(S["srt_tab"], 1)
            pool.wait_ge(S["kinv_st"], 16)
            with pool.Fori(0, NT // GU) as it:
                for j in range(GU):
                    if j % GB == 0:
                        pool.wait_ge(S["w_done"], 2 * it + j // GB + 1)
                        indices(2, it, j, 0)
                    pool.indirect_dma_start(out=kgat[:, j, :], out_offset=None, in_=kinv_d,
                                            in_offset=bass.IndirectOffsetOnAxis(ap=ixb[:, j:j + 1], axis=0)).then_inc(k_in[j // GB], 16)
            pool.wait_ge(S["w_done"], NT // GB + 2)
            gathers(0, ST_C1 + R0)
            gathers(1, ST_C1 + 2 * R0)
            gathers(2, ST_C2 + R0)
            gathers(3, ST_C2 + 2 * R0)
            gathers(4, ST_L1 + R1)
            gathers(5, ST_L1 + 2 * R1)

            def q_tiles(n):
                H, s = HEADS[n][0], A[n]

                def one(it, j, t):
                    if t in ADD_DVE:
                        return
                    pool.wait_ge(s["l_ok"], 5 * (2 * it + j) + t + 11)
                    pool.tensor_tensor(zt[:, t, :], zt[:, t, :], CT[:, t, :], ALU.add).then_inc(s["q_ok"], 1)
                if H == 1:
                    for t in range(NG):
                        one(0, 0, t)
                else:
                    with pool.Fori(0, H // 2) as it:
                        for j in range(2):
                            for t in range(NG):
                                one(it, j, t)
            pool.wait_ge(S["ct_ln"], 1)
            for n in range(3):
                q_tiles(n)

        @block.scalar
        def _(act):
            cp, rl = ACT.Copy, ACT.Relu

            def split(it, o):
                act.wait_ge(w_in[o % 2], 16 * (it + o // 2 + 1))
                act.wait_ge(S["steps"], 5 * (o + 2 * it) + 5)
                act.activation(w_hi[:, o % 2], raw[:, o % 2], cp).then_inc(S["w_hi"], 1)

            def evac(it, o, g, dst, stored):
                s = 5 * (o + 2 * it) + g
                act.wait_ge(S["steps"], s + 11)
                if stored is not None:
                    act.wait_ge(u_st[g], stored)
                act.activation(dst, ps[:, (o + g) % 2, 0:HALF] if len(dst.shape) == 2 else
                               ps[:, (o + g) % 2, 0:HALF].rearrange("p (h c) -> p h c", h=dst.shape[1]), cp).then_inc(S["evac"], 1)

            def ln(i):
                act.wait_ge(S["ln_var"], i + 1)
                act.activation(std[:], var[:], ACT.Sqrt).then_inc(S["ln_std"], 1)

            def transpose(k, fn):
                for kt in range(KT):
                    act.wait_ge(S["hT_tp"], KT * k + kt + 1)
                    b = 2 * (kt % 2)
                    act.activation(hT_hi[:, kt, :], psf[:, 512 * b:512 * b + NP], fn).then_inc(S["hT_hi"], 1)

            def msg(it, stride, o, phase):
                t = o + stride * it
                act.wait_ge(g_in[o % GB], 16 * (NT // GB * phase + (stride // GB) * it + o // GB + 1))
                act.wait_ge(S["agg_pe"], NT * phase + t + 1)
                act.activation(msg_hi[:, o % MB, :], gat[:, o % GB, :], cp,
                               scale=wgt[:, [0, 0, 0, 0, 1, 1][phase], ds(t, 1)]).then_inc(S["msg_hi"], 1)

            def phase(q0, nr, stride, n_it, st0, side0, side1):
                for hf, side in ((0, side0), (1, side1)):
                    o = q0 + hf * (nr + 1)
                    st = st0 + hf * nr

                    def ahead(it, t):
                        if side and not (isinstance(it, int) and stride * it + t + LEAD >= NT):
                            side(it, stride, t + LEAD)

                    def pair(it, sides, first=False):
                        for j in range(2):
                            split(it, o + j + 1)
                            for g in range(NG):
                                evac(it, o + j, g, ust[:, g, :], None if first and j == 0 else 16 * (st + 2 * it + j))
                                if sides:
                                    for t in sides_at(stride, 5 * j + g):
                                        ahead(it, t)
                    if side:
                        for t in range(LEAD):
                            side(0, stride, t)
                    lo = 0
                    if st == 0:
                        pair(0, False, True)
                        lo = 1
                    with act.Fori(lo, n_it) as it:
                        pair(it, True)
                    if n_it < nr // 2:
                        pair(n_it, True)
                        with act.Fori(n_it + 1, nr // 2) as it:
                            pair(it, False)
                    if o + nr + 1 < Q_END:
                        split(0, o + nr + 1)
                    for g in range(NG):
                        evac(0, o + nr, g, R[:, g, hf * HALF:(hf + 1) * HALF], None)
                        if n_it == nr // 2:
                            for t in sides_last(stride * n_it, g):
                                ahead(0, t)
                    if st == 0:
                        act.wait_ge(S["w_done"], NT // GB + 2)

            def tail(ph):
                with act.Fori(0, NT // GU) as it:
                    for o in range(GU):
                        msg(it, GU, o, ph)

            act.wait_ge(S["consts"], 11)
            act.sem_inc(S["evac"], 2)
            ln(0)
            split(0, 0)
            transpose(0, rl)
            phase(Q_C1, R0, 18, R0 // 2, ST_C1, None, lambda it, st, o: msg(it, st, o, 0))
            tail(1)
            transpose(1, rl)
            phase(Q_C2, R0, 18, R0 // 2, ST_C2, None, lambda it, st, o: msg(it, st, o, 2))
            tail(3)
            ln(1)
            transpose(2, rl)
            phase(Q_L1, R1, 6, NT // 6 - 1, ST_L1, None, lambda it, st, o: msg(it, st, o, 4))
            tail(5)
            for s in range(NG):
                act.wait_ge(S["ct_tp"], s + 1)
                b = 4 + 2 * (s % 2)
                act.activation(CT[:, s, :], psf[:, 512 * b:512 * b + NP], cp).then_inc(S["ct_cp"], 1)
            act.wait_ge(S["deg_ok"], 1)
            act.activation(std[:], deg[:], ACT.Sqrt).then_inc(S["deg_sq"], 1)
            transpose(3, cp)

            def dense(q, dst):
                for k in range(2):
                    if q + k + 1 < Q_SPLIT[q]:
                        split(0, q + k + 1)
                    for g in range(NG):
                        evac(0, q + k, g, dst(g, k), None)
            dense(Q_GCN, lambda g, k: R[:, g, k * HALF:(k + 1) * HALF])
            ln(2)
            transpose(4, rl)
            act.wait_ge(S["ln_c"], 1)
            act.activation(CT, CT, ACT.Ln).then_inc(S["ln_cc"], 1)
            dense(Q_G1, lambda g, k: R[:, g, 0:H2 * (C2 + 1)].rearrange("p (h c) -> p h c", c=C2 + 1)[:, 4 * k:4 * k + 4, 0:C2])

            def rows(n):
                H, s = HEADS[n][0], A[n]
                for k in range(3):
                    act.wait_ge(s["al_tp"], k + 1)
                    act.activation(alT[0:H, k, :], psf[0:H, 1024 * (k % 2):1024 * (k % 2) + NP], cp).then_inc(s["al_cp"], 1)

            def tiles_(n, out_tile):
                H, s = HEADS[n][0], A[n]
                act.sem_inc(s["z_ok"], 10)

                def z(it, i):
                    j, t = i // NG, i % NG
                    if t == 0:
                        act.wait_ge(s[f"rs{j % 2}"], 16 * (it + j // 2) + 16 * (max(1, H // 2) + 1))
                    act.wait_ge(s["p_ok"], 10 * it + i + 6)
                    act.activation(zt[:, t, :], rowS[:, j % 2, :], ACT.Identity,
                                   bias=al[:, 0, t, ds(2 * it + j, 1)]).then_inc(s["z_ok"], 1)

                def e(it, i):
                    j, t = i // NG, i % NG
                    by_dve = [u for u in range(NG) if u in ADD_DVE]
                    by_pool = [u for u in range(NG) if u not in ADD_DVE]
                    if t in ADD_DVE:
                        act.wait_ge(s["d_ok"], len(by_dve) * (2 * it + j) + by_dve.index(t) + 1)
                    else:
                        act.wait_ge(s["q_ok"], len(by_pool) * (2 * it + j) + by_pool.index(t) + 1)
                    if H > 1:
                        act.wait_ge(s["o_mm"], 10 * it + i + 1)
                    act.activation(out_tile(i % 2, i % NG), zt[:, i % NG, :], ACT.Exp).then_inc(s["p_ok"], 1)

                def heads(it, n, last):
                    for i in range(n):
                        if not (last and i + 3 >= n):
                            z(it, i + 3)
                        e(it, i)
                for i in range(3):
                    z(0, i)
                if H == 1:
                    heads(0, NG, True)
                else:
                    with act.Fori(0, H // 2 - 1) as it:
                        heads(it, 2 * NG, False)
                    heads(H // 2 - 1, 2 * NG, True)

            rows(0)
            tiles_(0, lambda b, t: pt[:, b, :])
            act.wait_ge(S["elu_m"], 1)
            act.activation(R[:, :, 0:D], R[:, :, 0:D], ACT.Exp).then_inc(S["elu_e"], 1)
            split(0, Q_G2)
            transpose(5, cp)
            dense(Q_G2, lambda g, k: R[:, g, k * HALF:(k + 1) * HALF])
            rows(1)
            tiles_(1, lambda b, t: h[:, t, 0:NP])
            ln(3)
            transpose(6, rl)
            for i in range(2 * NG):
                g = i // 2
                act.wait_ge(S["ft_mm"], i + 1)
                src = psf[:, 1024 * (i % 4):1024 * (i % 4) + D]
                if i % 2 == 0:
                    act.activation(R[:, g, :].rearrange("p (h c) -> p h c", c=C3 + 1)[:, :, 0:C3],
                                   src.rearrange("p (h c) -> p h c", c=C3), cp).then_inc(S["ft_ev"], 1)
                else:
                    act.activation(h[:, g, :], src, cp).then_inc(S["ft_ev"], 1)
            rows(2)
            tiles_(2, lambda b, t: pt[:, b, :])

        @block.vector
        def _(dve):
            n_chain = [0]

            def link(ins):
                n_chain[0] += 1
                ins.then_inc(S["chain"], 1)
                dve.wait_ge(S["chain"], n_chain[0])

            def ln(i):
                for g in range(NG):
                    for k in range(2):
                        ins = dve.bn_stats(bst[:, g, k, :], x[:, g, k * HALF:(k + 1) * HALF])
                link(ins)
                for g in range(NG):
                    ins = dve.bn_aggr(mv[:, g, :], bst[:, g, :, :])
                link(ins)
                dve.tensor_scalar(var[:], mv[:, :, 1], EPS, None, ALU.add).then_inc(S["ln_var"], 1)
                dve.wait_ge(S["ln_std"], i + 1)
                link(dve.reciprocal(rstd[:], std[:]))
                for g in range(NG):
                    dve.tensor_scalar(h[:, g, :], x[:, g, :], mv[:, g, 0:1], rstd[:, g:g + 1],
                                      ALU.subtract, ALU.mult).then_inc(S["ln_h"], 1)

            def transpose(k, relu):
                for kt in range(KT):
                    dve.wait_ge(S["hT_hi"], KT * k + kt + 1)
                    b = 2 * (kt % 2)
                    src, hi = psf[:, 512 * b:512 * b + NP], hT_hi[:, kt, :].bitcast(F32)
                    if relu:
                        dve.scalar_tensor_tensor(hT_lo[:, kt, :], src, 0.0, hi, ALU.max, ALU.subtract).then_inc(S["hT_lo"], 1)
                    else:
                        dve.tensor_tensor(hT_lo[:, kt, :], src, hi, ALU.subtract).then_inc(S["hT_lo"], 1)

            def split(it, o):
                dve.wait_ge(S["w_hi"], o + 2 * it + 1)
                dve.tensor_tensor(w_lo[:, o % 2], raw[:, o % 2], w_hi[:, o % 2].bitcast(F32), ALU.subtract).then_inc(S["w_lo"], 1)

            def sort():
                dve.wait_ge(S["edges_in"], 64)
                link(dve.tensor_copy(e_f[:], e_i[:]))
                for j in range(NG + 1):
                    ins = dve.tensor_scalar(ge[:, j, :], e_f[:, 1, :], float(P * j), None, ALU.is_ge)
                link(ins)
                link(dve.tensor_tensor(grp1[:], ge[:, 0:NG, :], ge[:, 1:NG + 1, :], ALU.subtract))
                for g in range(NG):
                    ins = dve.tensor_tensor_scan(pre[:, g, :], grp1[:, g, :], zer[:], 0.0, ALU.add, ALU.add)
                link(ins)
                dve.tensor_copy(rs[:], pre[:, :, EC - 1]).then_inc(S["srt_rs"], 1)
                dve.tensor_scalar(vals[:, :, 0], e_f[:, 0, :], 1.0, None, ALU.add)
                dve.tensor_copy(vals[:, :, 2], e_f[:, 2, :])
                dve.tensor_copy(vals[:, :, 3], e_f[:, 3, :])
                link(dve.tensor_reduce(hi_f[:], ge[:, 1:NG, :].rearrange("p g c -> p c g"), AX.X, ALU.add))
                link(dve.scalar_tensor_tensor(lo_f[:], hi_f[:], -float(P), e_f[:, 1, :], ALU.mult, ALU.add))
                link(dve.tensor_scalar(vals[:, :, 1], lo_f[:], 1.0, None, ALU.add))
                dve.wait_ge(S["srt_ps"], 1)
                link(dve.tensor_copy(tot[:], ps[:, 6, 0:NG]))
                for g in range(NG):
                    ins = dve.tensor_scalar(ntl[:, g, :], iota128[:], tot[:, g:g + 1], None, ALU.is_lt)
                link(ins)
                link(dve.tensor_reduce(tiles[:], ntl[:], AX.X, ALU.add))
                link(dve.tensor_tensor_scan(tbi[:], tiles[:], z16[:, 0:NG], 0.0, ALU.add, ALU.add))
                link(dve.tensor_tensor(tb[:], tbi[:], tiles[:], ALU.subtract))
                link(dve.scalar_tensor_tensor(off[:], tb[0:EP, :], float(P), ps[0:EP, 7, 0:NG], ALU.mult, ALU.add))
                for g in range(NG):
                    ins = dve.scalar_tensor_tensor(pre[:, g, :], pre[:, g, :], off[:, g:g + 1], grp1[:, g, :], ALU.add, ALU.mult)
                link(ins)
                link(dve.tensor_reduce(pos[:], pre[:].rearrange("p g c -> p c g"), AX.X, ALU.add))
                link(dve.tensor_scalar(pos_i[:], pos[:], -1.0, None, ALU.add))
                link(dve.tensor_single_scalar(hi_i[:], pos_i[:], 7, ALU.arith_shift_right))
                link(dve.tensor_copy(hi_f[:], hi_i[:]))
                link(dve.scalar_tensor_tensor(lo_f[:], hi_f[:], -float(P), pos[:], ALU.mult, ALU.add))
                for s in range(EC // RC):
                    b, c0 = s % 2, s * RC
                    if s >= 1:
                        dve.wait_ge(S["srt_rhs"], s)
                    if s >= 2:
                        dve.wait_ge(S["srt_mm"], s - 1)
                    dve.tensor_tensor(oh_lo[0:EP, b], lo_f[:, c0:c0 + RC].unsqueeze(2).to_broadcast([EP, RC, P]),
                                      iota[0:EP, 1:P + 1].unsqueeze(1).to_broadcast([EP, RC, P]), ALU.is_equal)
                    link(dve.tensor_tensor(oh_hi[0:EP], hi_f[:, c0:c0 + RC].unsqueeze(2).to_broadcast([EP, RC, NT]),
                                           iota[0:EP, 0:NT].unsqueeze(1).to_broadcast([EP, RC, NT]), ALU.is_equal))
                    dve.tensor_tensor(val_hi[0:EP, b], oh_hi[0:EP].unsqueeze(2).to_broadcast([EP, RC, 4, NT]),
                                      vals[:, c0:c0 + RC, :].unsqueeze(3).to_broadcast([EP, RC, 4, NT]), ALU.mult).then_inc(S["srt_rhs"], 1)
                dve.wait_ge(S["srt_mm"], EC // RC)
                link(dve.tensor_copy(tab[:].rearrange("p v t -> p (v t)"), ps[:, 5, 0:4 * NT]))
                for k in range(NG - 1):
                    dve.tensor_scalar(gt[:, k, :], iota[:, 0:NT], tb[:, k + 1:k + 2], None, ALU.is_ge)
                for k in range(2):
                    ins = dve.scalar_tensor_tensor(ix_f[:, k, :], tab[:, 2 + k, :], float(NP), tab[:, 0, :], ALU.mult, ALU.add)
                link(ins)
                link(dve.tensor_reduce(grp_f[:], gt[:].rearrange("p k t -> p t k"), AX.X, ALU.add))
                link(dve.scalar_tensor_tensor(ix_f[:, 2, :], grp_f[:], float(P), tab[:, 1, :], ALU.mult, ALU.add))
                dve.tensor_scalar(ix[:], ix_f[:], -1.0, 0.0, ALU.add, ALU.max)
                for k in range(GB):
                    ins = dve.tensor_scalar(grp_p[:, :, k], grp_f[:].rearrange("p (t k) -> p t k", k=GB)[:, :, k], float(8 ** k), None, ALU.mult)
                link(ins)
                link(dve.tensor_reduce(grp_f[:, 0:NT // GB], grp_p[:], AX.X, ALU.add))
                dve.tensor_copy(grp[:], grp_f[:, 0:NT // GB]).then_inc(S["srt_tab"], 1)

            def one_hot_dst(b, t):
                return dve.tensor_scalar(oh_d[:, b, :], iota16[:, 1:P + 1], tab[:, 1, ds(t, 1)], None, ALU.is_equal)

            def one_hots():
                dve.tensor_tensor(oh_all, iota[:, 1:P + 1].unsqueeze(1).to_broadcast([P, NT, P]),
                                  tab[:, 1, :].unsqueeze(2).to_broadcast([P, NT, P]), ALU.is_equal)
                for k, n, o in ((2, R0, 0), (3, R1, R0)):
                    ins = dve.tensor_tensor(oh_r[:, :, o:o + n], iota[:, 0:n].unsqueeze(1).to_broadcast([P, NT, n]),
                                            tab[:, k, :].unsqueeze(2).to_broadcast([P, NT, n]), ALU.is_equal)
                ins.then_inc(S["cnt_oh"], 1)

            def counted():
                dve.wait_ge(S["cnt_pe"], 1)
                link(dve.tensor_scalar(kinv[:].rearrange("p g n -> p (g n)"), ps[:, 6, 0:64 * NG], 1.0, None, ALU.max))
                dve.reciprocal(kinv[:], kinv[:]).then_inc(S["k_inv"], 1)

            def weigh(it, j):
                kg = kgat[:, GB * j:GB * (j + 1), :]
                t = ds(GU * it + GB * j, GB)
                dve.wait_ge(k_in[j], 16 * GB * it + 16 * GB)
                dve.tensor_tensor(kg, kg, oh_r[:, t, :], ALU.mult).then_inc(S["w_pr"], 1)
                dve.wait_ge(S["w_pr"], 2 * it + j + 1)
                dve.tensor_reduce(wgt[:, 0, t], kg[:, :, 0:R0], AX.X, ALU.add)
                dve.tensor_reduce(wgt[:, 1, t], kg[:, :, R0:R0 + R1], AX.X, ALU.add).then_inc(S["w_done"], 1)

            def weigh_end():
                with dve.Fori(R0 - 4, NT // GU) as it:
                    for j in range(2):
                        weigh(it, j)

            def c_side(part):
                def side(it, stride, o):
                    t = o + stride * it
                    dve.wait_ge(S["c_pe"], NT * part + t + 1)
                    one_hot_dst(o % 2, t)
                    dve.tensor_scalar(oh_s[:, o % 2, :], iota16[:, 1 + CW * part:1 + CW * (part + 1)], tab[:, 0, ds(t, 1)],
                                      None, ALU.is_equal).then_inc(S["c_oh"], 1)
                return side

            def msg(it, stride, o, ph):
                t = o + stride * it
                b = o % MB
                dve.wait_ge(S["agg_pe"], NT * ph + t + 1)
                dve.tensor_scalar(onehot[:, b, :], iota[:, 1:P + 1], tab[:, 1, ds(t, 1)], None, ALU.is_equal)
                dve.wait_ge(S["msg_hi"], NT * ph + t + 1)
                dve.scalar_tensor_tensor(msg_lo[:, b, :], gat[:, o % GB, :], wgt[:, [0, 0, 0, 0, 1, 1][ph], ds(t, 1)],
                                         msg_hi[:, b, :].bitcast(F32), ALU.mult, ALU.subtract).then_inc(S["msg_lo"], 1)

            def phase(q0, nr, stride, n_it, st0, side0, side1, v, after0, after1):
                for hf, side in ((0, side0), (1, side1)):
                    o = q0 + hf * (nr + 1)

                    def ahead(it, t):
                        if side and not (isinstance(it, int) and stride * it + t + LEAD >= NT):
                            side(it, stride, t + LEAD)

                    def pair(it, sides):
                        for j in range(2):
                            split(it, o + j + 1)
                            if sides:
                                for g in range(NG):
                                    for t in sides_at(stride, 5 * j + g):
                                        ahead(it, t)
                    if side:
                        for t in range(LEAD):
                            side(0, stride, t)
                    lo = 0
                    if st0 + hf == 0:
                        split(0, o + 1)
                        sort()
                        split(0, o + 2)
                        split(0, o + 3)
                        one_hots()
                        split(0, o + 4)
                        counted()
                        lo = 2

                        def pair(it, sides):
                            for j in range(2):
                                split(it, o + j + 1)
                                for k in range(2):
                                    weigh(2 * it - 4 + j, k)
                    with dve.Fori(lo, n_it) as it:
                        pair(it, True)
                    if n_it < nr // 2:
                        pair(n_it, True)
                        with dve.Fori(n_it + 1, nr // 2) as it:
                            pair(it, False)
                    split(0, o + nr + 1)
                    if n_it == nr // 2:
                        for g in range(NG):
                            for t in sides_last(stride * n_it, g):
                                ahead(0, t)
                    dve.wait_ge(S["evac"], 5 * (o + nr + 1) + 2)
                    dve.wait_ge(v_in[v % 2], 16 * (v // 2 + 1))
                    rh = R[:, :, hf * HALF:(hf + 1) * HALF]
                    ins = dve.tensor_tensor(rh, rh, vec[:, v % 2, hf * HALF:(hf + 1) * HALF].unsqueeze(1).to_broadcast([P, NG, HALF]), ALU.add)
                    if hf == 1:
                        ins.then_inc(S["vec_ok"], 1)
                    (after0 if hf == 0 else after1)()

            def counts_out(part):
                dve.wait_ge(S["c_pe"], NT * (part + 1) + 2)
                dve.tensor_copy(C[:, :, CW * part:CW * (part + 1)], ps[:, 2:2 + NG, 0:CW]).then_inc(S["acc_out"], 1)

            def sums_out(ph, into_x):
                hf = ph % 2
                cols = slice(hf * HALF, (hf + 1) * HALF)
                dve.wait_ge(S["agg_pe"], NT * (ph + 1) + MB)
                if into_x:
                    link(dve.tensor_tensor(R[:, :, cols], R[:, :, cols], ps[:, 2:2 + NG, 0:HALF], ALU.add))
                    ins = dve.tensor_tensor(x[:, :, cols], x[:, :, cols], R[:, :, cols], ALU.add)
                else:
                    ins = dve.tensor_tensor(h[:, :, cols], R[:, :, cols], ps[:, 2:2 + NG, 0:HALF], ALU.add)
                ins.then_inc(S["acc_out"], 1)

            def tail(ph):
                with dve.Fori(0, NT // GU) as it:
                    for o in range(GU):
                        msg(it, GU, o, ph)

            dve.wait_ge(S["consts"], 11)
            dve.sem_inc(S["w_lo"], 2)
            dve.sem_inc(S["msg_lo"], GB)
            dve.sem_inc(S["w_done"], 2)
            dve.wait_ge(S["x_in"], 32)
            ln(0)
            split(0, 0)
            transpose(0, True)
            dve.wait_ge(S["bd_z"], 1)
            dve.wait_ge(S["bd_tp"], 1)
            for k in range(2):
                for i in range(2):
                    r = slice(64 * i, 64 * i + 64)
                    ins = dve.tensor_copy(bd[r, k, r], ps[r, 4, 64 * k:64 * k + 64])
            link(ins)
            link(dve.tensor_copy(bd_hi[:], bd[:]))
            link(dve.tensor_tensor(bd_lo[:], bd[:], bd_hi[:].bitcast(F32), ALU.subtract))
            dve.sem_inc(S["bd_ok"], 1)
            phase(Q_C1, R0, 18, R0 // 2, ST_C1, None, lambda it, st, o: msg(it, st, o, 0), 0, weigh_end, lambda: sums_out(0, False))
            tail(1)
            sums_out(1, False)
            transpose(1, True)
            phase(Q_C2, R0, 18, R0 // 2, ST_C2, c_side(0), lambda it, st, o: msg(it, st, o, 2), 1, lambda: counts_out(0), lambda: sums_out(2, True))
            tail(3)
            sums_out(3, True)
            dve.wait_ge(S["acc_out"], 5)
            ln(1)
            transpose(2, True)
            phase(Q_L1, R1, 6, NT // 6 - 1, ST_L1, c_side(1), lambda it, st, o: msg(it, st, o, 4), 2, lambda: counts_out(1), lambda: sums_out(4, False))
            tail(5)
            sums_out(5, False)
            link(dve.tensor_reduce(deg[:], C, AX.X, ALU.add))
            link(dve.tensor_scalar(deg[:], deg[:], 1.0, None, ALU.add))
            dve.sem_inc(S["deg_ok"], 1)
            dve.wait_ge(S["ct_tp"], NG)
            dve.tensor_scalar(C, C, 0.0, NEG, ALU.is_equal, ALU.mult)
            dve.wait_ge(S["deg_sq"], 1)
            link(dve.reciprocal(dinv[:], std[:]))
            transpose(3, False)
            for k in range(2):
                if Q_GCN + k + 1 < Q_SPLIT[Q_GCN]:
                    split(0, Q_GCN + k + 1)
            dve.wait_ge(v_in[1], 32)
            dve.tensor_tensor(x[:], x[:], vec[:, 1, :].unsqueeze(1).to_broadcast([P, NG, D]), ALU.add).then_inc(S["vec_ok"], 1)
            dve.wait_ge(S["vec_ok"], 4)
            dve.wait_ge(S["evac"], 5 * (Q_GCN + 2) + 2)
            for g in range(NG):
                dve.tensor_scalar(R[:, g, 0:D], R[:, g, 0:D], dinv[:, g:g + 1], None, ALU.mult).then_inc(S["gcn_y"], 1)
            for i in range(2 * NG):
                j, cols = i // 2, slice((i % 2) * HALF, (i % 2 + 1) * HALF)
                dve.wait_ge(S["gcn_mm"], i + 1)
                ins = dve.scalar_tensor_tensor(x[:, j, cols], ps[:, 2 + i % 2, 0:HALF], dinv[:, j:j + 1], x[:, j, cols], ALU.mult, ALU.add)
                ins.then_inc(S["gcn_ev"], 1)
            dve.wait_ge(S["gcn_ev"], 2 * NG)
            ln(2)
            transpose(4, True)
            dve.wait_ge(S["hT_tp"], 5 * KT)
            link(dve.tensor_scalar(h[:, :, 0:NP], CT, 0.0, NEG, ALU.is_equal, ALU.mult))
            dve.tensor_scalar(CT, CT, 1.0, None, ALU.max).then_inc(S["ln_c"], 1)
            split(0, Q_G1 + 1)
            dve.wait_ge(S["ln_cc"], 1)
            dve.tensor_tensor(CT, CT, h[:, :, 0:NP], ALU.add).then_inc(S["ct_ln"], 1)

            def heads_of(n, g):
                H, c = HEADS[n]
                return R[:, g, 0:H * (c + 1)].rearrange("p (h c) -> p h c", c=c + 1) if H > 1 else R[:, g, 0:c].unsqueeze(1)

            def scores(n, v):
                H, c = HEADS[n]
                i = 0
                for k in range(2):
                    dve.wait_ge(v_in[v % 2], 16 * (v // 2 + 1))
                    for g in range(NG):
                        t = arena[:, 2560 + 1280 * (i % 2):2560 + 1280 * (i % 2) + D].rearrange("p (h c) -> p h c", c=c)
                        link(dve.tensor_tensor(t, heads_of(n, g)[:, :, 0:c], vec[:, v % 2, :].rearrange("p (h c) -> p h c", c=c), ALU.mult))
                        link(dve.tensor_reduce(al[:, k, g, 0:H], t, AX.X, ALU.add))
                        i += 1
                    dve.sem_inc(A[n]["al_ok"], 1)
                    dve.sem_inc(S["vec_ok"], 1)
                    v += 1

            def maxima(n):
                H, s = HEADS[n][0], A[n]

                def one(it, j):
                    hd = 2 * it + j
                    dve.wait_ge(s[f"rs{j}"], 16 * it + 16)
                    dve.wait_ge(s["seg"], hd + 2)
                    dve.sem_inc(S["dve_nop"], 1)
                    for g in range(NG):
                        t = arena[:, 2560 + NP * g:2560 + NP * (g + 1)]
                        ins = dve.tensor_tensor_reduce(t, rowS[:, j, :], C[:, g, :], 1.0, -3.0e38, ALU.add, ALU.max, mxt[:, j, g:g + 1])
                    ins.then_inc(s["o_r"], 1)
                    dve.wait_ge(s["o_r"], hd + 1)
                    dve.tensor_copy(mz[:, :, ds(hd, 1)], mxt[:, j, :].unsqueeze(2)).then_inc(s["seg"], 1)
                if H == 1:
                    one(0, 0)
                else:
                    with dve.Fori(0, H // 2) as it:
                        for j in range(2):
                            one(it, j)
                dve.wait_ge(s["seg"], H + 2)
                link(dve.tensor_tensor(mz[:, :, 0:H], mz[:, :, 0:H], al[:, 1, :, 0:H], ALU.add))
                link(dve.scalar_tensor_tensor(mz[:, :, 0:H], mz[:, :, 0:H], 0.2, mz[:, :, 0:H], ALU.mult, ALU.max))
                link(dve.scalar_tensor_tensor(al[:, 2, :, 0:H], al[:, 1, :, 0:H], 0.2, mz[:, :, 0:H], ALU.mult, ALU.subtract))
                dve.tensor_tensor(al[:, 1, :, 0:H], al[:, 1, :, 0:H], mz[:, :, 0:H], ALU.subtract).then_inc(s["al_ok"], 1)
                link(dve.tensor_scalar(al[:, 3, :, 0:H], al[:, 0, :, 0:H], 0.2, None, ALU.mult))

            def leaky(n, it, i):
                s = A[n]
                k = 10 * it + i
                j, t = i // NG, i % NG
                if t == 0:
                    dve.wait_ge(s[f"rm{j}"], 16 * it + 16)
                dve.wait_ge(s["z_ok"], k + 11)
                dve.sem_inc(S["dve_nop"], 1)
                dve.scalar_tensor_tensor(zt[:, t, :], rowM[:, j, :], al[:, 3, t, ds(2 * it + j, 1)], zt[:, t, :],
                                         ALU.add, ALU.max).then_inc(s["l_ok"], 1)
                if t - 1 in ADD_DVE:
                    dve.wait_ge(s["l_ok"], k + 10)
                    u = zt[:, t - 1, :]
                    dve.tensor_tensor(u, u, CT[:, t - 1, :], ALU.add).then_inc(s["d_ok"], 1)

            def head_out(n, it, j, put, steps):
                H, c = HEADS[n]
                s = A[n]
                hd = 2 * it + j
                base = H + steps * hd
                o = ps[:, 6 + j, 0:NG * (c + 1)].rearrange("p (g c) -> p g c", c=c + 1)
                dve.wait_ge(s["o_mm"], 5 * hd + 7)
                dve.tensor_scalar(rz[:, j, :].unsqueeze(2), o[:, :, c:c + 1], 1e-16, None, ALU.add if n == 0 else ALU.max).then_inc(s["o_r"], 1)
                dve.wait_ge(s["o_r"], base + 1)
                dve.reciprocal(rz[:, j, :], rz[:, j, :]).then_inc(s["o_r"], 1)
                dve.wait_ge(s["o_r"], base + 2)
                put(hd, o[:, :, 0:c], rz[:, j, :].unsqueeze(2).to_broadcast([P, NG, c]), s, base)

            def all_heads(n, put, steps):
                H = HEADS[n][0]

                def pair(it, first):
                    for i in range(2 * NG):
                        leaky(n, it, i)
                        if i == 3 and not first:
                            head_out(n, it - 1, 1, put, steps)
                        if i == NG + 3:
                            head_out(n, it, 0, put, steps)
                pair(0, True)
                with dve.Fori(1, H // 2) as it:
                    pair(it, False)
                head_out(n, H // 2 - 1, 1, put, steps)

            for n in range(3):
                for m, c in (("seg", 2), ("l_ok", 10)):
                    dve.sem_inc(A[n][m], c)

            dve.memset(R[:, :, 0:H2 * (C2 + 1)].rearrange("p g (h c) -> p g h c", c=C2 + 1)[:, :, :, C2:C2 + 1], 1.0).then_inc(S["bd_ok"], 1)
            dve.wait_ge(S["evac"], 5 * Q_G2 + 2)
            scores(0, 4)
            maxima(0)
            all_heads(0, lambda hd, o, r, s, base: dve.tensor_tensor(h[:, :, ds(hd * C2, C2)], o, r, ALU.mult).then_inc(s["o_ev"], 1), 2)
            dve.wait_ge(A[0]["o_ev"], H2 + 2)
            dve.wait_ge(v_in[0], 64)
            link(dve.tensor_tensor(h[:], h[:], vec[:, 0, :].unsqueeze(1).to_broadcast([P, NG, D]), ALU.add))
            dve.sem_inc(S["vec_ok"], 1)
            dve.tensor_scalar(R[:, :, 0:D], h[:], 0.0, None, ALU.min).then_inc(S["elu_m"], 1)
            dve.wait_ge(S["elu_m"], 1)
            link(dve.tensor_scalar(h[:], h[:], 0.0, None, ALU.max))
            dve.wait_ge(S["elu_e"], 1)
            dve.scalar_tensor_tensor(h[:], R[:, :, 0:D], -1.0, h[:], ALU.add, ALU.add).then_inc(S["elu_v"], 1)
            dve.wait_ge(S["elu_v"], 1)
            dve.memset(R[:, :, D:D + 1], 1.0).then_inc(S["bd_ok"], 1)
            split(0, Q_G2)
            transpose(5, False)
            split(0, Q_G2 + 1)
            dve.wait_ge(S["evac"], 5 * Q_END + 2)
            scores(1, 7)
            maxima(1)
            for t in range(NG):
                leaky(1, 0, t)
            dve.wait_ge(v_in[1], 80)
            link(dve.tensor_tensor(x[:], x[:], vec[:, 1, :].unsqueeze(1).to_broadcast([P, NG, D]), ALU.add))
            dve.sem_inc(S["vec_ok"], 1)
            for g in range(NG):
                b = 4 + 2 * (g % 2)
                dve.wait_ge(A[1]["o_mm"], g + 1)
                link(dve.tensor_scalar(rz[:, 0, g:g + 1], ps[:, b + 1, HALF:HALF + 1], 1e-16, None, ALU.add))
                link(dve.reciprocal(rz[:, 0, g:g + 1], rz[:, 0, g:g + 1]))
                for k in range(2):
                    cols = slice(k * HALF, (k + 1) * HALF)
                    ins = dve.scalar_tensor_tensor(x[:, g, cols], ps[:, b + k, 0:HALF], rz[:, 0, g:g + 1], x[:, g, cols], ALU.mult, ALU.add)
                ins.then_inc(A[1]["o_ev"], 1)
            dve.wait_ge(A[1]["o_ev"], NG)
            dve.memset(R[:, :, :].rearrange("p g (h c) -> p g h c", c=C3 + 1)[:, :, :, C3:C3 + 1], 1.0).then_inc(S["bd_ok"], 1)
            ln(3)
            transpose(6, True)
            dve.wait_ge(S["ft_ev"], 2 * NG)
            scores(2, 10)
            maxima(2)

            def residual(hd, o, r, s, base):
                t = kinv[:]
                cols = ds(hd * C3, C3)
                dve.tensor_tensor(t, o, r, ALU.mult).then_inc(s["o_r"], 1)
                dve.wait_ge(s["o_r"], base + 3)
                dve.tensor_tensor(t, t, h[:, :, cols], ALU.add).then_inc(s["o_r"], 1)
                dve.wait_ge(s["o_r"], base + 4)
                dve.scalar_tensor_tensor(x[:, :, cols], t, 0.0, x[:, :, cols], ALU.max, ALU.add).then_inc(s["o_ev"], 1)
                dve.wait_ge(s["o_ev"], hd + 3)
            all_heads(2, residual, 4)
            dve.sem_inc(S["x_ok"], 1)

        @block.tensor
        def _(pe):
            def transpose(k):
                for kt in range(KT):
                    b = 2 * (kt % 2)
                    if kt >= 2:
                        pe.wait_ge(S["hT_lo"], KT * k + kt - 1)
                    for g in range(NG):
                        ins = pe.transpose(psf[:, 512 * b + P * g:512 * b + P * (g + 1)], h[:, g, P * kt:P * (kt + 1)], ident[:])
                    ins.then_inc(S["hT_tp"], 1)

            def step(it, o, g):
                s = 5 * (o + 2 * it) + g
                if g == 0:
                    pe.wait_ge(S["w_lo"], o + 2 * it + 3)
                pe.wait_ge(S["evac"], s + 1)
                acc = ps[:, (o + g) % 2, 0:HALF]
                n = 0
                for kt in range(KT):
                    hi, lo = hT_hi[:, kt, P * g:P * (g + 1)], hT_lo[:, kt, P * g:P * (g + 1)]
                    for l, r in ((hi, w_hi), (hi, w_lo), (lo, w_hi)):
                        ins = pe.matmul(acc, l, r[:, o % 2, kt, :], start=(n == 0), stop=(n == 3 * KT - 1))
                        n += 1
                ins.then_inc(S["steps"], 1)

            packed = [None]

            def group(it, stride, o):
                if o % GB == 0:
                    packed[0] = pe.value_load(grp[0:1, ds(stride // GB * it + o // GB, 1)], min_val=0, max_val=8 ** GB - 1)
                return ((packed[0] >> (3 * (o % GB))) & 7).with_bounds(min_val=0, max_val=NG - 1)

            def bank(g, n):
                return ps[:, ds(g + 2, 1), 0:n].rearrange("p a n -> p (a n)")

            def clear(i):
                if i:
                    pe.wait_ge(S["acc_out"], i)
                else:
                    pe.wait_ge(S["k_inv"], 1)
                for g in range(NG):
                    pe.matmul(ps[:, 2 + g, :], z16[:, 0:P], z16[:], start=True, stop=True)

            def c_side(part):
                def side(it, stride, o):
                    t = o + stride * it
                    g = group(it, stride, o)
                    pe.wait_ge(S["c_oh"], NT * part + t + 1)
                    pe.matmul(bank(g, CW), oh_d[:, o % 2, :], oh_s[:, o % 2, :], start=False, stop=True, skip_group_check=True).then_inc(S["c_pe"], 1)
                return side

            def msg(it, stride, o, ph):
                t = o + stride * it
                b = o % MB
                g = group(it, stride, o)
                pe.wait_ge(S["msg_lo"], NT * ph + t + 1 + GB)
                pe.matmul(bank(g, HALF), onehot[:, b, :], msg_hi[:, b, :], start=False, stop=False, skip_group_check=True)
                pe.matmul(bank(g, HALF), onehot[:, b, :], msg_lo[:, b, :], start=False, stop=True, skip_group_check=True).then_inc(S["agg_pe"], 1)

            def sort():
                for s in range(EC // RC):
                    pe.wait_ge(S["srt_rhs"], s + 1)
                    for c in range(RC):
                        ins = pe.matmul(ps[:, 5, 0:4 * NT], oh_lo[0:EP, s % 2, c, :], val_hi[0:EP, s % 2, c].rearrange("p v n -> p (v n)"),
                                        start=(s + c == 0), stop=(s * RC + c == EC - 1))
                    ins.then_inc(S["srt_mm"], 1)

            def count():
                pe.wait_ge(S["srt_tab"], 1)
                pe.wait_ge(S["cnt_oh"], 1)
                pe.matmul(ps[:, 6, :], z16[:, 0:P], z16[:], start=True, stop=True)
                with pe.Fori(0, NT // GU) as it:
                    for j in range(GU):
                        t = GU * it + j
                        g = group(it, GU, j)
                        pe.matmul(ps[:, 6, ds(g * 64, R0 + R1)], oh_all[:, ds(t, 1), :].rearrange("p t n -> p (t n)"),
                                  oh_r[:, ds(t, 1), :].rearrange("p t n -> p (t n)"), start=False, stop=True, skip_group_check=True)
                pe.matmul(ps[:, 7, :], z16[:, 0:P], z16[:], start=True, stop=True).then_inc(S["cnt_pe"], 1)

            def phase(q0, nr, stride, n_it, st0, side0, side1, clear0, clear1):
                for hf, side in ((0, side0), (1, side1)):
                    o = q0 + hf * (nr + 1)
                    i = (clear0, clear1)[hf]
                    if i is not None:
                        clear(i)

                    def pair(it, sides):
                        for j in range(2):
                            for g in range(NG):
                                step(it, o + j, g)
                                if sides and side:
                                    for t in sides_at(stride, 5 * j + g):
                                        side(it, stride, t)
                    lo = 0
                    if st0 + hf == 0:
                        pair(0, False)
                        sort()
                        pair(1, False)
                        count()
                        lo = 2
                    with pe.Fori(lo, n_it) as it:
                        pair(it, True)
                    if n_it < nr // 2:
                        pair(n_it, True)
                        with pe.Fori(n_it + 1, nr // 2) as it:
                            pair(it, False)
                    for g in range(NG):
                        step(0, o + nr, g)
                        if n_it == nr // 2 and side:
                            for t in sides_last(stride * n_it, g):
                                side(0, stride, t)

            def tail(ph, i):
                clear(i)
                with pe.Fori(0, NT // GU) as it:
                    for o in range(GU):
                        msg(it, GU, o, ph)

            pe.sem_inc(S["steps"], 10)
            pe.sem_inc(S["c_pe"], 2)
            pe.sem_inc(S["agg_pe"], MB)
            pe.wait_ge(S["consts"], 11)
            pe.wait_ge(S["ln_h"], NG)
            transpose(0)
            pe.wait_ge(S["w64_in"], 64)
            for k in range(2):
                ins = pe.transpose(ps[:, 4, 64 * k:64 * k + 64], w64[:, k, :], ident[0:64, 0:64])
            ins.then_inc(S["bd_tp"], 1)
            pe.wait_ge(S["srt_rs"], 1)
            pe.matmul(ps[0:EP, 7, 0:NG], below[:], rs[:], start=True, stop=True)
            pe.matmul(ps[:, 6, 0:NG], ones[0:EP, :], rs[:], start=True, stop=True).then_inc(S["srt_ps"], 1)
            pe.wait_ge(S["hT_lo"], KT)
            phase(Q_C1, R0, 18, R0 // 2, ST_C1, None, lambda it, st, o: msg(it, st, o, 0), None, 0)
            tail(1, 1)
            pe.wait_ge(S["acc_out"], 2)
            transpose(1)
            pe.wait_ge(S["hT_lo"], 2 * KT)
            phase(Q_C2, R0, 18, R0 // 2, ST_C2, c_side(0), lambda it, st, o: msg(it, st, o, 2), 2, 3)
            tail(3, 4)
            pe.wait_ge(S["ln_h"], 2 * NG)
            transpose(2)
            pe.wait_ge(S["hT_lo"], 3 * KT)
            phase(Q_L1, R1, 6, NT // 6 - 1, ST_L1, c_side(1), lambda it, st, o: msg(it, st, o, 4), 5, 6)
            tail(5, 7)
            pe.wait_ge(S["acc_out"], 8)
            for s in range(NG):
                if s >= 2:
                    pe.wait_ge(S["ct_cp"], s - 1)
                b = 4 + 2 * (s % 2)
                for g in range(NG):
                    ins = pe.transpose(psf[:, 512 * b + P * g:512 * b + P * (g + 1)], C[:, g, P * s:P * (s + 1)], ident[:])
                ins.then_inc(S["ct_tp"], 1)
            transpose(3)
            pe.wait_ge(S["hT_lo"], 4 * KT)
            for k in range(2):
                for g in range(NG):
                    step(0, Q_GCN + k, g)
            pe.wait_ge(S["gcn_y"], NG)
            pe.wait_ge(S["ct_cp"], NG)
            for i in range(2 * NG):
                j, cols = i // 2, slice((i % 2) * HALF, (i % 2 + 1) * HALF)
                if i >= 2:
                    pe.wait_ge(S["gcn_ev"], i - 1)
                acc = ps[:, 2 + i % 2, 0:HALF]
                for s in range(NG):
                    pe.matmul(acc, CT[:, s, P * j:P * (j + 1)], R[:, s, cols], start=(s == 0), stop=False)
                pe.matmul(acc, ident[:], R[:, j, cols], start=False, stop=True).then_inc(S["gcn_mm"], 1)
            pe.wait_ge(S["ln_h"], 3 * NG)
            transpose(4)
            pe.wait_ge(S["hT_lo"], 5 * KT)
            for k in range(2):
                for g in range(NG):
                    step(0, Q_G1 + k, g)

            def rows(n):
                H, s = HEADS[n][0], A[n]
                for k in range(3):
                    pe.wait_ge(s["al_ok"], 1 if k == 0 else 3)
                    if k == 2:
                        pe.wait_ge(s["al_cp"], 1)
                    for g in range(NG):
                        o = 1024 * (k % 2) + P * g
                        ins = pe.transpose(psf[0:H, o:o + P], al[:, k, g, 0:H], ident[:])
                    ins.then_inc(s["al_tp"], 1)

            def tiles_(n):
                H, c = HEADS[n]
                s = A[n]
                for m, v in (("o_mm", 2), ("o_ev", 2)):
                    pe.sem_inc(s[m], v)

                def one(it, j, t):
                    k = 5 * (2 * it + j) + t
                    b = (5 * j + t) % 2
                    if t == 0:
                        pe.wait_ge(s["o_ev"], 2 * it + j + 1)
                        pe.matmul(ps[:, 6 + j, :], z16[:, 0:P], z16[:], start=True, stop=True)
                    pe.wait_ge(s["p_ok"], k + 11)
                    for g in range(NG):
                        ins = pe.matmul(ps[:, 6 + j, (c + 1) * g:(c + 1) * (g + 1)], pt[:, b, P * g:P * (g + 1)],
                                        R[:, t, ds((2 * it + j) * (c + 1), c + 1)], start=False, stop=True, skip_group_check=True)
                    ins.then_inc(s["o_mm"], 1)
                with pe.Fori(0, H // 2) as it:
                    for j in range(2):
                        for t in range(NG):
                            one(it, j, t)

            for n in range(3):
                pe.sem_inc(A[n]["p_ok"], 10)
            rows(0)
            tiles_(0)
            pe.wait_ge(S["elu_v"], 1)
            transpose(5)
            pe.wait_ge(S["hT_lo"], 6 * KT)
            for k in range(2):
                for g in range(NG):
                    step(0, Q_G2 + k, g)
            rows(1)
            pe.wait_ge(A[1]["p_ok"], NG + 10)
            for g in range(NG):
                b = 4 + 2 * (g % 2)
                if g >= 2:
                    pe.wait_ge(A[1]["o_ev"], g - 1)
                for k, (c0, c1) in enumerate(((0, HALF), (HALF, D + 1))):
                    for t in range(NG):
                        ins = pe.matmul(ps[:, b + k, 0:c1 - c0], h[:, t, P * g:P * (g + 1)], R[:, t, c0:c1],
                                        start=(t == 0), stop=(t == NG - 1))
                ins.then_inc(A[1]["o_mm"], 1)
            pe.wait_ge(S["ln_h"], 4 * NG)
            transpose(6)
            pe.wait_ge(S["hT_lo"], 7 * KT)
            pe.wait_ge(S["bd_ok"], 1)
            for i in range(2 * NG):
                g, k = i // 2, i % 2
                if i >= 4:
                    pe.wait_ge(S["ft_ev"], i - 3)
                for kt in range(KT):
                    o = 1024 * (i % 4) + P * kt
                    rows_ = slice(P * g, P * (g + 1))
                    for m, (l, r) in enumerate(((hT_hi, bd_hi), (hT_hi, bd_lo), (hT_lo, bd_hi))):
                        ins = pe.matmul(psf[:, o:o + P], l[:, kt, rows_], r[:, k, :], start=(m == 0), stop=(m == 2))
                ins.then_inc(S["ft_mm"], 1)
            rows(2)
            tiles_(2)


def kernel(**inputs):
    import numpy as _np
    import concourse.bacc as _bacc
    from concourse import mybir as _mybir
    from concourse.bass_utils import run_bass_kernel_spmd as _run

    nc = _bacc.Bacc("TRN2", target_bir_lowering=False, num_devices=1)
    arrays, aps = {}, {}
    for name, value in inputs.items():
        arr = _np.ascontiguousarray(value)
        arrays[f"in_{name}"] = arr
        aps[name] = nc.dram_tensor(f"in_{name}", arr.shape, _mybir.dt.from_np(arr.dtype), kind="ExternalInput").ap()
    out = nc.dram_tensor("out_x", (N, D), _mybir.dt.float32, kind="ExternalOutput").ap()
    gnn_kernel(nc, aps, out)
    r = _run(nc, [arrays], core_ids=[0])
    return r.results[0]["out_x"]
```

```python
from contextlib import ExitStack

import concourse.bass as bass
from concourse import mybir

ALU = mybir.AluOpType
ACT = mybir.ActivationFunctionType
AX = mybir.AxisListType
F32 = mybir.dt.float32
F32R = mybir.dt.float32r
F16 = mybir.dt.float16
I32 = mybir.dt.int32

P = 128
N, D, E = 625, 768, 10000
NG = -(-N // P)
NP = NG * P
LAST = N - (NG - 1) * P
KT = D // P
HALF = D // 2
EP, EC = 125, 80
NT = 84
R0, R1 = 8, 34
H2, C2 = 8, 96
H3, C3 = 12, 64
NEG = -1.0e30
TC = 2
TO = NG - TC
NVB = 8
NV = -(-(E // 171) // NVB) * NVB
GB = 6
MB = 4
GU = 2 * GB
CW = NP // 2
EPS = 1e-5
ds = bass.ds


def gnn_kernel(nc, a, out):
    ctx = ExitStack()
    with ctx:
        def sb(name, shape, dt=F32):
            return ctx.enter_context(nc.sbuf_tensor(name, shape, dt))

        def sem(name):
            return ctx.enter_context(nc.semaphore(name))

        x = sb("x", [P, NG, D])
        h = sb("h", [P, NG, D])
        hT_hi = sb("hT_hi", [P, KT, NP], F32R)
        hT_lo = sb("hT_lo", [P, KT, NP], F32R)
        w_hi = sb("w_hi", [P, 2, KT, HALF], F32R)
        w_lo = sb("w_lo", [P, 2, KT, HALF], F32R)
        R = sb("R", [P, NG, 780])
        arena = sb("arena", [P, 6528 + GB * D])
        raw = arena[:, 0:4608].rearrange("p (b k n) -> p b k n", b=2, k=KT)
        ust = arena[:, 4608:6528].rearrange("p (g n) -> p g n", g=NG)
        gat = arena[:, 6528:6528 + GB * D].rearrange("p (b n) -> p b n", b=GB)
        rowS = arena[:, 0:1280].rearrange("p (b n) -> p b n", b=2)
        rowM = arena[:, 1280:2560].rearrange("p (b n) -> p b n", b=2)
        zt = arena[:, 2560:5760].rearrange("p (b n) -> p b n", b=NG)
        pt = arena[:, 5760:7040].rearrange("p (b n) -> p b n", b=2)
        alT = arena[0:H3, 7680:8320]
        rowZ = arena[:, 8320:9600].rearrange("p (b n) -> p b n", b=2)
        mx_scr = [arena[:, o:o + NP] for o in (7040, 9600, 10240)]
        hrow = arena[0:2 * NG, 10880:10880 + 2 * P].rearrange("p (b n) -> p b n", b=2)
        msg_hi, msg_lo = (t[:].rearrange("p k n -> p (k n)")[:, 0:MB * D].rearrange("p (b n) -> p b n", b=MB)
                          for t in (hT_hi, hT_lo))
        onehot = sb("onehot", [P, MB, P], F32R)
        counts = sb("counts", [P, 2, NG, NP])
        C = counts[:, 0]
        CT = counts[:, 1]
        rad = counts[:].rearrange("p a g n -> p (a g n)").bitcast(F16)
        RC = 10
        oh_lo = rad[:, 0:2 * RC * P].rearrange("p (b c n) -> p b c n", b=2, c=RC)
        oh_hi = rad[:, 2560:2560 + RC * NT].rearrange("p (c n) -> p c n", c=RC)
        val_hi = rad[:, 3400:3400 + 2 * RC * 4 * NT].rearrange("p (b c v n) -> p b c v n", b=2, c=RC, v=4)
        vec = sb("vec", [P, 2, D])
        oh_all = rad[:, 0:NT * P].rearrange("p (t n) -> p t n", t=NT)
        kgat = counts[:].rearrange("p a g n -> p (a g n)")[:, NT * P // 2:NT * P // 2 + GU * (R0 + R1)].rearrange(
            "p (b n) -> p b n", b=GU)
        oh_r = gat.rearrange("p b n -> p (b n)").bitcast(F16)[:, 0:NT * (R0 + R1)].rearrange("p (t n) -> p t n", t=NT)
        ctw = counts[0:R1, 1].rearrange("p g n -> p (g n)")
        has, rank, key, urow = (ctw[:, NP * i:NP * (i + 1)] for i in range(4))
        ov_f = ctw[0:1, NP * 4:NP * 4 + 4 * TO * R1].rearrange("p (a b) -> p a b", a=4)
        ov_cmp = gat[0:1].rearrange("p b n -> p (b n)").bitcast(F16)[:, 0:NV * TO * R1].rearrange("p (a b) -> p a b", a=NV)
        src_rows = h[:, 0:2 * TC, :]
        hc = [[t[:].rearrange("p k n -> p (k n)")[:, KT * TC * P * i:KT * TC * P * (i + 1)].rearrange("p (k n) -> p k n", k=KT)
               for t in (hT_hi, hT_lo)] for i in range(2)]
        hv_hi, hv_lo = (t[:].rearrange("p k n -> p (k n)")[:, 0:KT * P].rearrange("p (k n) -> p k n", k=KT)
                        for t in (hT_hi, hT_lo))
        ohl = gat.rearrange("p b n -> p (b n)").bitcast(F16)
        oh_l = h[:].rearrange("p g d -> p (g d)").bitcast(F16)[:, 0:2 * NG * TC * P].rearrange("p (b t n) -> p b t n", b=2, t=NG)
        oh_v = ohl[:, 0:NG * P].rearrange("p (t n) -> p t n", t=NG)
        at = [0]

        def edge(shape, dt=F32):
            n = 1
            for d in shape[1:]:
                n *= d
            t = R[:].rearrange("p g n -> p (g n)")[0:shape[0], at[0]:at[0] + n]
            at[0] += n
            if dt != F32:
                t = t.bitcast(dt)
            if len(shape) == 3:
                t = t.rearrange("p (a b) -> p a b", a=shape[1])
            return t
        e_i = edge([EP, 4, EC], I32)
        e_f = edge([EP, 4, EC])
        ge = edge([EP, NG + 1, EC])
        grp1 = edge([EP, NG, EC])
        pre = edge([EP, NG, EC])
        zer = edge([EP, EC])
        rs = edge([EP, NG])
        off = edge([EP, NG])
        pos = edge([EP, EC])
        pos_i = edge([EP, EC], I32)
        hi_i = edge([EP, EC], I32)
        hi_f = edge([EP, EC])
        lo_f = edge([EP, EC])
        vals = edge([EP, EC, 4])
        tot = edge([P, NG])
        ntl = edge([P, NG, EC])
        tiles = edge([P, NG])
        tb = edge([P, NG])
        tbi = edge([P, NG])
        ones = edge([P, P])
        below = edge([EP, EP])
        iota128 = edge([P, EC])
        tab = sb("tab", [P, 4, NT])
        gt = sb("gt", [P, 4, NT])
        grp_f = sb("grp_f", [P, NT])
        grp_p = sb("grp_p", [P, NT // GB, GB])
        grp = sb("grp", [P, NT // GB], I32)
        ix_f = sb("ix_f", [P, 3, NT])
        ix = sb("ix", [P, 4, NT], I32)
        ixb = sb("ixb", [P, GU], I32)
        wgt = sb("wgt", [P, 2, NT])
        oh_d = sb("oh_d", [P, 2, P], F16)
        oh_s = sb("oh_s", [P, 2, NP], F16)
        oh_rr = sb("oh_rr", [P, 2, R1], F16)
        keyT = sb("keyT", [P, NG, R1])
        lidx = sb("lidx", [P, TC * R1], I32)
        vidx = sb("vidx", [P, 1], I32)
        lixb = sb("lixb", [P, 2, TC], I32)
        urow_g = sb("urow_g", [P, GU])
        ubase = sb("ubase", [P, 2])
        nid = sb("nid", [P, NG], F16)
        ov = sb("ov", [1, 2, NV + 1], I32)
        kinv = sb("kinv", [P, NG, 64])
        ident = sb("ident", [P, P])
        iota = sb("iota", [P, P + 2])
        iota16 = sb("iota16", [P, NP + 1], F16)
        z16 = sb("z16", [P, 512], F16)
        bst = sb("bst", [P, NG, 2, 6])
        mv = sb("mv", [P, NG, 2])
        var = sb("var", [P, NG])
        std = sb("std", [P, NG])
        rstd = sb("rstd", [P, NG])
        deg = sb("deg", [P, NG])
        dinv = sb("dinv", [P, NG])
        al = sb("al", [P, 3, NG, H3])
        mxt = sb("mxt", [P, 2, NG])
        mz = sb("mz", [P, 2, NG])
        mcol = sb("mcol", [P, 2, 2, NG])
        rz = sb("rz", [P, 2, NG])
        bd = arena[:, 8832:9088].rearrange("p (k n) -> p k n", k=2)
        bd_hi = sb("bd_hi", [P, 2, P], F32R)
        bd_lo = sb("bd_lo", [P, 2, P], F32R)
        w64 = arena[0:64, 9088:9344].rearrange("p (k n) -> p k n", k=2)
        ps = ctx.enter_context(nc.psum_tensor("ps", [P, 8, 512], F32))
        psf = ps[:].rearrange("p b n -> p (b n)")
        U = nc.dram_tensor("U", [R1 * NP, D], F32, kind="Internal").ap()
        UMAIN = R1 * TO * P
        urow_d = nc.dram_tensor("urow_d", [R1 * NP, 1], F32, kind="Internal").ap()
        h_d = nc.dram_tensor("h_d", [NP, D], F32, kind="Internal").ap()
        kinv_d = nc.dram_tensor("kinv_d", [NP, R0 + R1], F32, kind="Internal").ap()
        rows_d = nc.dram_tensor("rows_d", [3, H3, NP], F32, kind="Internal").ap()
        terms_d = nc.dram_tensor("terms_d", [3, H3, 2, NP], F32, kind="Internal").ap()

        S = {n: sem(n) for n in (
            "x_in edges_in dve_nop w64_in consts vec_ok ln_var ln_std ln_h hT_tp hT_hi hT_lo "
            "w_hi w_lo steps evac pool_idx pool_nop msg_hi msg_lo agg_pe acc_out "
            "srt_rs srt_ps srt_rhs srt_mm srt_tab cnt_oh cnt_pe k_inv kinv_st w_pr w_done "
            "key_ok key_tp ov_ok urow_st urow_ok u_zero l_oh l_pe l_ix h_st lix_ok hc_tp hc_hi hc_lo "
            "v_in v_hi v_lo v_mm v_ev "
            "c_oh c_pe ct_tp ct_cp deg_ok deg_sq gcn_y gcn_mm gcn_ev x_ok ln_c ln_cc ct_ln "
            "elu_v elu_m elu_e bd_z bd_tp bd_ok ft_mm ft_ev chain out_st").split()}
        w_in = [sem("w_in0"), sem("w_in1")]
        v_in = [sem("v_in0"), sem("v_in1")]
        u_st = [sem(f"u_st{g}") for g in range(NG)]
        hc_in = [sem("hc_in0"), sem("hc_in1")]
        vw_in = [sem("vw_in0"), sem("vw_in1")]
        v_st = [sem(f"v_st{j}") for j in range(2)]
        k_in = [sem("k_in0"), sem("k_in1")]
        g_in = [sem(f"g_in{b}") for b in range(GB)]
        A = [{m: sem(f"{m}_{n}") for m in ("al_ok row_tp row_cp row_st rs0 rd0 rm0 mx mx_ok q_ok z_ok l_ok d_ok p_ok o_mm o_ev"
                                           + (" rs1 rd1 rm1 o_r" if n != 1 else "")).split()} for n in range(3)]
        ADD_DVE = ((), (1, 3), ())
        FT_BANK = (0, 4, 6)
        HEADS = ((H2, C2), (1, D), (H3, C3))

        Q_C1, Q_C2 = 0, 2 * (R0 + 1)
        Q_L1 = 2 * Q_C2
        Q_GCN = Q_L1 + 2 * (R1 + 1)
        Q_G1, Q_G2 = Q_GCN + 2, Q_GCN + 4
        Q_END = Q_G2 + 2
        Q_REL = Q_L1 + 2
        S_REL = NG * Q_REL
        S_SKIP = 2 * R1 * (NG - TC)
        Q_SPLIT = {Q_GCN: Q_G1 + 1, Q_G1: Q_G2, Q_G2: Q_END}
        ST_C1, ST_C2, ST_L1 = 0, 2 * R0, 4 * R0

        block = ctx.enter_context(nc.Block())

        LEAD = 2

        def sides_at(stride, i, n=10):
            return list(range(stride * i // n, stride * (i + 1) // n))

        def lists_at(k, j=None, i=None):
            if i is None:
                return [r for n in range(5) for r in lists_at(k, None, 5 * j + n)]
            return [R1 // 2 * k + r for r in sides_at(R1 // 2, i)]

        ZR = 288
        ZN = 2 * 2 * (R0 - 1)
        assert ZN * ZR >= UMAIN - R0 * NP

        def each_further(eng, n_ov, steps):
            with eng.Fori(0, NV // NVB) as b:
                with eng.If(b * NVB < n_ov):
                    with eng.Fori(0, NVB) as i:
                        with eng.If(b * NVB + i < n_ov):
                            steps(b * NVB + i)

        def sums(c0, g=None):
            if g is None:
                return ps[:, 0:NG, :] if c0 == 0 else psf[:, 512 * NG:512 * NG + 256 * NG].rearrange("p (g n) -> p g n", g=NG)
            return psf[:, ds(512 * g, 512)] if c0 == 0 else psf[:, ds(512 * NG + 256 * g, 256)]

        @block.sync
        def _(sp):
            sp.dma_start(x[:, 0:NG - 1, :], a["x"][0:(NG - 1) * P, :].rearrange("(g p) d -> p g d", p=P)).then_inc(S["x_in"], 16)
            sp.wait_ge(S["consts"], 1)
            sp.dma_start(x[0:LAST, NG - 1, :], a["x"][(NG - 1) * P:N, :]).then_inc(S["x_in"], 16)
            for k, name in enumerate(("src", "dst", "edge_type_8", "edge_type_34")):
                sp.dma_start(e_i[:, k, :], a[name].rearrange("(p c) -> p c", c=EC)).then_inc(S["edges_in"], 16)
            for k, name in enumerate(("L3_gnn_W", "L3_gnn_W_res")):
                for i in range(2):
                    sp.dma_start(w64[:, k, 64 * i:64 * i + 64], a[name]).then_inc(S["w64_in"], 16)

            def load(it, o, src):
                sp.wait_ge(S["w_lo"], o + 2 * it + 1)
                sp.dma_start(raw[:, o % 2], src).then_inc(w_in[o % 2], 16)

            def halves(w, hf):
                return w[:, hf * HALF:(hf + 1) * HALF].rearrange("(k p) n -> p k n", p=P)

            def rel(w, r, hf):
                return w[ds(r, 1), :, hf * HALF:(hf + 1) * HALF].rearrange("r (k p) n -> p (r k) n", p=P)

            def store(it, o, r, hf):
                for g in range(NG):
                    sp.wait_ge(S["evac"], 5 * (o + 2 * it) + g + 3)
                    sp.dma_start(U[ds(r * NP + g * P, P), hf * HALF:(hf + 1) * HALF], ust[:, g, :]).then_inc(u_st[g], 16)

            def phase(Wr, root, o, nr, after):
                def pair(it):
                    for j in range(2):
                        load(it, o + 2 + j, rel(Wr, it + 1, j))
                        store(it, o + j, it, j)
                        f = 2 * it + j + (0 if o == Q_C1 else ZN // 2)
                        sp.dma_start(U[ds(f * ZR + R0 * NP, ZR), :].rearrange("r (c n) -> (r c) n", n=256).rearrange("(t p) n -> p t n", p=96),
                                     z16[0:96].bitcast(F32).unsqueeze(1).to_broadcast([96, ZR * D // 256 // 96, 256])
                                     ).then_inc(S["u_zero"], 16)
                lo = 0
                if o == Q_C1:
                    with sp.Fori(0, 5) as it:
                        pair(it)
                    sp.wait_ge(S["k_inv"], 1)
                    sp.dma_start(kinv_d.rearrange("(g p) r -> p g r", p=P), kinv[:, :, 0:R0 + R1]).then_inc(S["kinv_st"], 16)
                    lo = 5
                if o == Q_C2:
                    with sp.Fori(0, NT // 18 + 1) as it:
                        pair(it)
                    sp.wait_ge(S["key_ok"], 1)
                    sp.dma_start(urow_d.rearrange("(r n) o -> r (n o)", n=NP), urow).then_inc(S["urow_st"], 16)
                    lo = NT // 18 + 1
                with sp.Fori(lo, nr - 1) as it:
                    pair(it)
                for j in range(2):
                    load(0, o + 2 * nr + j, halves(root, j))
                    store(0, o + 2 * nr - 2 + j, nr - 1, j)
                for j in range(2):
                    after(j)

            def vector(name, v):
                if v >= 2:
                    sp.wait_ge(S["vec_ok"], v - 1)
                src = a[name]
                if len(src.shape) == 2:
                    src = src.rearrange("h c -> (h c)")
                elif len(src.shape) == 3:
                    src = src.rearrange("o h c -> (o h c)")
                sp.dma_start(vec[:, v % 2, :], src.partition_broadcast(P)).then_inc(v_in[v % 2], 16)

            load(0, 0, rel(a["L0_gnn_W1"], 0, 0))
            load(0, 1, rel(a["L0_gnn_W1"], 0, 1))
            vector("L0_gnn_b1", 0)
            phase(a["L0_gnn_W1"], a["L0_gnn_root1"], Q_C1, R0,
                  lambda k: load(0, Q_C2 + k, rel(a["L0_gnn_W2"], 0, k)))
            vector("L0_gnn_b2", 1)
            phase(a["L0_gnn_W2"], a["L0_gnn_root2"], Q_C2, R0,
                  lambda k: load(0, Q_L1 + k, halves(a["L1_gnn_W_root"], k)))
            vector("L1_gnn_b_rgcn", 2)
            sp.wait_ge(S["ln_h"], 2 * NG)
            sp.dma_start(h_d.rearrange("(g p) d -> p g d", p=P), h[:]).then_inc(S["h_st"], 16)
            Wr = a["L1_gnn_W_rel"]
            sp.wait_ge(S["u_zero"], 16 * ZN)

            def store_rel(it, j):
                for g in range(TC):
                    sp.wait_ge(S["evac"], S_REL + 2 * TC * it + TC * j + g + 3)
                    sp.dma_start(U[ds(it * (TC * P) + UMAIN + g * P, P), j * HALF:(j + 1) * HALF],
                                 ust[:, TC * j + g, :]).then_inc(u_st[TC * j + g], 16)
            for j in range(2):
                load(0, Q_REL + j, rel(Wr, 0, j))
            with sp.Fori(0, R1 - 1) as it:
                for j in range(2):
                    load(it, Q_REL + 2 + j, rel(Wr, it + 1, j))
                    store_rel(it, j)
            sp.wait_ge(S["w_lo"], Q_REL + 2 * R1 + 2)
            sp.wait_ge(S["ov_ok"], 1)
            n_ov = sp.value_load(ov[0:1, 0, NV:NV + 1], min_val=0, max_val=NV)

            def further_w(c):
                r = sp.value_load(ov[0:1, 0, ds(c, 1)], min_val=0, max_val=R1 - 1)
                for j in range(2):
                    sp.wait_ge(S["v_lo"], 2 * c + j + 1)
                    sp.dma_start(raw[:, j], rel(Wr, r, j)).then_inc(vw_in[j], 16)
            each_further(sp, n_ov, further_w)
            sp.wait_ge(S["v_lo"], n_ov * 2 + 2)
            for k in range(2):
                load(0, Q_GCN + k, halves(a["L1_gnn_W_gcn"], k))
            vector("L1_gnn_b_gcn", 3)
            for k in range(2):
                load(0, Q_G1 + k, halves(a["L2_gnn_W1"], k))


            def spread(row, j, buf, done):
                sp.dma_start(buf[:, j, :], row.rearrange("o n -> (o n)").partition_broadcast(P)).then_inc(done, 16)

            def attention(n, v, bias):
                H, s = HEADS[n][0], A[n]
                sp.wait_ge(s["row_cp"], 1)
                sp.dma_start(rows_d[n, 0:H, :], alT[0:H, :]).then_inc(s["row_st"], 16)
                sp.wait_ge(s["row_st"], 16)
                for j in range(min(H, 2)):
                    spread(rows_d[n, j:j + 1, :], j, rowS, s[f"rs{j}"])
                if bias is not None:
                    vector(bias, v)

                def head(it, j, more):
                    hd = 2 * it + j
                    sp.wait_ge(s["row_cp"], hd + 2)
                    sp.dma_start(terms_d[n, ds(hd, 1)].rearrange("o k (g p) -> (o k g) p", p=P), hrow[:, j, :]).then_inc(s["row_st"], 16)
                    if more:
                        spread(rows_d[n, ds(hd + 2, 1), :], j, rowS, s[f"rs{j}"])
                    sp.wait_ge(s["row_st"], 16 * hd + 32)
                    sp.wait_ge(s["z_ok"], 5 * hd + 5)
                    spread(terms_d[n, ds(hd, 1), 0, :], j, rowZ, s[f"rd{j}"])
                    sp.wait_ge(s["l_ok"], 5 * hd + 5)
                    spread(terms_d[n, ds(hd, 1), 1, :], j, rowM, s[f"rm{j}"])
                if H == 1:
                    head(0, 0, False)
                else:
                    with sp.Fori(0, H // 2 - 1) as it:
                        for j in range(2):
                            head(it, j, True)
                    for j in range(2):
                        head(H // 2 - 1, j, False)

            vector("L2_gnn_a_src1", 4)
            vector("L2_gnn_a_dst1", 5)
            attention(0, 6, "L2_gnn_b1")
            for k, past in enumerate(("elu_m", "elu_e")):
                sp.wait_ge(S[past], 1)
                load(0, Q_G2 + k, halves(a["L2_gnn_W2"], k))
            vector("L2_gnn_a_src2", 7)
            vector("L2_gnn_a_dst2", 8)
            attention(1, 9, "L2_gnn_b2")
            vector("L3_gnn_attn_l", 10)
            vector("L3_gnn_attn_r", 11)
            attention(2, None, None)
            sp.wait_ge(S["x_ok"], 1)
            sp.dma_start(out[0:(NG - 1) * P, :].rearrange("(g p) d -> p g d", p=P), x[:, 0:NG - 1, :]).then_inc(S["out_st"], 16)
            sp.dma_start(out[(NG - 1) * P:N, :], x[0:LAST, NG - 1, :]).then_inc(S["out_st"], 16)
            sp.wait_ge(S["out_st"], 32)

        @block.gpsimd
        def _(pool):
            pool.memset(x[:, NG - 1, :], 0.0).then_inc(S["consts"], 1)
            pool.memset(ident[:], 0.0).then_inc(S["consts"], 1)
            pool.memset(below[:], 1.0).then_inc(S["consts"], 1)
            pool.memset(bd[:], 0.0).then_inc(S["bd_z"], 1)
            pool.iota(ubase[:, 0:1], [[1, 1]], base=UMAIN - 1, channel_multiplier=TC * P, allow_small_or_imprecise_dtypes=True).then_inc(S["consts"], 1)
            pool.iota(ubase[:, 1:2], [[1, 1]], base=-UMAIN - TC * P, channel_multiplier=(TO - TC) * P,
                      allow_small_or_imprecise_dtypes=True).then_inc(S["consts"], 1)
            pool.iota(nid[:], [[P, NG]], base=0, channel_multiplier=1, allow_small_or_imprecise_dtypes=True).then_inc(S["consts"], 1)
            pool.wait_ge(S["consts"], 6)
            pool.affine_select(out=ident[:], in_=ident[:], compare_op=ALU.not_equal, fill=1.0, base=0,
                               pattern=[[-1, P]], channel_multiplier=1).then_inc(S["consts"], 1)
            pool.affine_select(out=below[:], in_=below[:], compare_op=ALU.is_gt, fill=0.0, base=0,
                               pattern=[[1, EP]], channel_multiplier=-1).then_inc(S["consts"], 1)
            pool.memset(ones[:], 1.0).then_inc(S["consts"], 1)
            pool.memset(z16[:], 0.0).then_inc(S["consts"], 1)
            pool.memset(zer[:], 0.0).then_inc(S["consts"], 1)
            pool.iota(iota[:], [[1, P + 2]], base=0, channel_multiplier=0, allow_small_or_imprecise_dtypes=True).then_inc(S["consts"], 1)
            pool.iota(iota16[:], [[1, NP + 1]], base=0, channel_multiplier=0, allow_small_or_imprecise_dtypes=True).then_inc(S["consts"], 1)
            pool.iota(iota128[:], [[P, EC]], base=0, channel_multiplier=0, allow_small_or_imprecise_dtypes=True).then_inc(S["consts"], 1)

            def indices(table, it, j, k):
                pool.tensor_copy(ixb[:, j:j + GB], ix[:, table, ds(GU * it + j, GB)]).then_inc(S["pool_idx"], 1)
                pool.wait_ge(S["pool_idx"], NT // GB * k + 2 * it + j // GB + 1)
                pool.sem_inc(S["pool_nop"], 1)

            def gather(it, j, phase):
                t = j + GU * it
                b = j % GB
                table = (0, 0, 3)[phase]
                pool.wait_ge(S["msg_lo"], NT * phase + t + 1)
                if b == 0:
                    indices(table, it, j, (1, 3, 4)[phase])
                else:
                    pool.sem_inc(S["pool_nop"], 1)
                pool.indirect_dma_start(out=gat[:, b, :], out_offset=None, in_=U[0:NP * (R0, R0, R1)[phase], :],
                                        in_offset=bass.IndirectOffsetOnAxis(ap=ixb[:, j:j + 1], axis=0)).then_inc(g_in[b], 16)

            def gathers(phase):
                with pool.Fori(0, NT // GU) as it:
                    for j in range(GU):
                        gather(it, j, phase)

            pool.wait_ge(S["srt_tab"], 1)
            pool.wait_ge(S["kinv_st"], 16)
            with pool.Fori(0, NT // GU) as it:
                for j in range(GU):
                    if j % GB == 0:
                        pool.wait_ge(S["w_done"], 2 * it + j // GB + 1)
                        indices(2, it, j, 0)
                    pool.indirect_dma_start(out=kgat[:, j, :], out_offset=None, in_=kinv_d,
                                            in_offset=bass.IndirectOffsetOnAxis(ap=ixb[:, j:j + 1], axis=0)).then_inc(k_in[j // GB], 16)
            pool.wait_ge(S["w_done"], NT // GB + 2)
            for g in range(NG):
                pool.wait_ge(u_st[g], 16 * (ST_C1 + 2 * R0))
            gathers(0)
            pool.wait_ge(S["urow_st"], 16)
            def urow_out(it, j):
                pool.wait_ge(k_in[j], 16 * GB * it + 16 * GB * (NT // GU + 1))
                pool.tensor_copy(ix[:, 3, ds(GU * it + GB * j, GB)], urow_g[:, GB * j:GB * (j + 1)]).then_inc(S["urow_ok"], 1)

            def lookup(it, first):
                for j in range(2):
                    indices(1, it, GB * j, 2)
                    if not (first and j == 0):
                        pool.wait_ge(S["urow_ok"], 2 * it + j - 1 + 1)
                        pool.sem_inc(S["pool_nop"], 1)
                    for k in range(GB * j, GB * (j + 1)):
                        pool.indirect_dma_start(out=urow_g[:, k:k + 1], out_offset=None, in_=urow_d,
                                                in_offset=bass.IndirectOffsetOnAxis(ap=ixb[:, k:k + 1], axis=0)).then_inc(k_in[j], 16)
                    if j == 1:
                        urow_out(it, 0)
                    elif not first:
                        urow_out(it - 1, 1)
            pool.sem_inc(S["urow_ok"], 1)
            lookup(0, True)
            with pool.Fori(1, NT // GU) as it:
                lookup(it, False)
            urow_out(NT // GU - 1, 1)
            pool.wait_ge(S["urow_ok"], NT // GB + 1)
            pool.wait_ge(S["ov_ok"], 1)
            for g in range(NG):
                pool.wait_ge(u_st[g], 16 * (ST_C2 + 2 * R0))
            gathers(1)
            pool.wait_ge(S["l_ix"], 1)
            pool.wait_ge(S["h_st"], 16)
            pool.wait_ge(S["hT_tp"], 3 * KT)
            with pool.Fori(0, R1 // 2) as it:
                for j in range(2):
                    pool.wait_ge(S["hc_tp"], 6 * it + 3 * j + 3)
                    pool.tensor_copy(lixb[:, j, :], lidx[:, ds(2 * TC * it + TC * j, TC)]).then_inc(S["lix_ok"], 1)
                    pool.wait_ge(S["lix_ok"], 2 * it + j + 1)
                    pool.sem_inc(S["pool_nop"], 1)
                    for g in range(TC):
                        pool.indirect_dma_start(out=src_rows[:, TC * j + g, :], out_offset=None, in_=h_d,
                                                in_offset=bass.IndirectOffsetOnAxis(ap=lixb[:, j, g:g + 1], axis=0)).then_inc(hc_in[j], 16)
            pool.wait_ge(S["ov_ok"], 1)
            n_ov = pool.value_load(ov[0:1, 0, NV:NV + 1], min_val=0, max_val=NV)

            def further_rows(c):
                pool.wait_ge(S["l_ix"], c + 2)
                pool.sem_inc(S["pool_nop"], 1)
                pool.indirect_dma_start(out=h[:, 0, :], out_offset=None, in_=h_d,
                                        in_offset=bass.IndirectOffsetOnAxis(ap=vidx[:], axis=0)).then_inc(S["v_in"], 16)
            each_further(pool, n_ov, further_rows)
            for g in range(2 * TC):
                pool.wait_ge(u_st[g], 16 * (ST_L1 + R1))
            for j in range(2):
                pool.wait_ge(v_st[j], n_ov * 16 + 16)
                pool.sem_inc(S["pool_nop"], 1)
            gathers(2)

            def q_tiles(n):
                H, s = HEADS[n][0], A[n]

                def one(it, j, t):
                    if t in ADD_DVE[n]:
                        return
                    pool.wait_ge(s["l_ok"], 5 * (2 * it + j) + t + 11)
                    pool.tensor_tensor(zt[:, t, :], zt[:, t, :], CT[:, t, :], ALU.add).then_inc(s["q_ok"], 1)
                if H == 1:
                    for t in range(NG):
                        one(0, 0, t)
                else:
                    with pool.Fori(0, H // 2) as it:
                        for j in range(2):
                            for t in range(NG):
                                one(it, j, t)
            pool.wait_ge(S["ct_ln"], 1)
            for n in range(3):
                q_tiles(n)

        @block.scalar
        def _(act):
            cp, rl = ACT.Copy, ACT.Relu

            def split(it, o):
                act.wait_ge(w_in[o % 2], 16 * (it + o // 2 + 1))
                act.wait_ge(S["steps"], 5 * (o + 2 * it) + 5)
                act.activation(w_hi[:, o % 2], raw[:, o % 2], cp).then_inc(S["w_hi"], 1)

            def evac(it, o, g, dst, stored):
                s = 5 * (o + 2 * it) + g
                act.wait_ge(S["steps"], s + 11)
                if stored is not None:
                    act.wait_ge(u_st[g], stored)
                act.activation(dst, ps[:, (o + g) % 2, 0:HALF] if len(dst.shape) == 2 else
                               ps[:, (o + g) % 2, 0:HALF].rearrange("p (h c) -> p h c", h=dst.shape[1]), cp).then_inc(S["evac"], 1)

            def ln(i):
                act.wait_ge(S["ln_var"], i + 1)
                act.activation(std[:], var[:], ACT.Sqrt).then_inc(S["ln_std"], 1)

            def transpose(k, fn):
                for kt in range(KT):
                    act.wait_ge(S["hT_tp"], KT * k + kt + 1)
                    b = 2 * (kt % 2)
                    act.activation(hT_hi[:, kt, :], psf[:, 512 * b:512 * b + NP], fn).then_inc(S["hT_hi"], 1)

            def phase(o, nr, st):
                def pair(it, first=False):
                    for j in range(2):
                        split(it, o + j + 1)
                        for g in range(NG):
                            evac(it, o + j, g, ust[:, g, :], None if first and j == 0 else 16 * (st + 2 * it + j))
                lo = 0
                if st == 0:
                    pair(0, True)
                    lo = 1
                with act.Fori(lo, nr) as it:
                    pair(it)
                for j in range(2):
                    split(0, o + 2 * nr + j + 1)
                    for g in range(NG):
                        evac(0, o + 2 * nr + j, g, R[:, g, j * HALF:(j + 1) * HALF], None)

            def hc_part(it, j, i):
                act.wait_ge(S["hc_tp"], 6 * it + 3 * j + i + 7)
                act.activation(hc[j][0][:, 2 * i:2 * i + 2, :], ps[:, 7, :].rearrange("p (k n) -> p k n", k=2), rl).then_inc(S["hc_hi"], 1)

            def relations(o, st):
                for j in range(2):
                    split(0, o + j + 1)
                    for g in range(NG):
                        evac(0, o + j, g, R[:, g, j * HALF:(j + 1) * HALF], None)
                for i in range(3):
                    hc_part(0, 0, i)

                def pair(it, last):
                    for rr in range(2):
                        for j in range(2):
                            end = last and rr == 1
                            if not (end and j == 1):
                                act.wait_ge(w_in[1 - j], 16 * (2 * it + rr + j + Q_REL // 2 + 1))
                                act.wait_ge(S["steps"], S_REL + 4 * TC * it + TC * (2 * rr + j) + 10)
                                act.activation(w_hi[:, 1 - j], raw[:, 1 - j], cp).then_inc(S["w_hi"], 1)
                            for g in range(TC):
                                k = TC * (2 * rr + j) + g
                                act.wait_ge(S["steps"], S_REL + 4 * TC * it + k + 11)
                                act.wait_ge(u_st[TC * j + g], 16 * (2 * it + rr + st))
                                act.activation(ust[:, TC * j + g, :], ps[:, g, 0:HALF], cp).then_inc(S["evac"], 1)
                                if TC * j + g < 3 and not end:
                                    hc_part(it + rr, 1 - rr, TC * j + g)
                with act.Fori(0, R1 // 2 - 1) as it:
                    pair(it, False)
                pair(R1 // 2 - 1, True)
                act.wait_ge(S["evac"], S_REL + 2 * TC * R1 + 2)
                for j in range(2):
                    for g in range(TC):
                        act.dma_start(U[(R1 - 1) * TC * P + UMAIN + g * P:(R1 - 1) * TC * P + UMAIN + (g + 1) * P, j * HALF:(j + 1) * HALF],
                                      ust[:, TC * j + g, :]).then_inc(u_st[TC * j + g], 16)
                act.sem_inc(S["evac"], S_SKIP)

            def further():
                for g in range(2 * TC):
                    act.wait_ge(u_st[g], 16 * (ST_L1 + R1))
                act.wait_ge(S["ov_ok"], 1)
                n_ov = act.value_load(ov[0:1, 0, NV:NV + 1], min_val=0, max_val=NV)

                def tile(c):
                    for j in range(2):
                        act.wait_ge(vw_in[j], 16 * c + 16)
                        act.activation(w_hi[:, j], raw[:, j], cp).then_inc(S["v_hi"], 1)
                        if j == 0:
                            for i in range(2):
                                act.wait_ge(S["hc_tp"], 3 * R1 + 6 + 2 * c + i + 1)
                                act.activation(hv_hi[:, 3 * i:3 * i + 3, :], ps[:, 2 + i, 0:HALF].rearrange("p (k n) -> p k n", n=P),
                                               rl).then_inc(S["hc_hi"], 1)
                    r = act.value_load(ov[0:1, 0, ds(c, 1)], min_val=0, max_val=R1 - 1)
                    k = act.value_load(ov[0:1, 1, ds(c, 1)], min_val=0, max_val=TO - 1)
                    for j in range(2):
                        act.wait_ge(S["v_mm"], 2 * c + j + 1)
                        act.wait_ge(v_st[j], 16 * c + 16)
                        act.activation(ust[:, j, :], ps[:, j, 0:HALF], cp).then_inc(S["v_ev"], 1)
                    for j in range(2):
                        act.wait_ge(S["v_ev"], 2 * c + j + 1)
                        act.dma_start(U[ds(r * (TO * P) + k * P, P), j * HALF:(j + 1) * HALF], ust[:, j, :]).then_inc(v_st[j], 16)
                each_further(act, n_ov, tile)
                split(0, Q_GCN)

            def messages(ph):
                with act.Fori(0, NT // GU) as it:
                    for o in range(GU):
                        t = o + GU * it
                        act.wait_ge(g_in[o % GB], 16 * (NT // GB * ph + 2 * it + o // GB + 1))
                        act.wait_ge(S["agg_pe"], NT * ph + t + 1)
                        act.activation(msg_hi[:, o % MB, :], gat[:, o % GB, :], cp,
                                       scale=wgt[:, ph // 2, ds(t, 1)]).then_inc(S["msg_hi"], 1)

            act.wait_ge(S["consts"], 14)
            act.sem_inc(S["evac"], 2)
            for j in range(2):
                act.sem_inc(v_st[j], 16)
            ln(0)
            split(0, 0)
            transpose(0, rl)
            phase(Q_C1, R0, ST_C1)
            act.wait_ge(S["w_done"], NT // GB + 2)
            messages(0)
            transpose(1, rl)
            phase(Q_C2, R0, ST_C2)
            messages(1)
            ln(1)
            transpose(2, rl)
            relations(Q_L1, ST_L1)
            further()
            messages(2)
            for s in range(NG):
                act.wait_ge(S["ct_tp"], s + 1)
                b = 4 + 2 * (s % 2)
                act.activation(CT[:, s, :], psf[:, 512 * b:512 * b + NP], cp).then_inc(S["ct_cp"], 1)
            act.wait_ge(S["deg_ok"], 1)
            act.activation(std[:], deg[:], ACT.Sqrt).then_inc(S["deg_sq"], 1)
            transpose(3, cp)

            def dense(q, dst):
                for k in range(2):
                    if q + k + 1 < Q_SPLIT[q]:
                        split(0, q + k + 1)
                    for g in range(NG):
                        evac(0, q + k, g, dst(g, k), None)
            dense(Q_GCN, lambda g, k: R[:, g, k * HALF:(k + 1) * HALF])
            ln(2)
            transpose(4, rl)
            act.wait_ge(S["ln_c"], 1)
            act.activation(CT, CT, ACT.Ln).then_inc(S["ln_cc"], 1)
            dense(Q_G1, lambda g, k: R[:, g, 0:H2 * (C2 + 1)].rearrange("p (h c) -> p h c", c=C2 + 1)[:, 4 * k:4 * k + 4, 0:C2])

            def rows(n):
                H, s = HEADS[n][0], A[n]
                act.wait_ge(s["row_tp"], 1)
                act.activation(alT[0:H, :], psf[0:H, 1024:1024 + NP], cp).then_inc(s["row_cp"], 1)

            def head_rows(n, it, j):
                s = A[n]
                hd = 2 * it + j
                if not (isinstance(it, int) and it == 0):
                    act.wait_ge(s["row_st"], 16 * hd)
                act.wait_ge(s["row_tp"], hd + 2)
                act.activation(hrow[:, j, :], ps[0:2 * NG, 2 + j, 0:P], cp).then_inc(s["row_cp"], 1)

            def tiles_(n, out_tile):
                H, s = HEADS[n][0], A[n]
                act.sem_inc(s["z_ok"], 10)

                def z(it, i):
                    j, t = i // NG, i % NG
                    if t == 0:
                        act.wait_ge(s[f"rd{j % 2}"], 16 * (it + j // 2) + 16)
                    act.wait_ge(s["p_ok"], 10 * it + i + 6)
                    act.activation(zt[:, t, :], rowZ[:, j % 2, :], ACT.Identity,
                                   bias=al[:, 0, t, ds(2 * it + j, 1)]).then_inc(s["z_ok"], 1)

                def e(it, i):
                    j, t = i // NG, i % NG
                    by_dve = [u for u in range(NG) if u in ADD_DVE[n]]
                    by_pool = [u for u in range(NG) if u not in ADD_DVE[n]]
                    if t in ADD_DVE[n]:
                        act.wait_ge(s["d_ok"], len(by_dve) * (2 * it + j) + by_dve.index(t) + 1)
                    else:
                        act.wait_ge(s["q_ok"], len(by_pool) * (2 * it + j) + by_pool.index(t) + 1)
                    if H > 1:
                        act.wait_ge(s["o_mm"], 10 * it + i + 1)
                    act.activation(out_tile(i % 2, i % NG), zt[:, i % NG, :], ACT.Exp).then_inc(s["p_ok"], 1)

                def heads(it, m, last):
                    for i in range(m):
                        if not (last and i + 3 >= m):
                            z(it, i + 3)
                        e(it, i)
                        if i % NG == 3 and not last:
                            head_rows(n, it + 1, i // NG)
                for i in range(3):
                    z(0, i)
                if H == 1:
                    heads(0, NG, True)
                else:
                    with act.Fori(0, H // 2 - 1) as it:
                        heads(it, 2 * NG, False)
                    heads(H // 2 - 1, 2 * NG, True)

            rows(0)
            for j in range(2):
                head_rows(0, 0, j)
            tiles_(0, lambda b, t: pt[:, b, :])
            for k in range(2):
                act.wait_ge(S["elu_m"], k + 1)
                c = slice(k * HALF, (k + 1) * HALF)
                act.activation(R[:, :, c], R[:, :, c], ACT.Exp).then_inc(S["elu_e"], 1)
            split(0, Q_G2)
            transpose(5, cp)
            dense(Q_G2, lambda g, k: R[:, g, k * HALF:(k + 1) * HALF])
            rows(1)
            head_rows(1, 0, 0)
            tiles_(1, lambda b, t: h[:, t, 0:NP])
            ln(3)
            transpose(6, rl)
            for i in range(2 * NG):
                g = i % NG
                act.wait_ge(S["ft_mm"], i + 1)
                src = psf[:, FT_BANK[i % 3] * 512:FT_BANK[i % 3] * 512 + D]
                if i < NG:
                    act.activation(R[:, g, :].rearrange("p (h c) -> p h c", c=C3 + 1)[:, :, 0:C3],
                                   src.rearrange("p (h c) -> p h c", c=C3), cp).then_inc(S["ft_ev"], 1)
                else:
                    act.activation(h[:, g, :], src, cp).then_inc(S["ft_ev"], 1)
                if i == NG + 1:
                    rows(2)
                if i >= 2 * NG - 2:
                    head_rows(2, 0, i - 2 * NG + 2)
            tiles_(2, lambda b, t: pt[:, b, :])

        @block.vector
        def _(dve):
            n_chain = [0]

            def link(ins):
                n_chain[0] += 1
                ins.then_inc(S["chain"], 1)
                dve.wait_ge(S["chain"], n_chain[0])

            def stats(g):
                for k in range(2):
                    ins = dve.bn_stats(bst[:, g, k, :], x[:, g, k * HALF:(k + 1) * HALF])
                return ins

            def ln(i, groups=range(NG)):
                for g in groups:
                    ins = stats(g)
                link(ins)
                for g in range(NG):
                    ins = dve.bn_aggr(mv[:, g, :], bst[:, g, :, :])
                link(ins)
                dve.tensor_scalar(var[:], mv[:, :, 1], EPS, None, ALU.add).then_inc(S["ln_var"], 1)
                dve.wait_ge(S["ln_std"], i + 1)
                link(dve.reciprocal(rstd[:], std[:]))
                for g in range(NG):
                    dve.tensor_scalar(h[:, g, :], x[:, g, :], mv[:, g, 0:1], rstd[:, g:g + 1],
                                      ALU.subtract, ALU.mult).then_inc(S["ln_h"], 1)

            def transpose(k, relu):
                for kt in range(KT):
                    dve.wait_ge(S["hT_hi"], KT * k + kt + 1)
                    b = 2 * (kt % 2)
                    src, hi = psf[:, 512 * b:512 * b + NP], hT_hi[:, kt, :].bitcast(F32)
                    if relu:
                        dve.scalar_tensor_tensor(hT_lo[:, kt, :], src, 0.0, hi, ALU.max, ALU.subtract).then_inc(S["hT_lo"], 1)
                    else:
                        dve.tensor_tensor(hT_lo[:, kt, :], src, hi, ALU.subtract).then_inc(S["hT_lo"], 1)

            def split(it, o):
                dve.wait_ge(S["w_hi"], o + 2 * it + 1)
                dve.tensor_tensor(w_lo[:, o % 2], raw[:, o % 2], w_hi[:, o % 2].bitcast(F32), ALU.subtract).then_inc(S["w_lo"], 1)

            def sort(between):
                dve.wait_ge(S["edges_in"], 64)
                link(dve.tensor_copy(e_f[:], e_i[:]))
                for j in range(NG + 1):
                    ins = dve.tensor_scalar(ge[:, j, :], e_f[:, 1, :], float(P * j), None, ALU.is_ge)
                link(ins)
                link(dve.tensor_tensor(grp1[:], ge[:, 0:NG, :], ge[:, 1:NG + 1, :], ALU.subtract))
                for g in range(NG):
                    ins = dve.tensor_tensor_scan(pre[:, g, :], grp1[:, g, :], zer[:], 0.0, ALU.add, ALU.add)
                link(ins)
                dve.tensor_copy(rs[:], pre[:, :, EC - 1]).then_inc(S["srt_rs"], 1)
                dve.tensor_scalar(vals[:, :, 0], e_f[:, 0, :], 1.0, None, ALU.add)
                dve.tensor_copy(vals[:, :, 2], e_f[:, 2, :])
                dve.tensor_copy(vals[:, :, 3], e_f[:, 3, :])
                link(dve.tensor_reduce(hi_f[:], ge[:, 1:NG, :].rearrange("p g c -> p c g"), AX.X, ALU.add))
                link(dve.scalar_tensor_tensor(lo_f[:], hi_f[:], -float(P), e_f[:, 1, :], ALU.mult, ALU.add))
                link(dve.tensor_scalar(vals[:, :, 1], lo_f[:], 1.0, None, ALU.add))
                dve.wait_ge(S["srt_ps"], 1)
                link(dve.tensor_copy(tot[:], ps[:, 6, 0:NG]))
                for g in range(NG):
                    ins = dve.tensor_scalar(ntl[:, g, :], iota128[:], tot[:, g:g + 1], None, ALU.is_lt)
                link(ins)
                link(dve.tensor_reduce(tiles[:], ntl[:], AX.X, ALU.add))
                link(dve.tensor_tensor_scan(tbi[:], tiles[:], z16[:, 0:NG], 0.0, ALU.add, ALU.add))
                link(dve.tensor_tensor(tb[:], tbi[:], tiles[:], ALU.subtract))
                link(dve.scalar_tensor_tensor(off[:], tb[0:EP, :], float(P), ps[0:EP, 7, 0:NG], ALU.mult, ALU.add))
                for g in range(NG):
                    ins = dve.scalar_tensor_tensor(pre[:, g, :], pre[:, g, :], off[:, g:g + 1], grp1[:, g, :], ALU.add, ALU.mult)
                link(ins)
                link(dve.tensor_reduce(pos[:], pre[:].rearrange("p g c -> p c g"), AX.X, ALU.add))
                link(dve.tensor_scalar(pos_i[:], pos[:], -1.0, None, ALU.add))
                link(dve.tensor_single_scalar(hi_i[:], pos_i[:], 7, ALU.arith_shift_right))
                link(dve.tensor_copy(hi_f[:], hi_i[:]))
                link(dve.scalar_tensor_tensor(lo_f[:], hi_f[:], -float(P), pos[:], ALU.mult, ALU.add))
                for s in range(EC // RC):
                    b, c0 = s % 2, s * RC
                    if s in (1, 4, 6):
                        between((1, 4, 6).index(s))
                    if s >= 1:
                        dve.wait_ge(S["srt_rhs"], s)
                    if s >= 2:
                        dve.wait_ge(S["srt_mm"], s - 1)
                    dve.tensor_tensor(oh_lo[0:EP, b], lo_f[:, c0:c0 + RC].unsqueeze(2).to_broadcast([EP, RC, P]),
                                      iota[0:EP, 1:P + 1].unsqueeze(1).to_broadcast([EP, RC, P]), ALU.is_equal)
                    link(dve.tensor_tensor(oh_hi[0:EP], hi_f[:, c0:c0 + RC].unsqueeze(2).to_broadcast([EP, RC, NT]),
                                           iota[0:EP, 0:NT].unsqueeze(1).to_broadcast([EP, RC, NT]), ALU.is_equal))
                    dve.tensor_tensor(val_hi[0:EP, b], oh_hi[0:EP].unsqueeze(2).to_broadcast([EP, RC, 4, NT]),
                                      vals[:, c0:c0 + RC, :].unsqueeze(3).to_broadcast([EP, RC, 4, NT]), ALU.mult).then_inc(S["srt_rhs"], 1)
                dve.wait_ge(S["srt_mm"], EC // RC)
                link(dve.tensor_copy(tab[:].rearrange("p v t -> p (v t)"), ps[:, 5, 0:4 * NT]))
                for k in range(NG - 1):
                    dve.tensor_scalar(gt[:, k, :], iota[:, 0:NT], tb[:, k + 1:k + 2], None, ALU.is_ge)
                for k in range(2):
                    ins = dve.scalar_tensor_tensor(ix_f[:, k, :], tab[:, 2 + k, :], float(NP), tab[:, 0, :], ALU.mult, ALU.add)
                link(ins)
                link(dve.tensor_reduce(grp_f[:], gt[:].rearrange("p k t -> p t k"), AX.X, ALU.add))
                link(dve.scalar_tensor_tensor(ix_f[:, 2, :], grp_f[:], float(P), tab[:, 1, :], ALU.mult, ALU.add))
                dve.tensor_scalar(ix[:, 0:3, :], ix_f[:], -1.0, 0.0, ALU.add, ALU.max)
                for k in range(GB):
                    ins = dve.tensor_scalar(grp_p[:, :, k], grp_f[:].rearrange("p (t k) -> p t k", k=GB)[:, :, k], float(8 ** k), None, ALU.mult)
                link(ins)
                link(dve.tensor_reduce(grp_f[:, 0:NT // GB], grp_p[:], AX.X, ALU.add))
                dve.tensor_copy(grp[:], grp_f[:, 0:NT // GB]).then_inc(S["srt_tab"], 1)

            def one_hot_dst(b, t):
                return dve.tensor_scalar(oh_d[:, b, :], iota16[:, 1:P + 1], tab[:, 1, ds(t, 1)], None, ALU.is_equal)

            def one_hots(between):
                dve.tensor_tensor(oh_all, iota[:, 1:P + 1].unsqueeze(1).to_broadcast([P, NT, P]),
                                  tab[:, 1, :].unsqueeze(2).to_broadcast([P, NT, P]), ALU.is_equal)
                between()
                for k, n, o in ((2, R0, 0), (3, R1, R0)):
                    ins = dve.tensor_tensor(oh_r[:, :, o:o + n], iota[:, 0:n].unsqueeze(1).to_broadcast([P, NT, n]),
                                            tab[:, k, :].unsqueeze(2).to_broadcast([P, NT, n]), ALU.is_equal)
                ins.then_inc(S["cnt_oh"], 1)

            def counted():
                dve.wait_ge(S["cnt_pe"], 1)
                link(dve.tensor_scalar(kinv[:].rearrange("p g n -> p (g n)"), ps[:, 6, 0:64 * NG], 1.0, None, ALU.max))
                dve.reciprocal(kinv[:], kinv[:]).then_inc(S["k_inv"], 1)

            def weigh(it, j):
                kg = kgat[:, GB * j:GB * (j + 1), :]
                t = ds(GU * it + GB * j, GB)
                dve.wait_ge(k_in[j], 16 * GB * it + 16 * GB)
                dve.tensor_tensor(kg, kg, oh_r[:, t, :], ALU.mult).then_inc(S["w_pr"], 1)
                dve.wait_ge(S["w_pr"], 2 * it + j + 1)
                dve.tensor_reduce(wgt[:, 0, t], kg[:, :, 0:R0], AX.X, ALU.add)
                dve.tensor_reduce(wgt[:, 1, t], kg[:, :, R0:R0 + R1], AX.X, ALU.add).then_inc(S["w_done"], 1)

            def c_side(part):
                def side(it, stride, o):
                    t = o + stride * it
                    dve.wait_ge(S["c_pe"], NT * part + t + 1)
                    one_hot_dst(o % 2, t)
                    if part == 0:
                        dve.tensor_scalar(oh_rr[:, o % 2, :], iota16[:, 0:R1], tab[:, 3, ds(t, 1)], None, ALU.is_equal)
                    n = NP if part == 0 else CW
                    dve.tensor_scalar(oh_s[:, o % 2, 0:n], iota16[:, 1 + CW * part:1 + CW * part + n], tab[:, 0, ds(t, 1)],
                                      None, ALU.is_equal).then_inc(S["c_oh"], 1)
                return side

            def messages(ph):
                with dve.Fori(0, NT // GU) as it:
                    for o in range(GU):
                        t = o + GU * it
                        b = o % MB
                        dve.wait_ge(S["agg_pe"], NT * ph + t + 1)
                        dve.tensor_scalar(onehot[:, b, :], iota[:, 1:P + 1], tab[:, 1, ds(t, 1)], None, ALU.is_equal)
                        dve.wait_ge(S["msg_hi"], NT * ph + t + 1)
                        dve.scalar_tensor_tensor(msg_lo[:, b, :], gat[:, o % GB, :], wgt[:, ph // 2, ds(t, 1)],
                                                 msg_hi[:, b, :].bitcast(F32), ALU.mult, ALU.subtract).then_inc(S["msg_lo"], 1)

            def sources():
                dve.wait_ge(S["c_pe"], NT + 2)
                dve.tensor_scalar(has[:, 0:512], ps[0:R1, 7, :], 1.0, None, ALU.min)
                link(dve.tensor_scalar(has[:, 512:NP], ps[0:R1, 2, CW:CW + NP - 512], 1.0, None, ALU.min))
                link(dve.tensor_tensor_scan(rank, has, has, 0.0, ALU.add, ALU.max))
                dve.tensor_tensor(key, rank, has, ALU.mult)
                link(dve.tensor_scalar(urow, rank, float(TC * P), ubase[0:R1, 1:2], ALU.is_gt, ALU.mult))
                link(dve.scalar_tensor_tensor(urow, rank, ubase[0:R1, 0:1], urow, ALU.add, ALU.add))
                dve.sem_inc(S["key_ok"], 1)
                counts_out(0)

            def keys():
                dve.wait_ge(S["key_tp"], 1)
                dve.tensor_copy(keyT[:].rearrange("p t r -> p (t r)"), ps[:, 3, 0:NG * R1])
                for k in range(TO):
                    ins = dve.tensor_scalar(ov_f[:, 0, R1 * k:R1 * (k + 1)], ps[0:1, 3, NG * R1:(NG + 1) * R1], float((TC + k) * P), None, ALU.is_gt)
                link(ins)

            def further_list():
                link(dve.tensor_tensor_scan(ov_f[:, 1, :], ov_f[:, 0, :], ov_f[:, 0, :], 0.0, ALU.add, ALU.max))
                link(dve.tensor_tensor(ov_cmp, ov_f[:, 1, :].unsqueeze(1).to_broadcast([1, NV, TO * R1]),
                                       iota[0:1, 0:NV].unsqueeze(2).to_broadcast([1, NV, TO * R1]), ALU.is_le))
                place, rel = ov_f[:, 2, 0:NV], ov_f[:, 3, 0:NV]
                link(dve.tensor_reduce(rel, ov_cmp, AX.X, ALU.add))
                link(dve.tensor_scalar(place, rel, float(R1), None, ALU.is_ge))
                link(dve.scalar_tensor_tensor(place, rel, 2.0 * R1, place, ALU.is_ge, ALU.add))
                link(dve.scalar_tensor_tensor(rel, place, -float(R1), rel, ALU.mult, ALU.add))
                dve.tensor_copy(ov[:, 0, 0:NV], rel)
                dve.tensor_copy(ov[:, 1, 0:NV], place)
                dve.tensor_copy(ov[:, 0, NV:NV + 1], ov_f[:, 1, TO * R1 - 1:TO * R1]).then_inc(S["ov_ok"], 1)

            def list_one_hot(r, b):
                dve.wait_ge(S["l_pe"], r + 1)
                for g in range(NG):
                    ins = dve.tensor_scalar(oh_l[:, b, g, :], iota16[:, 1:TC * P + 1], keyT[:, g, ds(r, 1)], None, ALU.is_equal)
                ins.then_inc(S["l_oh"], 1)

            def hc_part(it, j, i):
                dve.wait_ge(S["hc_hi"], 6 * it + 3 * j + i + 1)
                dve.scalar_tensor_tensor(hc[j][1][:, 2 * i:2 * i + 2, :], ps[:, 7, :].rearrange("p (k n) -> p k n", k=2), 0.0,
                                         hc[j][0][:, 2 * i:2 * i + 2, :].bitcast(F32), ALU.max, ALU.subtract).then_inc(S["hc_lo"], 1)

            def bias(o, v, j):
                if j == 0:
                    dve.wait_ge(v_in[v % 2], 16 * (v // 2 + 1))
                dve.wait_ge(S["evac"], 5 * (o + j + 1) + 2)
                rh = R[:, :, j * HALF:(j + 1) * HALF]
                return dve.tensor_tensor(rh, rh, vec[:, v % 2, j * HALF:(j + 1) * HALF].unsqueeze(1).to_broadcast([P, NG, HALF]), ALU.add)

            def relations(o, v, stride, side):
                split(0, o + 1)
                bias(o, v, 0)
                split(0, o + 2)
                for i in range(3):
                    hc_part(0, 0, i)
                bias(o, v, 1).then_inc(S["vec_ok"], 1)
                dve.wait_ge(S["vec_ok"], v + 1)
                for t in range(LEAD):
                    side(0, stride, t)

                def pair(it, sides, last=False):
                    for rr in range(2):
                        for j in range(2):
                            end = last and rr == 1
                            if not (end and j == 1):
                                dve.wait_ge(S["w_hi"], Q_REL + 4 * it + 2 * rr + j + 2)
                                dve.tensor_tensor(w_lo[:, 1 - j], raw[:, 1 - j], w_hi[:, 1 - j].bitcast(F32), ALU.subtract).then_inc(S["w_lo"], 1)
                            for g in range(TC):
                                if TC * j + g < 3 and not end:
                                    hc_part(it + rr, 1 - rr, TC * j + g)
                                if sides:
                                    for t in sides_at(stride, TC * (2 * rr + j) + g, 4 * TC):
                                        if not (isinstance(it, int) and stride * it + t + LEAD >= NT):
                                            side(it, stride, t + LEAD)
                lo = (NT - LEAD) // stride
                with dve.Fori(0, lo) as it:
                    pair(it, True)
                pair(lo, True)
                with dve.Fori(lo + 1, R1 // 2 - 1) as it:
                    pair(it, False)
                pair(R1 // 2 - 1, False, True)
                counts_out(1)

            def further():
                n_ov = dve.value_load(ov[0:1, 0, NV:NV + 1], min_val=0, max_val=NV)

                def tile(c):
                    r = dve.value_load(ov[0:1, 0, ds(c, 1)], min_val=0, max_val=R1 - 1)
                    k = dve.value_load(ov[0:1, 1, ds(c, 1)], min_val=0, max_val=TO - 1)
                    for g in range(NG):
                        ins = dve.tensor_scalar(oh_v[:, g, :], iota16[:, ds(k * P + TC * P + 1, P)], keyT[:, g, ds(r, 1)], None, ALU.is_equal)
                    ins.then_inc(S["l_oh"], 1)
                    dve.wait_ge(S["l_pe"], R1 + c + 3)
                    dve.tensor_copy(vidx[:], ps[:, 6, 0:1]).then_inc(S["l_ix"], 1)
                    for j in range(2):
                        dve.wait_ge(S["v_hi"], 2 * c + j + 1)
                        dve.tensor_tensor(w_lo[:, j], raw[:, j], w_hi[:, j].bitcast(F32), ALU.subtract).then_inc(S["v_lo"], 1)
                        if j == 0:
                            for i in range(2):
                                dve.wait_ge(S["hc_hi"], 3 * R1 + 2 * c + i + 1)
                                dve.scalar_tensor_tensor(hv_lo[:, 3 * i:3 * i + 3, :], ps[:, 2 + i, 0:HALF].rearrange("p (k n) -> p k n", n=P), 0.0,
                                                         hv_hi[:, 3 * i:3 * i + 3, :].bitcast(F32), ALU.max, ALU.subtract).then_inc(S["hc_lo"], 1)
                each_further(dve, n_ov, tile)
                split(0, Q_GCN)

            def phase(o, nr, v, stride=0, side=None):
                def ahead(it, t):
                    if not (isinstance(it, int) and stride * it + t + LEAD >= NT):
                        side(it, stride, t + LEAD)

                def pair(it, sides):
                    for j in range(2):
                        split(it, o + j + 1)
                        if sides:
                            for i in range(5 * j, 5 * j + 5):
                                for t in sides_at(stride, i):
                                    ahead(it, t)
                lo = 0
                if side:
                    for t in range(LEAD):
                        side(0, stride, t)
                    lo = (NT - LEAD) // stride
                    with dve.Fori(0, lo) as it:
                        pair(it, True)
                    pair(lo, True)
                    lo += 1
                    sources()
                    pair(lo, False)
                    lo += 1
                    keys()
                    for it in range(lo, nr):
                        for j in range(2):
                            for n, r in enumerate(lists_at(it - lo, j)):
                                if n == 2:
                                    split(it, o + j + 1)
                                list_one_hot(r, r % 2)
                    lo = nr
                    dve.wait_ge(S["l_pe"], R1 + 2)
                    dve.tensor_copy(lidx[:], ps[:, 7, 0:TC * R1]).then_inc(S["l_ix"], 1)
                if o == Q_C1:
                    split(0, o + 1)
                    sort(lambda k: split(0, o + 2 + k))
                    one_hots(lambda: split(0, o + 5))
                    split(0, o + 6)
                    with dve.Fori(3, 5) as it:
                        pair(it, False)
                    counted()
                    lo = 5 + NT // GU // 2
                    with dve.Fori(5, lo) as it:
                        for j in range(2):
                            split(it, o + j + 1)
                            for k in range(2):
                                weigh(2 * it - 10 + j, k)
                    for k in range(2):
                        weigh(NT // GU - 1, k)
                    dve.wait_ge(S["w_done"], NT // GB + 2)
                if lo < nr:
                    with dve.Fori(lo, nr) as it:
                        pair(it, False)
                split(0, o + 2 * nr + 1)
                if side:
                    further_list()
                split(0, o + 2 * nr + 2)
                bias(o + 2 * nr, v, 0)
                bias(o + 2 * nr, v, 1).then_inc(S["vec_ok"], 1)
                dve.wait_ge(S["vec_ok"], v + 1)

            def counts_out(part):
                dve.wait_ge(S["c_pe"], NT * (part + 1) + 2)
                dve.tensor_copy(C[:, :, CW * part:CW * (part + 1)], ps[:, 2:2 + NG, 0:CW]).then_inc(S["acc_out"], 1)

            def sums_out(ph, into_x):
                dve.wait_ge(S["agg_pe"], NT * (ph + 1) + MB)
                for c0, c1 in ((0, 512), (512, D)):
                    ins = dve.tensor_tensor((R if into_x else h)[:, :, c0:c1], R[:, :, c0:c1], sums(c0), ALU.add)
                if into_x:
                    link(ins)
                    ins = dve.tensor_tensor(x[:], x[:], R[:, :, 0:D], ALU.add)
                ins.then_inc(S["acc_out"], 1)

            dve.wait_ge(S["consts"], 14)
            dve.sem_inc(S["w_lo"], 2)
            dve.sem_inc(S["msg_lo"], GB)
            dve.sem_inc(S["w_done"], 2)
            dve.sem_inc(S["hc_lo"], 1)
            dve.sem_inc(S["v_lo"], 2)
            dve.wait_ge(S["x_in"], 32)
            ln(0)
            split(0, 0)
            transpose(0, True)
            dve.wait_ge(S["bd_z"], 1)
            dve.wait_ge(S["bd_tp"], 1)
            for k in range(2):
                for i in range(2):
                    r = slice(64 * i, 64 * i + 64)
                    ins = dve.tensor_copy(bd[r, k, r], ps[r, 4, 64 * k:64 * k + 64])
            link(ins)
            link(dve.tensor_copy(bd_hi[:], bd[:]))
            link(dve.tensor_tensor(bd_lo[:], bd[:], bd_hi[:].bitcast(F32), ALU.subtract))
            dve.sem_inc(S["bd_ok"], 1)
            phase(Q_C1, R0, 0)
            messages(0)
            sums_out(0, False)
            transpose(1, True)
            phase(Q_C2, R0, 1, 18, c_side(0))
            messages(1)
            sums_out(1, True)
            dve.wait_ge(S["acc_out"], 3)
            ln(1)
            transpose(2, True)
            relations(Q_L1, 2, 6, c_side(1))
            further()
            messages(2)
            sums_out(2, False)
            dve.wait_ge(S["acc_out"], 5)
            link(dve.tensor_reduce(deg[:], C, AX.X, ALU.add))
            link(dve.tensor_scalar(deg[:], deg[:], 1.0, None, ALU.add))
            dve.sem_inc(S["deg_ok"], 1)
            dve.wait_ge(S["ct_tp"], NG)
            dve.tensor_scalar(C, C, 0.0, NEG, ALU.is_equal, ALU.mult)
            dve.wait_ge(S["deg_sq"], 1)
            link(dve.reciprocal(dinv[:], std[:]))
            transpose(3, False)
            for k in range(2):
                if Q_GCN + k + 1 < Q_SPLIT[Q_GCN]:
                    split(0, Q_GCN + k + 1)
            dve.wait_ge(v_in[1], 32)
            dve.tensor_tensor(x[:], x[:], vec[:, 1, :].unsqueeze(1).to_broadcast([P, NG, D]), ALU.add).then_inc(S["vec_ok"], 1)
            dve.wait_ge(S["vec_ok"], 4)
            dve.wait_ge(S["evac"], 5 * (Q_GCN + 2) + 2)
            for g in range(NG):
                dve.tensor_scalar(R[:, g, 0:D], R[:, g, 0:D], dinv[:, g:g + 1], None, ALU.mult).then_inc(S["gcn_y"], 1)
            for i in range(2 * NG):
                j, cols = i // 2, slice((i % 2) * HALF, (i % 2 + 1) * HALF)
                if j and i % 2 == 0:
                    dve.wait_ge(S["gcn_ev"], i)
                    stats(j - 1)
                dve.wait_ge(S["gcn_mm"], i + 1)
                ins = dve.scalar_tensor_tensor(x[:, j, cols], ps[:, 2 + i % 2, 0:HALF], dinv[:, j:j + 1], x[:, j, cols], ALU.mult, ALU.add)
                ins.then_inc(S["gcn_ev"], 1)
            dve.wait_ge(S["gcn_ev"], 2 * NG)
            ln(2, (NG - 1,))
            transpose(4, True)
            dve.wait_ge(S["hT_tp"], 5 * KT)
            link(dve.tensor_scalar(h[:, :, 0:NP], CT, 0.0, NEG, ALU.is_equal, ALU.mult))
            dve.tensor_scalar(CT, CT, 1.0, None, ALU.max).then_inc(S["ln_c"], 1)
            split(0, Q_G1 + 1)
            dve.wait_ge(S["ln_cc"], 1)
            dve.tensor_tensor(CT, CT, h[:, :, 0:NP], ALU.add).then_inc(S["ct_ln"], 1)

            def heads_of(n, g):
                H, c = HEADS[n]
                return R[:, g, 0:H * (c + 1)].rearrange("p (h c) -> p h c", c=c + 1) if H > 1 else R[:, g, 0:c].unsqueeze(1)

            def scores(n, v, parts):
                H, c = HEADS[n]
                for k in range(2):
                    dve.wait_ge(v_in[(v + k) % 2], 16 * ((v + k) // 2 + 1))
                for g, h0, h1, done, value in parts:
                    dve.wait_ge(done, value)
                    t = [arena[:, 2560 + 1280 * k:2560 + 1280 * k + (h1 - h0) * c].rearrange("p (h c) -> p h c", c=c) for k in range(2)]
                    for k in range(2):
                        ins = dve.tensor_tensor(t[k], heads_of(n, g)[:, h0:h1, 0:c],
                                                vec[:, (v + k) % 2, h0 * c:h1 * c].rearrange("p (h c) -> p h c", c=c), ALU.mult)
                    link(ins)
                    for k in range(2):
                        ins = dve.tensor_reduce(al[:, k, g, h0:h1], t[k], AX.X, ALU.add)
                    link(ins)
                dve.sem_inc(A[n]["al_ok"], 1)
                dve.sem_inc(S["vec_ok"], 2)
                link(dve.tensor_scalar(al[:, 2, :, 0:H], al[:, 0, :, 0:H], 0.2, None, ALU.mult))

            def maximum(n, it, j, groups):
                s = A[n]
                hd = 2 * it + j
                first = isinstance(it, int) and it == 0
                m = mz[:, j, :].unsqueeze(2)
                d = al[:, 1, :, ds(hd, 1)]
                for g in groups:
                    if g == 0:
                        dve.wait_ge(s[f"rs{j}"], 16 * it + 16)
                        if not first or j:
                            dve.wait_ge(s["mx"], 7 * hd)
                    if g >= 3:
                        dve.wait_ge(s["mx"], 7 * hd + g - 2)
                    dve.sem_inc(S["dve_nop"], 1)
                    dve.tensor_tensor_reduce(mx_scr[g % 3], rowS[:, j, :], C[:, g, :], 1.0, -3.0e38, ALU.add, ALU.max,
                                             mxt[:, j, g:g + 1]).then_inc(s["mx"], 1)
                if NG - 1 in groups:
                    dve.wait_ge(s["mx"], 7 * hd + 5)
                    dve.tensor_tensor(m, mxt[:, j, :].unsqueeze(2), d, ALU.add).then_inc(s["mx"], 1)
                    dve.wait_ge(s["mx"], 7 * hd + 6)
                    dve.scalar_tensor_tensor(m, m, 0.2, m, ALU.mult, ALU.max).then_inc(s["mx"], 1)
                    if not first:
                        dve.wait_ge(s["row_tp"], hd)
                    dve.wait_ge(s["mx"], 7 * hd + 7)
                    dve.sem_inc(S["dve_nop"], 1)
                    dve.scalar_tensor_tensor(mcol[:, j, 1, :].unsqueeze(2), d, 0.2, m, ALU.mult, ALU.subtract)
                    dve.tensor_tensor(mcol[:, j, 0, :].unsqueeze(2), d, m, ALU.subtract).then_inc(s["mx_ok"], 1)

            def leaky(n, it, i):
                s = A[n]
                k = 10 * it + i
                j, t = i // NG, i % NG
                if t == 0:
                    dve.wait_ge(s[f"rm{j}"], 16 * it + 16)
                dve.wait_ge(s["z_ok"], k + 11)
                dve.sem_inc(S["dve_nop"], 1)
                dve.scalar_tensor_tensor(zt[:, t, :], rowM[:, j, :], al[:, 2, t, ds(2 * it + j, 1)], zt[:, t, :],
                                         ALU.add, ALU.max).then_inc(s["l_ok"], 1)
                if t - 1 in ADD_DVE[n]:
                    dve.wait_ge(s["l_ok"], k + 10)
                    u = zt[:, t - 1, :]
                    dve.tensor_tensor(u, u, CT[:, t - 1, :], ALU.add).then_inc(s["d_ok"], 1)

            def head_out(n, it, j, put, steps):
                H, c = HEADS[n]
                s = A[n]
                hd = 2 * it + j
                base = steps * hd
                o = ps[:, 6 + j, 0:NG * (c + 1)].rearrange("p (g c) -> p g c", c=c + 1)
                dve.wait_ge(s["o_mm"], 5 * hd + 7)
                dve.tensor_scalar(rz[:, j, :].unsqueeze(2), o[:, :, c:c + 1], 1e-16, None, ALU.add if n == 0 else ALU.max).then_inc(s["o_r"], 1)
                dve.wait_ge(s["o_r"], base + 1)
                dve.reciprocal(rz[:, j, :], rz[:, j, :]).then_inc(s["o_r"], 1)
                dve.wait_ge(s["o_r"], base + 2)
                put(hd, o[:, :, 0:c], rz[:, j, :].unsqueeze(2).to_broadcast([P, NG, c]), s, base)

            def all_heads(n, put, steps, beside=None):
                H = HEADS[n][0]

                def pair(it, first, last):
                    for i in range(2 * NG):
                        leaky(n, it, i)
                        if i % NG < 3 and not last:
                            maximum(n, it + 1, i // NG, ((0, 1), (2, 3), (4,))[i % NG])
                        if i == 3 and not first:
                            head_out(n, it - 1, 1, put, steps)
                        if i == NG + 3:
                            head_out(n, it, 0, put, steps)
                for j in range(2):
                    maximum(n, 0, j, range(NG))
                pair(0, True, False)
                with dve.Fori(1, H // 2 - 1) as it:
                    pair(it, False, False)
                pair(H // 2 - 1, False, True)
                if beside:
                    beside()
                head_out(n, H // 2 - 1, 1, put, steps)

            for n in range(3):
                dve.sem_inc(A[n]["l_ok"], 10)

            dve.memset(R[:, :, 0:H2 * (C2 + 1)].rearrange("p g (h c) -> p g h c", c=C2 + 1)[:, :, :, C2:C2 + 1], 1.0).then_inc(S["bd_ok"], 1)
            dve.wait_ge(S["w_lo"], Q_G1 + 4)
            scores(0, 4, [(g, H2 // 2 * k, H2 // 2 * (k + 1), S["evac"], 5 * (Q_G1 + k) + g + 3) for k in range(2) for g in range(NG)])
            def elu_parts(k):
                c = slice(k * HALF, (k + 1) * HALF)
                if k == 0:
                    dve.wait_ge(v_in[0], 64)
                dve.wait_ge(A[0]["o_ev"], H2 // 2 * (k + 1) + 2)
                dve.sem_inc(S["dve_nop"], 1)
                link(dve.tensor_tensor(h[:, :, c], h[:, :, c], vec[:, 0, c].unsqueeze(1).to_broadcast([P, NG, HALF]), ALU.add))
                dve.tensor_scalar(R[:, :, c], h[:, :, c], 0.0, None, ALU.min).then_inc(S["elu_m"], 1)
                dve.wait_ge(S["elu_m"], k + 1)
                link(dve.tensor_scalar(h[:, :, c], h[:, :, c], 0.0, None, ALU.max))

            def elu(k):
                c = slice(k * HALF, (k + 1) * HALF)
                dve.wait_ge(S["elu_e"], k + 1)
                dve.scalar_tensor_tensor(h[:, :, c], R[:, :, c], -1.0, h[:, :, c], ALU.add, ALU.add).then_inc(S["elu_v"], 1)
            all_heads(0, lambda hd, o, r, s, base: dve.tensor_tensor(h[:, :, ds(hd * C2, C2)], o, r, ALU.mult).then_inc(s["o_ev"], 1), 2,
                      lambda: elu_parts(0))
            elu_parts(1)
            dve.sem_inc(S["vec_ok"], 1)
            for k in range(2):
                elu(k)
            dve.wait_ge(S["elu_v"], 2)
            dve.memset(R[:, :, D:D + 1], 1.0).then_inc(S["bd_ok"], 1)
            transpose(5, False)
            split(0, Q_G2)
            split(0, Q_G2 + 1)
            dve.wait_ge(S["w_lo"], Q_G2 + 4)
            scores(1, 7, [(g, 0, 1, S["evac"], 5 * (Q_G2 + 1) + g + 3) for g in range(NG)])
            maximum(1, 0, 0, range(NG))
            for t in range(NG):
                leaky(1, 0, t)
            dve.wait_ge(v_in[1], 80)
            link(dve.tensor_tensor(x[:], x[:], vec[:, 1, :].unsqueeze(1).to_broadcast([P, NG, D]), ALU.add))
            dve.sem_inc(S["vec_ok"], 1)
            for g in range(NG):
                b = 4 + 2 * (g % 2)
                if g:
                    dve.wait_ge(A[1]["o_ev"], g)
                    stats(g - 1)
                dve.wait_ge(A[1]["o_mm"], g + 1)
                link(dve.tensor_scalar(rz[:, 0, g:g + 1], ps[:, b + 1, HALF:HALF + 1], 1e-16, None, ALU.add))
                link(dve.reciprocal(rz[:, 0, g:g + 1], rz[:, 0, g:g + 1]))
                for k in range(2):
                    cols = slice(k * HALF, (k + 1) * HALF)
                    ins = dve.scalar_tensor_tensor(x[:, g, cols], ps[:, b + k, 0:HALF], rz[:, 0, g:g + 1], x[:, g, cols], ALU.mult, ALU.add)
                ins.then_inc(A[1]["o_ev"], 1)
            dve.wait_ge(A[1]["o_ev"], NG)
            dve.memset(R[:, :, :].rearrange("p g (h c) -> p g h c", c=C3 + 1)[:, :, :, C3:C3 + 1], 1.0).then_inc(S["bd_ok"], 1)
            ln(3, (NG - 1,))
            transpose(6, True)
            scores(2, 10, [(g, 0, H3, S["ft_ev"], g + 1) for g in range(NG)])

            def residual(hd, o, r, s, base):
                t = kinv[:]
                cols = ds(hd * C3, C3)
                dve.tensor_tensor(t, o, r, ALU.mult).then_inc(s["o_r"], 1)
                dve.wait_ge(s["o_r"], base + 3)
                dve.tensor_tensor(t, t, h[:, :, cols], ALU.add).then_inc(s["o_r"], 1)
                dve.wait_ge(s["o_r"], base + 4)
                dve.scalar_tensor_tensor(x[:, :, cols], t, 0.0, x[:, :, cols], ALU.max, ALU.add).then_inc(s["o_ev"], 1)
                dve.wait_ge(s["o_ev"], hd + 3)
            all_heads(2, residual, 4)
            dve.sem_inc(S["x_ok"], 1)

        @block.tensor
        def _(pe):
            def transpose(k, half_done=None):
                for kt in range(KT):
                    b = 2 * (kt % 2)
                    if half_done is not None and kt % (KT // 2) == 0:
                        pe.wait_ge(half_done, kt // (KT // 2) + 1)
                    if kt >= 2:
                        pe.wait_ge(S["hT_lo"], KT * k + kt - 1)
                    for g in range(NG):
                        ins = pe.transpose(psf[:, 512 * b + P * g:512 * b + P * (g + 1)], h[:, g, P * kt:P * (kt + 1)], ident[:])
                    ins.then_inc(S["hT_tp"], 1)

            def step(it, o, g):
                s = 5 * (o + 2 * it) + g
                if g == 0:
                    pe.wait_ge(S["w_lo"], o + 2 * it + 3)
                pe.wait_ge(S["evac"], s + 1)
                acc = ps[:, (o + g) % 2, 0:HALF]
                product(acc, (hT_hi, hT_lo), o % 2, slice(P * g, P * (g + 1))).then_inc(S["steps"], 1)

            packed = [None]

            def group(it, stride, o):
                if o % GB == 0:
                    packed[0] = pe.value_load(grp[0:1, ds(stride // GB * it + o // GB, 1)], min_val=0, max_val=8 ** GB - 1)
                return ((packed[0] >> (3 * (o % GB))) & 7).with_bounds(min_val=0, max_val=NG - 1)

            def bank(g, n):
                return ps[:, ds(g + 2, 1), 0:n].rearrange("p a n -> p (a n)")

            def clear(i, banks):
                if i:
                    pe.wait_ge(S["acc_out"], i)
                else:
                    pe.wait_ge(S["k_inv"], 1)
                for b in banks:
                    pe.matmul(ps[:, b, :], z16[:, 0:P], z16[:], start=True, stop=True)

            def c_side(part):
                def side(it, stride, o):
                    t = o + stride * it
                    g = group(it, stride, o)
                    pe.wait_ge(S["c_oh"], NT * part + t + 1)
                    b = o % 2
                    if part == 0:
                        pe.matmul(ps[0:R1, 7, :], oh_rr[:, b, :], oh_s[:, b, 0:512], start=False, stop=True, skip_group_check=True)
                        pe.matmul(ps[0:R1, 2, CW:CW + NP - 512], oh_rr[:, b, :], oh_s[:, b, 512:NP], start=False, stop=True, skip_group_check=True)
                    pe.matmul(bank(g, CW), oh_d[:, b, :], oh_s[:, b, 0:CW], start=False, stop=True, skip_group_check=True).then_inc(S["c_pe"], 1)
                return side

            def messages(ph, q, i):
                pe.wait_ge(S["evac"], 5 * q + 2)
                clear(i, range(8))
                with pe.Fori(0, NT // GU) as it:
                    for o in range(GU):
                        b = o % MB
                        g = group(it, GU, o)
                        pe.wait_ge(S["msg_lo"], NT * ph + o + GU * it + 1 + GB)
                        for part in (msg_hi, msg_lo):
                            for c0, c1 in ((0, 512), (512, D)):
                                ins = pe.matmul(sums(c0, g), onehot[:, b, :], part[:, b, c0:c1], start=False,
                                                stop=part is msg_lo, skip_group_check=True)
                        ins.then_inc(S["agg_pe"], 1)

            def sort(beside):
                for s in range(EC // RC):
                    pe.wait_ge(S["srt_rhs"], s + 1)
                    for c in range(RC):
                        ins = pe.matmul(ps[:, 5, 0:4 * NT], oh_lo[0:EP, s % 2, c, :], val_hi[0:EP, s % 2, c].rearrange("p v n -> p (v n)"),
                                        start=(s + c == 0), stop=(s * RC + c == EC - 1))
                    ins.then_inc(S["srt_mm"], 1)
                    beside(s)

            def count_side(it, stride, o):
                t = stride * it + o
                g = group(it, stride, o)
                pe.matmul(ps[:, 6, ds(g * 64, R0 + R1)], oh_all[:, ds(t, 1), :].rearrange("p t n -> p (t n)"),
                          oh_r[:, ds(t, 1), :].rearrange("p t n -> p (t n)"), start=False, stop=True, skip_group_check=True)

            def phase(o, nr, stride=0, side=None):
                def pair(it, sides):
                    for j in range(2):
                        for g in range(NG):
                            step(it, o + j, g)
                            if sides:
                                for t in sides_at(stride, 5 * j + g):
                                    if not (isinstance(it, int) and stride * it + t >= NT):
                                        side(it, stride, t)
                lo = 0
                if side:
                    lo = NT // stride
                    with pe.Fori(0, lo) as it:
                        pair(it, True)
                    pair(lo, True)
                    pair(lo + 1, False)
                    lo += 2
                    keys()
                    for it in range(lo, nr):
                        for i in range(2 * NG):
                            step(it, o + i // NG, i % NG)
                            for r in lists_at(it - lo, None, i):
                                node_list(r, r % 2)
                    lo = nr
                if o == Q_C1:
                    pair(0, False)
                    def steps(k0, k1):
                        for k in range(k0, k1):
                            step(0, o + 2 + k // NG, k % NG)
                    n = EC // RC
                    sort(lambda k: steps(3 * k // 2, 3 * (k + 1) // 2))
                    steps(3 * n // 2, 4 * NG)
                    pe.wait_ge(S["srt_tab"], 1)
                    pe.wait_ge(S["cnt_oh"], 1)
                    pe.matmul(ps[:, 6, :], z16[:, 0:P], z16[:], start=True, stop=True)
                    with pe.Fori(0, 2) as it:
                        for i in range(2 * NG):
                            step(it, o + 6 + i // NG, i % NG)
                            for t in sides_at(NT // 2, i):
                                count_side(it, NT // 2, t)
                    pe.matmul(ps[:, 7, :], z16[:, 0:P], z16[:], start=True, stop=True).then_inc(S["cnt_pe"], 1)
                    lo = 5
                if lo < nr:
                    with pe.Fori(lo, nr) as it:
                        pair(it, False)
                for j in range(2):
                    for g in range(NG):
                        step(0, o + 2 * nr + j, g)

            def keys():
                pe.wait_ge(S["key_ok"], 1)
                pe.wait_ge(S["acc_out"], 2)
                for g in range(NG):
                    pe.transpose(ps[:, 3, R1 * g:R1 * (g + 1)], key[:, P * g:P * (g + 1)], ident[0:R1, 0:R1])
                pe.transpose(ps[0:1, 3, R1 * NG:R1 * (NG + 1)], rank[:, NP - 1:NP], ident[0:R1, 0:R1]).then_inc(S["key_tp"], 1)
                pe.matmul(ps[:, 7, :], z16[:, 0:P], z16[:], start=True, stop=True)

            def node_list(r, b):
                pe.wait_ge(S["l_oh"], r + 1)
                for k in range(TC):
                    for g in range(NG):
                        ins = pe.matmul(ps[:, 7, TC * r + k:TC * r + k + 1], oh_l[:, b, g, P * k:P * (k + 1)], nid[:, g:g + 1],
                                        start=False, stop=True, skip_group_check=True)
                ins.then_inc(S["l_pe"], 1)

            def product(acc, part, j, kt_rows):
                n = 0
                for kt in range(KT):
                    hi, lo = (t[:, kt, kt_rows] for t in part)
                    for l, r in ((hi, w_hi), (hi, w_lo), (lo, w_hi)):
                        ins = pe.matmul(acc, l, r[:, j, kt, :], start=(n == 0), stop=(n == 3 * KT - 1))
                        n += 1
                return ins

            def relations(stride, side):
                def hc_part(it, j, i):
                    if i == 0:
                        pe.wait_ge(hc_in[j], 16 * TC * it + 16 * TC)
                    pe.wait_ge(S["hc_lo"], 6 * it + 3 * j + i + 1)
                    for k in range(2):
                        kt = 2 * i + k
                        for g in range(TC):
                            ins = pe.transpose(ps[:, 7, P * (TC * k + g):P * (TC * k + g + 1)],
                                               src_rows[:, TC * j + g, P * kt:P * (kt + 1)], ident[:])
                    ins.then_inc(S["hc_tp"], 1)

                for j in range(2):
                    for g in range(NG):
                        step(0, Q_L1 + j, g)
                pe.wait_ge(S["l_ix"], 1)
                for i in range(3):
                    hc_part(0, 0, i)

                def pair(it, sides, last=False):
                    for rr in range(2):
                        for j in range(2):
                            for g in range(TC):
                                k = TC * (2 * rr + j) + g
                                if g == 0:
                                    pe.wait_ge(S["w_lo"], Q_REL + 4 * it + 2 * rr + j + 3)
                                if j + g == 0:
                                    pe.wait_ge(S["hc_lo"], 6 * it + 3 * rr + 4)
                                pe.wait_ge(S["evac"], S_REL + 4 * TC * it + k + 1)
                                product(ps[:, g, 0:HALF], hc[rr], j, slice(P * g, P * (g + 1))).then_inc(S["steps"], 1)
                                if TC * j + g < 3 and not (last and rr == 1):
                                    hc_part(it + rr, 1 - rr, TC * j + g)
                                if sides:
                                    for t in sides_at(stride, k, 4 * TC):
                                        side(it, stride, t)
                lo = NT // stride
                with pe.Fori(0, lo) as it:
                    pair(it, True)
                with pe.Fori(lo, R1 // 2 - 1) as it:
                    pair(it, False)
                pair(R1 // 2 - 1, False, True)
                pe.wait_ge(S["evac"], S_REL + 2 * TC * R1 + 2)
                pe.sem_inc(S["steps"], S_SKIP)

            def further():
                pe.wait_ge(S["evac"], 5 * Q_GCN + 2)
                n_ov = pe.value_load(ov[0:1, 0, NV:NV + 1], min_val=0, max_val=NV)

                def tile(c):
                    pe.wait_ge(S["l_oh"], R1 + c + 1)
                    for g in range(NG):
                        ins = pe.matmul(ps[:, 6, 0:1], oh_v[:, g, :], nid[:, g:g + 1], start=(g == 0), stop=(g == NG - 1))
                    ins.then_inc(S["l_pe"], 1)
                    pe.wait_ge(S["v_in"], 16 * c + 16)
                    pe.wait_ge(S["hc_lo"], 3 * R1 + 2 * c + 1)
                    for kt in range(KT):
                        ins = pe.transpose(ps[:, 2 + kt // 3, P * (kt % 3):P * (kt % 3 + 1)], h[:, 0, P * kt:P * (kt + 1)], ident[:])
                        if kt % 3 == 2:
                            ins.then_inc(S["hc_tp"], 1)
                    pe.wait_ge(S["hc_lo"], 3 * R1 + 2 * c + 3)
                    for j in range(2):
                        pe.wait_ge(S["v_lo"], 2 * c + j + 3)
                        product(ps[:, j, 0:HALF], (hv_hi, hv_lo), j, slice(0, P)).then_inc(S["v_mm"], 1)
                each_further(pe, n_ov, tile)
                pe.wait_ge(S["v_ev"], n_ov * 2)

            pe.sem_inc(S["l_pe"], 2)
            pe.sem_inc(S["hc_tp"], 6)
            pe.sem_inc(S["steps"], 10)
            pe.sem_inc(S["c_pe"], 2)
            pe.sem_inc(S["agg_pe"], MB)
            pe.wait_ge(S["consts"], 14)
            pe.wait_ge(S["ln_h"], NG)
            transpose(0)
            pe.wait_ge(S["w64_in"], 64)
            for k in range(2):
                ins = pe.transpose(ps[:, 4, 64 * k:64 * k + 64], w64[:, k, :], ident[0:64, 0:64])
            ins.then_inc(S["bd_tp"], 1)
            pe.wait_ge(S["srt_rs"], 1)
            pe.matmul(ps[0:EP, 7, 0:NG], below[:], rs[:], start=True, stop=True)
            pe.matmul(ps[:, 6, 0:NG], ones[0:EP, :], rs[:], start=True, stop=True).then_inc(S["srt_ps"], 1)
            pe.wait_ge(S["hT_lo"], KT)
            phase(Q_C1, R0)
            messages(0, Q_C2, 0)
            pe.wait_ge(S["acc_out"], 1)
            transpose(1)
            pe.wait_ge(S["hT_lo"], 2 * KT)
            clear(1, range(2, 8))
            phase(Q_C2, R0, 18, c_side(0))
            pe.wait_ge(S["l_ix"], 1)
            messages(1, Q_L1, 2)
            pe.wait_ge(S["ln_h"], 2 * NG)
            transpose(2)
            pe.wait_ge(S["hT_lo"], 3 * KT)
            clear(3, range(2, 2 + NG))
            relations(6, c_side(1))
            further()
            messages(2, Q_GCN, 4)
            pe.wait_ge(S["acc_out"], 5)
            for s in range(NG):
                if s >= 2:
                    pe.wait_ge(S["ct_cp"], s - 1)
                b = 4 + 2 * (s % 2)
                for g in range(NG):
                    ins = pe.transpose(psf[:, 512 * b + P * g:512 * b + P * (g + 1)], C[:, g, P * s:P * (s + 1)], ident[:])
                ins.then_inc(S["ct_tp"], 1)
            transpose(3)
            pe.wait_ge(S["hT_lo"], 4 * KT)
            for k in range(2):
                for g in range(NG):
                    step(0, Q_GCN + k, g)
            pe.wait_ge(S["gcn_y"], NG)
            pe.wait_ge(S["ct_cp"], NG)
            for i in range(2 * NG):
                j, cols = i // 2, slice((i % 2) * HALF, (i % 2 + 1) * HALF)
                if i >= 2:
                    pe.wait_ge(S["gcn_ev"], i - 1)
                acc = ps[:, 2 + i % 2, 0:HALF]
                for s in range(NG):
                    pe.matmul(acc, CT[:, s, P * j:P * (j + 1)], R[:, s, cols], start=(s == 0), stop=False)
                pe.matmul(acc, ident[:], R[:, j, cols], start=False, stop=True).then_inc(S["gcn_mm"], 1)
            pe.wait_ge(S["ln_h"], 3 * NG)
            transpose(4)
            pe.wait_ge(S["hT_lo"], 5 * KT)
            for k in range(2):
                for g in range(NG):
                    step(0, Q_G1 + k, g)

            def rows(n):
                H, s = HEADS[n][0], A[n]
                pe.wait_ge(s["al_ok"], 1)
                for g in range(NG):
                    ins = pe.transpose(psf[0:H, 1024 + P * g:1024 + P * (g + 1)], al[:, 0, g, 0:H], ident[:])
                ins.then_inc(s["row_tp"], 1)

            def head_rows(n, it, j):
                s = A[n]
                hd = 2 * it + j
                if not (isinstance(it, int) and it == 0):
                    pe.wait_ge(s["row_cp"], hd)
                pe.wait_ge(s["mx_ok"], hd + 1)
                pe.transpose(ps[0:2 * NG, 2 + j, 0:P], mcol[:, j].rearrange("p k g -> p (k g)"), ident[:]).then_inc(s["row_tp"], 1)

            def tiles_(n):
                H, c = HEADS[n]
                s = A[n]
                for m, v in (("o_mm", 2), ("o_ev", 2)):
                    pe.sem_inc(s[m], v)

                def one(it, j, t):
                    k = 5 * (2 * it + j) + t
                    b = (5 * j + t) % 2
                    if t == 0:
                        pe.wait_ge(s["o_ev"], 2 * it + j + 1)
                        pe.matmul(ps[:, 6 + j, :], z16[:, 0:P], z16[:], start=True, stop=True)
                    pe.wait_ge(s["p_ok"], k + 11)
                    for g in range(NG):
                        ins = pe.matmul(ps[:, 6 + j, (c + 1) * g:(c + 1) * (g + 1)], pt[:, b, P * g:P * (g + 1)],
                                        R[:, t, ds((2 * it + j) * (c + 1), c + 1)], start=False, stop=True, skip_group_check=True)
                    ins.then_inc(s["o_mm"], 1)
                with pe.Fori(0, H // 2 - 1) as it:
                    for j in range(2):
                        for t in range(NG):
                            one(it, j, t)
                            if t == 2:
                                head_rows(n, it + 1, j)
                for j in range(2):
                    for t in range(NG):
                        one(H // 2 - 1, j, t)

            for n in range(3):
                pe.sem_inc(A[n]["p_ok"], 10)
            rows(0)
            for j in range(2):
                head_rows(0, 0, j)
            tiles_(0)
            transpose(5, S["elu_v"])
            pe.wait_ge(S["hT_lo"], 6 * KT)
            for k in range(2):
                for g in range(NG):
                    step(0, Q_G2 + k, g)
            rows(1)
            head_rows(1, 0, 0)
            pe.wait_ge(A[1]["p_ok"], NG + 10)
            for g in range(NG):
                b = 4 + 2 * (g % 2)
                if g >= 2:
                    pe.wait_ge(A[1]["o_ev"], g - 1)
                for k, (c0, c1) in enumerate(((0, HALF), (HALF, D + 1))):
                    for t in range(NG):
                        ins = pe.matmul(ps[:, b + k, 0:c1 - c0], h[:, t, P * g:P * (g + 1)], R[:, t, c0:c1],
                                        start=(t == 0), stop=(t == NG - 1))
                ins.then_inc(A[1]["o_mm"], 1)
            pe.wait_ge(S["ln_h"], 4 * NG)
            transpose(6)
            pe.wait_ge(S["hT_lo"], 7 * KT)
            pe.wait_ge(S["bd_ok"], 1)
            for i in range(2 * NG):
                g, k = i % NG, i // NG
                if i >= 3:
                    pe.wait_ge(S["ft_ev"], i - 2)
                for kt in range(KT):
                    o = FT_BANK[i % 3] * 512 + P * kt
                    rows_ = slice(P * g, P * (g + 1))
                    for m, (l, r) in enumerate(((hT_hi, bd_hi), (hT_hi, bd_lo), (hT_lo, bd_hi))):
                        ins = pe.matmul(psf[:, o:o + P], l[:, kt, rows_], r[:, k, :], start=(m == 0), stop=(m == 2))
                ins.then_inc(S["ft_mm"], 1)
                if i == NG + 1:
                    rows(2)
                if i >= 2 * NG - 2:
                    head_rows(2, 0, i - 2 * NG + 2)
            pe.wait_ge(S["ft_ev"], 2 * NG)
            tiles_(2)


def kernel(**inputs):
    import numpy as _np
    import concourse.bacc as _bacc
    from concourse import mybir as _mybir
    from concourse.bass_utils import run_bass_kernel_spmd as _run

    nc = _bacc.Bacc("TRN2", target_bir_lowering=False, num_devices=1)
    arrays, aps = {}, {}
    for name, value in inputs.items():
        arr = _np.ascontiguousarray(value)
        arrays[f"in_{name}"] = arr
        aps[name] = nc.dram_tensor(f"in_{name}", arr.shape, _mybir.dt.from_np(arr.dtype), kind="ExternalInput").ap()
    out = nc.dram_tensor("out_x", (N, D), _mybir.dt.float32, kind="ExternalOutput").ap()
    gnn_kernel(nc, aps, out)
    r = _run(nc, [arrays], core_ids=[0])
    return r.results[0]["out_x"]
```
